# Optimizing a Trainium2 kernel written in Bass

```python
import numpy as np
import jax
import jax.numpy as jnp

def _softmax(x, axis=-1):
    return jax.nn.softmax(x, axis=axis)

def _gelu(x):
    return jax.nn.gelu(x, approximate=True)

def _silu(x):
    return jax.nn.silu(x)

def _sigmoid(x):
    return jax.nn.sigmoid(x)

def _layernorm(x, axis=-1, eps=1e-05):
    m = jnp.mean(x, axis=axis, keepdims=True)
    v = jnp.var(x, axis=axis, keepdims=True)
    return (x - m) / jnp.sqrt(v + eps)

def _scatter_add(tgt, idx, src, axis=0):
    return tgt.at[idx].add(src)

def _segment_sum(src, seg, n):
    return jax.ops.segment_sum(src, seg, n)
kernel_name = 'mk_prb_d1_jaxref_r4_87a0d9'

def setup_inputs(seed: int=0):
    np.random.seed(seed)
    _w = jnp.asarray

    def _L0_attn_setup():
        import jax, jax.numpy as jnp
        import numpy as np
        D_MODEL = 256
        NUM_HEADS = 16
        D_K = D_MODEL // NUM_HEADS
        MAX_LEN = 256
        BATCH = 8
        SEQ = 256
        key = jax.random.key(seed)
        ks = jax.random.split(key, 12)
        s = 0.02
        inp = {'x': jax.random.normal(ks[0], (BATCH, SEQ, D_MODEL), dtype=jnp.float32), 'Wq': jax.random.normal(ks[1], (D_MODEL, D_MODEL), dtype=jnp.float32) * s, 'bq': jnp.zeros((D_MODEL,), dtype=jnp.float32), 'Wk': jax.random.normal(ks[2], (D_MODEL, D_MODEL), dtype=jnp.float32) * s, 'bk': jnp.zeros((D_MODEL,), dtype=jnp.float32), 'Wv': jax.random.normal(ks[3], (D_MODEL, D_MODEL), dtype=jnp.float32) * s, 'bv': jnp.zeros((D_MODEL,), dtype=jnp.float32), 'Wo': jax.random.normal(ks[4], (D_MODEL, D_MODEL), dtype=jnp.float32) * s, 'bo': jnp.zeros((D_MODEL,), dtype=jnp.float32), 'relative_k': jax.random.normal(ks[5], (2 * MAX_LEN - 1, D_K), dtype=jnp.float32), 'relative_v': jax.random.normal(ks[6], (2 * MAX_LEN - 1, D_K), dtype=jnp.float32)}
        return inp
    _L0_attn_in = _L0_attn_setup()

    def _L0_ffn_setup():
        import jax, jax.numpy as jnp
        import numpy as np
        D_MODEL, D_FF, N_EXPERTS, TOP_K = (256, 512, 8, 2)
        B, S = (2, 512)
        key = jax.random.key(seed)
        ks = jax.random.split(key, 6)
        sd = 1.0 / np.sqrt(D_MODEL)
        sf = 1.0 / np.sqrt(D_FF)
        return {'x': jax.random.normal(ks[0], (B, S, D_MODEL), jnp.float32), 'router_w': jax.random.normal(ks[1], (N_EXPERTS, D_MODEL), jnp.float32) * sd, 'gate_w': jax.random.normal(ks[2], (N_EXPERTS, D_MODEL, D_FF), jnp.float32) * sd, 'gate_b': jnp.zeros((N_EXPERTS, D_FF), jnp.float32), 'up_w': jax.random.normal(ks[3], (N_EXPERTS, D_MODEL, D_FF), jnp.float32) * sd, 'up_b': jnp.zeros((N_EXPERTS, D_FF), jnp.float32), 'down_w': jax.random.normal(ks[4], (N_EXPERTS, D_FF, D_MODEL), jnp.float32) * sf, 'down_b': jnp.zeros((N_EXPERTS, D_MODEL), jnp.float32)}
    _L0_ffn_in = _L0_ffn_setup()
    _d = {'L0_attn_x': _L0_attn_in['x'], 'L0_attn_Wq': _L0_attn_in['Wq'], 'L0_attn_bq': _L0_attn_in['bq'], 'L0_attn_Wk': _L0_attn_in['Wk'], 'L0_attn_bk': _L0_attn_in['bk'], 'L0_attn_Wv': _L0_attn_in['Wv'], 'L0_attn_bv': _L0_attn_in['bv'], 'L0_attn_Wo': _L0_attn_in['Wo'], 'L0_attn_bo': _L0_attn_in['bo'], 'L0_attn_relative_k': _L0_attn_in['relative_k'], 'L0_attn_relative_v': _L0_attn_in['relative_v'], 'L0_ffn_router_w': _L0_ffn_in['router_w'], 'L0_ffn_gate_w': _L0_ffn_in['gate_w'], 'L0_ffn_gate_b': _L0_ffn_in['gate_b'], 'L0_ffn_up_w': _L0_ffn_in['up_w'], 'L0_ffn_up_b': _L0_ffn_in['up_b'], 'L0_ffn_down_w': _L0_ffn_in['down_w'], 'L0_ffn_down_b': _L0_ffn_in['down_b']}
    _x0 = _d['L0_attn_x']
    _d['L0_attn_x'] = jax.random.normal(jax.random.fold_in(jax.random.key(seed), 1), (2, 2048, 256), dtype=_x0.dtype)
    del _x0
    return _d

def reference(L0_attn_x, L0_attn_Wq, L0_attn_bq, L0_attn_Wk, L0_attn_bk, L0_attn_Wv, L0_attn_bv, L0_attn_Wo, L0_attn_bo, L0_attn_relative_k, L0_attn_relative_v, L0_ffn_router_w, L0_ffn_gate_w, L0_ffn_gate_b, L0_ffn_up_w, L0_ffn_up_b, L0_ffn_down_w, L0_ffn_down_b):

    def _L0_attn_ref(x, Wq, bq, Wk, bk, Wv, bv, Wo, bo, relative_k, relative_v):
        import jax, jax.numpy as jnp
        import numpy as np
        D_MODEL = 256
        NUM_HEADS = 16
        D_K = D_MODEL // NUM_HEADS
        MAX_LEN = 256
        BATCH = 8
        SEQ = 256
        B, L, D = x.shape
        H, dk = (NUM_HEADS, D_K)
        Q = (x @ Wq.T + bq).reshape(B, L, H, dk).transpose(0, 2, 1, 3)
        K = (x @ Wk.T + bk).reshape(B, L, H, dk).transpose(0, 2, 1, 3)
        V = (x @ Wv.T + bv).reshape(B, L, H, dk).transpose(0, 2, 1, 3)
        rel_pos = jnp.arange(L)[None, :] - jnp.arange(L)[:, None] + (MAX_LEN - 1)
        rel_k = relative_k[rel_pos]
        rel_v = relative_v[rel_pos]
        scale = 1.0 / np.sqrt(dk).astype(np.float32)
        scores = jnp.einsum('bhld,bhrd->bhlr', Q, K) * scale
        scores = scores + jnp.einsum('bhld,lrd->bhlr', Q, rel_k)
        attn = jax.nn.softmax(scores, axis=-1)
        out = jnp.einsum('bhlr,bhrd->bhld', attn, V)
        out = out + jnp.einsum('bhlr,lrd->bhld', attn, rel_v)
        out = out.transpose(0, 2, 1, 3).reshape(B, L, D)
        return out @ Wo.T + bo

    def _L0_ffn_ref(x, router_w, gate_w, gate_b, up_w, up_b, down_w, down_b):
        import jax, jax.numpy as jnp
        import numpy as np
        D_MODEL, D_FF, N_EXPERTS, TOP_K = (256, 512, 8, 2)
        B, S = (2, 512)
        b, s, d = x.shape
        xf = x.reshape(b * s, d)
        n = xf.shape[0]
        router_logits = xf @ router_w.T
        probs = jax.nn.softmax(router_logits, axis=-1)
        topv, topi = jax.lax.top_k(probs, TOP_K)
        mask = jnp.zeros_like(probs).at[jnp.arange(n)[:, None], topi].set(1.0)
        probs = probs * mask
        probs = probs / (probs.sum(axis=-1, keepdims=True) + 1e-09)
        g = jnp.einsum('nd,edf->nef', xf, gate_w) + gate_b
        u = jnp.einsum('nd,edf->nef', xf, up_w) + up_b
        h = jax.nn.silu(g) * u
        expert_out = jnp.einsum('nef,efd->ned', h, down_w) + down_b
        y = jnp.einsum('ne,ned->nd', probs, expert_out)
        return y.reshape(b, s, d)
    x = L0_attn_x
    xn = _layernorm(x, axis=-1)
    x = x + _L0_attn_ref(xn, L0_attn_Wq, L0_attn_bq, L0_attn_Wk, L0_attn_bk, L0_attn_Wv, L0_attn_bv, L0_attn_Wo, L0_attn_bo, L0_attn_relative_k, L0_attn_relative_v) + _L0_ffn_ref(xn, L0_ffn_router_w, L0_ffn_gate_w, L0_ffn_gate_b, L0_ffn_up_w, L0_ffn_up_b, L0_ffn_down_w, L0_ffn_down_b)
    return x

_drawn_inputs = setup_inputs


def setup_inputs(seed=0):
    import zlib

    import numpy as np

    out = dict(_drawn_inputs(seed))
    spreads = {'L0_attn_bq': (0.0, 0.419),
     'L0_attn_bk': (0.0, 0.8),
     'L0_attn_bv': (0.0, 0.287),
     'L0_attn_bo': (0.0, 0.1),
     'L0_ffn_gate_b': (0.0, 0.1),
     'L0_ffn_up_b': (0.0, 0.1),
     'L0_ffn_down_b': (0.0, 0.1)}
    factors = {'L0_attn_Wk': 8.0, 'L0_attn_Wv': 8.0}
    for name, (base, spread) in spreads.items():
        noise = np.random.default_rng([zlib.crc32(name.encode()), seed]).standard_normal(out[name].shape)
        drawn = base * np.exp(spread * noise) if base else spread * noise
        out[name] = jnp.asarray(drawn.astype(out[name].dtype))
    for name, factor in factors.items():
        out[name] = (out[name] * factor).astype(out[name].dtype)
    return out
```

```python
import math
from contextlib import ExitStack

import concourse.bass as bass
from concourse import mybir

FP32 = mybir.dt.float32
BF16 = mybir.dt.bfloat16
FP16 = mybir.dt.float16
ALU = mybir.AluOpType
ACT = mybir.ActivationFunctionType
AX = mybir.AxisListType

P = 128
B, L, D, H, DK = 2, 2048, 256, 16, 16
MAXLEN = 256
TOK = B * L
BH = B * H
NB = L // P
KD = D // P
CH = 512
NCH = TOK // CH
TPC = CH // P
NE, F = 8, 512
FT = F // P
EPS = 1e-5
PARTS = 6 * DK
Q_PLANES = (0, 0, 1, 1, 0, 2)
K_PLANES = (0, 1, 0, 1, 2, 0)

M_LO, M_HI = -6, 2
WIN = (M_HI - M_LO + 1) * P
RELW = WIN + P
REL0 = P * M_LO - (P - 1)


def window(c):
    return max(M_LO, -c), min(M_HI, NB - 1 - c)


def blocks(c):
    lo, hi = window(c)
    return hi - lo + 1


def rel_groups(c):
    return -(-(blocks(c) + 1) // 4)


GROUPS_BH = sum(rel_groups(c) for c in range(NB))
GROUPS_BEFORE = [sum(rel_groups(i) for i in range(c)) for c in range(NB)]
PGROUPS = NB // 4
TGROUPS_BH = PGROUPS * NB + GROUPS_BH
STEP = 2 * NB
UNITS = BH * NB
LAG_RSTORE, LAG_SKEW, LAG_S, LAG_E, LAG_PSTORE, LAG_UNSKEW, LAG_T, LAG_O = 1, 2, 3, 4, 5, 6, 7, 8
VC = DK + 2
PROB_SCALE_LN = 12 * math.log(2.0)
PEEL = 10


def rel_group_index(it, k):
    return it * (2 * GROUPS_BH) + (k // NB) * GROUPS_BH + GROUPS_BEFORE[k % NB]


def t_group_index(it, k):
    return it * (2 * TGROUPS_BH) + t_group_static(k)


def t_group_static(k):
    c = k % NB
    return (k // NB) * TGROUPS_BH + PGROUPS * c + GROUPS_BEFORE[c]


def evac_plan(c):
    rel = rel_groups(c)
    return ["act", "dve", "act", "act"] + ["dve"] + ["act"] * (rel - 2) + ["dve"] * (rel > 1)


EV = {e: [sum(evac_plan(i).count(e) for i in range(c)) for c in range(NB)] for e in ("act", "dve")}
EV_BH = {e: sum(evac_plan(c).count(e) for c in range(NB)) for e in ("act", "dve")}


def evac_count(e, it, k, g):
    c = k % NB
    return it * (2 * EV_BH[e]) + (k // NB) * EV_BH[e] + EV[e][c] + evac_plan(c)[: g + 1].count(e)


def evac_of(it, k, g):
    while g < 0:
        k -= 1
        g += len(evac_plan(k % NB))
    e = evac_plan(k % NB)[g]
    return e, evac_count(e, it, k, g)


def bank_items(k):
    scores = [("scores", k - LAG_S, bank) for bank in range(L // CH)] if k >= LAG_S else []
    return scores + [("rel", k, n) for n in range(rel_groups(k % NB))]


BANKS = 3
BANK_ITEMS = [item for k in range(PEEL + STEP + LAG_O) for item in bank_items(k)]
ITEM_INDEX = {item: i for i, item in enumerate(BANK_ITEMS)}
assert (TGROUPS_BH * 2) % (2 * BANKS) == 0
assert ITEM_INDEX[("rel", PEEL + STEP, 0)] - ITEM_INDEX[("rel", PEEL, 0)] == 2 * TGROUPS_BH


def group_blocks(c, g):
    if g < PGROUPS:
        return range(4 * g, 4 * g + 4)
    n = 4 * (g - PGROUPS)
    return range(n, min(n + 4, blocks(c) + 1))


def segments(c):
    lo, hi = window(c)
    edges = [(0, (c + lo) * P, 1), ((c + lo) * P, (c + hi + 1) * P, 0), ((c + hi + 1) * P, L, 2)]
    out = []
    for bank in range(L // CH):
        for a, z, kind in edges:
            a, z = max(a, bank * CH), min(z, (bank + 1) * CH)
            if a < z:
                out.append((bank, a, z, kind))
    return out


def project(nc, hbm, keep):
    with ExitStack() as ctx:
        def sb(name, shape, dt=FP32):
            return ctx.enter_context(nc.sbuf_tensor(name, shape, dt))

        def sem(name):
            return ctx.enter_context(nc.semaphore(name))

        wq = sb("wq", [P, KD, D])
        wk = sb("wk", [P, KD, D])
        wv = sb("wv", [P, KD, D])
        wr = sb("wr", [P, KD, NE])
        bq = sb("bq", [P, 2])
        bk = sb("bk", [P, 2])
        rel_ends = sb("rel_ends", [P, 2])
        kbias = sb("kbias", [P, 3, 2])
        bv = sb("bv", [P, D])
        rk = sb("rk", [DK, RELW])
        rk_rest = sb("rk_rest", [DK, RELW])
        rk_parts = sb("rk_parts", [DK, 3, RELW], BF16)
        xin = sb("xin", [P, 2, TPC, D])
        stats = sb("stats", [P, TPC, 6])
        moments = sb("moments", [P, 2, TPC, 2])
        eps = sb("eps", [P, 1])
        std = sb("std", [P, 2, TPC])
        rstd = sb("rstd", [P, 2, TPC])
        xn = sb("xn", [P, 2, TPC, D])
        xc = [sb(f"xc{i}", [P, KD, CH]) for i in range(2)]
        full = sb("full", [P, 2, CH])
        rest = sb("rest", [P, 2, CH])
        planes = sb("planes", [P, 2, 3, CH], BF16)
        psum = [ctx.enter_context(nc.psum_tensor(f"pa{i}", [P, CH], FP32)) for i in range(8)]
        xt_ps, qk_ps, v_ps, r_ps = psum[0:2], psum[2:4], psum[6:8], psum[4]

        s_w = sem("a_weights")
        s_rk = sem("a_rel_k")
        s_rkp = sem("a_rel_k_parts")
        s_rkd = sem("a_rel_k_stacked")
        s_kb = sem("a_k_bias")
        s_x = [sem(f"a_x{i}") for i in range(2)]
        s_st = sem("a_stats")
        s_mo = sem("a_moments")
        s_std = sem("a_std")
        s_rstd = sem("a_rstd")
        s_xn = sem("a_xn")
        s_xt = sem("a_xt")
        s_xc = sem("a_xc")
        s_xcw = [sem(f"a_xc_stored{i}") for i in range(2)]
        s_qk = sem("a_qk")
        s_f = sem("a_full")
        s_hi = sem("a_high")
        s_fr = sem("a_rest")
        s_mid = sem("a_middle")
        s_pl = sem("a_planes")
        s_plw = [sem(f"a_planes_stored{i}") for i in range(2)]
        s_v = sem("a_v_router")
        s_ve = sem("a_v_router_read")
        s_id = sem("a_constants")
        s_pre = sem("a_memset")
        block = ctx.enter_context(nc.Block())

        full_of = [(0, 0), (0, 1)] + [(kind, half) for half in range(2) for kind in (1, 2, 3)]
        NFULL = len(full_of)
        weights = 11

        @block.sync
        def _(sp):
            for t, src in ((wq, hbm["wqT"]), (wk, hbm["wkT"]), (wv, hbm["wvT"]), (wr, hbm["router_wT"])):
                sp.dma_start(t[:, :, :], src.rearrange("(k p) n -> p k n", p=P)).then_inc(s_w, 16)
            for t, src in ((bq, hbm["bq"]), (bk, hbm["bk"])):
                sp.dma_start(t[:, :], src).then_inc(s_w, 16)
            sp.dma_start(rel_ends[:, :], hbm["rel_k_ends"]).then_inc(s_w, 16)
            sp.dma_start(bv[:, :], hbm["bv"].to_broadcast([P, D])).then_inc(s_w, 16)
            sp.dma_start(keep["rv"][:, :, :], hbm["rel_v"].rearrange("(n p) d -> p n d", p=P)).then_inc(s_w, 16)
            sp.dma_start(keep["rv_lo"][:, :], hbm["rel_v"][0:1, :].to_broadcast([P, DK])).then_inc(s_w, 16)
            sp.dma_start(keep["rv_hi"][:, :], hbm["rel_v"][RELW - 1:RELW, :].to_broadcast([P, DK])).then_inc(s_w, 16)
            sp.dma_start(rk[:, :], hbm["rel_kT"]).then_inc(s_rk, 16)
            sp.wait_ge(s_rkp, 4)
            sp.nop(nofuse=True)
            for s, plane in enumerate(K_PLANES):
                sp.dma_start(keep["rk_stack"][DK * s:DK * (s + 1), :], rk_parts[:, plane, :]).then_inc(s_rkd, 16)
            def pair(gg):
                for par in range(2):
                    g = gg * 2 + par
                    sp.wait_ge(s_xn, g + 1)
                    sp.nop(nofuse=True)
                    sp.dma_start(xin[:, par, :, :], hbm["x"][bass.ds(g * CH, CH), :].rearrange(
                        "(t p) d -> p t d", p=P)).then_inc(s_x[par], 16)
                for par in range(2):
                    g = gg * 2 + par
                    sp.wait_ge(s_xc, g + 2)
                    sp.nop(nofuse=True)
                    sp.dma_start(hbm["xT"][:, :, bass.ds(g * CH, CH)], xc[par][:, :, :]).then_inc(s_xcw[par], 16)
                    for v, (kind, half) in enumerate(full_of):
                        sp.wait_ge(s_pl, g * NFULL + v + 3)
                        sp.nop(nofuse=True)
                        rows = hbm["planes"][kind, :, half * P:(half + 1) * P, bass.ds(g * CH, CH)]
                        sp.dma_start(rows.rearrange("r p n -> p r n"),
                                     planes[:, v % 2, :, :]).then_inc(s_plw[v % 2], 16)
            pair(0)
            with sp.Fori(1, NCH // 2) as gg:
                pair(gg)
            sp.wait_ge(s_rkd, 16 * len(K_PLANES))
            sp.nop(nofuse=True)
            for i in range(2):
                sp.wait_ge(s_xcw[i], 16 * NCH // 2)
                sp.nop(nofuse=True)
                sp.wait_ge(s_plw[i], 16 * NCH * NFULL // 2)
                sp.nop(nofuse=True)

        @block.gpsimd
        def _(pool):
            pool.sem_inc(s_pl, 2)
            ident, mask = keep["ident"], keep["mask"]
            nc.gpsimd.memset(ident[:, :], 0.0).then_inc(s_pre, 1)
            nc.gpsimd.memset(mask[:, :, :, :], 1.0).then_inc(s_pre, 1)
            pool.wait_ge(s_pre, 2)
            nc.gpsimd.affine_select(out=ident[:, :], in_=ident[:, :], compare_op=ALU.not_equal,
                                    fill=1.0, base=0, pattern=[[-1, P]], channel_multiplier=1).then_inc(s_id, 1)
            nc.gpsimd.affine_select(out=mask[:, 0, :, :], in_=mask[:, 0, :, :], compare_op=ALU.is_ge,
                                    fill=0.0, base=-(P - 1), pattern=[[0, 2], [1, P]], channel_multiplier=1).then_inc(s_id, 1)
            nc.gpsimd.affine_select(out=mask[:, 1, :, :], in_=mask[:, 1, :, :], compare_op=ALU.is_ge,
                                    fill=0.0, base=P - 2, pattern=[[0, 2], [-1, P]], channel_multiplier=-1).then_inc(s_id, 1)
            with pool.Fori(0, NCH) as g:
                for v in range(NFULL):
                    i = g * NFULL + v
                    pool.wait_ge(s_fr, i + 3)
                    pool.nop(nofuse=True)
                    nc.gpsimd.tensor_copy(planes[:, v % 2, 1, :], rest[:, v % 2, :]).then_inc(s_mid, 1)
                    pool.wait_ge(s_mid, i + 1)
                    nc.gpsimd.tensor_tensor(planes[:, v % 2, 2, :], rest[:, v % 2, :], planes[:, v % 2, 1, :],
                                            ALU.subtract).then_inc(s_pl, 1)

        @block.scalar
        def _(act):
            act.sem_inc(s_f, NFULL)
            act.wait_ge(s_kb, 4)
            with act.Fori(0, NCH // 2) as gg:
                for par in range(2):
                    g = gg * 2 + par
                    act.wait_ge(s_mo, g * TPC + TPC)
                    nc.scalar.activation(std[:, par, :], moments[:, par, :, 1], ACT.Sqrt,
                                         bias=eps[:, 0:1]).then_inc(s_std, 1)
                    for v, (kind, half) in enumerate(full_of):
                        act.wait_ge(s_qk, g * 4 + (half if kind == 0 else 2 + half) + 1)
                        act.wait_ge(s_fr, g * NFULL + v + 1)
                        bias, scale = (bq, 1.0) if kind == 0 else (kbias[:, kind - 1, :], DK ** -0.5)
                        nc.scalar.activation(full[:, v % 2, :], qk_ps[half][:, :], ACT.Identity,
                                             bias=bias[:, half:half + 1], scale=scale).then_inc(s_f, 1)

        @block.vector
        def _(dve):
            dve.sem_inc(s_xn, 2)
            dve.sem_inc(s_xc, 1)
            dve.sem_inc(s_fr, 2)
            dve.sem_inc(s_ve, 3)
            nc.vector.memset(eps[:, :], EPS).then_inc(s_kb, 1)
            dve.wait_ge(s_w, 16 * weights)
            nc.vector.tensor_scalar(kbias[:, 0, :], bk[:, :], DK ** -0.5, None, ALU.mult).then_inc(s_kb, 1)
            dve.wait_ge(s_kb, 2)
            for e in range(2):
                nc.vector.tensor_scalar(kbias[:, 1 + e, :], kbias[:, 0, :], rel_ends[:, e:e + 1], None,
                                        ALU.add).then_inc(s_kb, 1)
            dve.wait_ge(s_rk, 16)
            nc.vector.tensor_copy(rk_parts[:, 0, :], rk[:, :]).then_inc(s_rkp, 1)
            dve.wait_ge(s_rkp, 1)
            nc.vector.tensor_tensor(rk_rest[:, :], rk[:, :], rk_parts[:, 0, :], ALU.subtract).then_inc(s_rkp, 1)
            dve.wait_ge(s_rkp, 2)
            nc.vector.tensor_copy(rk_parts[:, 1, :], rk_rest[:, :]).then_inc(s_rkp, 1)
            dve.wait_ge(s_rkp, 3)
            nc.vector.tensor_tensor(rk_parts[:, 2, :], rk_rest[:, :], rk_parts[:, 1, :],
                                    ALU.subtract).then_inc(s_rkp, 1)
            def pair(gg, first):
                for par in range(2):
                    g = gg * 2 + par
                    dve.wait_ge(s_x[par], gg * 16 + 16)
                    for t in range(TPC):
                        nc.vector.bn_stats(stats[:, t, :], xin[:, par, t, :]).then_inc(s_st, 1)
                    dve.wait_ge(s_st, g * TPC + TPC)
                    dve.nop(nofuse=True)
                    for t in range(TPC):
                        nc.vector.bn_aggr(moments[:, par, t, :], stats[:, t, :]).then_inc(s_mo, 1)
                    dve.wait_ge(s_std, g + 1)
                    nc.vector.reciprocal(rstd[:, par, :], std[:, par, :]).then_inc(s_rstd, 1)
                    dve.wait_ge(s_rstd, g + 1)
                    for t in range(TPC):
                        ins = nc.vector.tensor_scalar(xn[:, par, t, :], xin[:, par, t, :], moments[:, par, t, 0:1],
                                                      rstd[:, par, t:t + 1], ALU.subtract, ALU.mult)
                    ins.then_inc(s_xn, 1)
                    if not first:
                        dve.wait_ge(s_xcw[par], gg * 16)
                    dve.wait_ge(s_xt, g + 1)
                    for k in range(KD):
                        ins = nc.vector.tensor_copy(xc[par][:, k, :], xt_ps[k][:, :])
                    ins.then_inc(s_xc, 1)
                    for v in range(NFULL):
                        i = g * NFULL + v
                        dve.wait_ge(s_f, i + NFULL + 1)
                        if not (first and par == 0 and v < 2):
                            dve.wait_ge(s_plw[v % 2], (g * (NFULL // 2) + v // 2) * 16)
                        nc.vector.tensor_copy(planes[:, v % 2, 0, :], full[:, v % 2, :]).then_inc(s_hi, 1)
                        dve.wait_ge(s_pl, i + 1)
                        dve.wait_ge(s_hi, i + 1)
                        nc.vector.tensor_tensor(rest[:, v % 2, :], full[:, v % 2, :], planes[:, v % 2, 0, :],
                                                ALU.subtract).then_inc(s_fr, 1)
                    for t in range(TPC):
                        if t % 2 == 0:
                            dve.wait_ge(s_v, g * 3 + t // 2 + 1)
                        ins = nc.vector.tensor_tensor(
                            keep["v"][:, :, g * TPC + t, :],
                            v_ps[t // 2][:, (t % 2) * D:(t % 2 + 1) * D].rearrange("p (h d) -> p h d", h=H),
                            bv[:, :].rearrange("p (h d) -> p h d", h=H), ALU.add)
                        if t % 2:
                            ins.then_inc(s_ve, 1)
                    dve.wait_ge(s_v, g * 3 + 3)
                    nc.vector.tensor_copy(keep["logits"][:, bass.ds(g * TPC, TPC), :],
                                          r_ps[:, 0:TPC * NE].rearrange("p (t e) -> p t e", t=TPC)).then_inc(s_ve, 1)

            pair(0, True)
            with dve.Fori(1, NCH // 2) as gg:
                pair(gg, False)

        @block.tensor
        def _(pe):
            pe.wait_ge(s_id, 3)
            pe.wait_ge(s_w, 16 * weights)
            with pe.Fori(0, NCH // 2) as gg:
                for par in range(2):
                    g = gg * 2 + par
                    pe.wait_ge(s_xn, g + 3)
                    pe.wait_ge(s_xc, g + 1)
                    for k in range(KD):
                        for t in range(TPC):
                            ins = nc.tensor.transpose(xt_ps[k][:, t * P:(t + 1) * P],
                                                      xn[:, par, t, k * P:(k + 1) * P], keep["ident"][:, :])
                    ins.then_inc(s_xt, 1)
                    pe.wait_ge(s_xc, g + 2)
                    for w, half, read in ((wq, 0, 5), (wq, 1, 8), (wk, 0, NFULL + 1), (wk, 1, NFULL + 2)):
                        pe.wait_ge(s_f, g * NFULL + read)
                        for k in range(KD):
                            ins = nc.tensor.matmul(qk_ps[half][:, :], w[:, k, half * P:(half + 1) * P],
                                                   xc[par][:, k, :], start=(k == 0), stop=(k == KD - 1))
                        ins.then_inc(s_qk, 1)
                    for t in range(TPC):
                        if t % 2 == 0:
                            pe.wait_ge(s_ve, g * 3 + t // 2 + 1)
                        for k in range(KD):
                            ins = nc.tensor.matmul(v_ps[t // 2][:, (t % 2) * D:(t % 2 + 1) * D],
                                                   xc[par][:, k, t * P:(t + 1) * P], wv[:, k, :],
                                                   start=(k == 0), stop=(k == KD - 1))
                        if t % 2:
                            ins.then_inc(s_v, 1)
                    pe.wait_ge(s_ve, g * 3 + 3)
                    for t in range(TPC):
                        for k in range(KD):
                            ins = nc.tensor.matmul(r_ps[:, t * NE:(t + 1) * NE], xc[par][:, k, t * P:(t + 1) * P],
                                                   wr[:, k, :], start=(k == 0), stop=(k == KD - 1))
                    ins.then_inc(s_v, 1)


def attend(nc, hbm, keep):
    with ExitStack() as ctx:
        def sb(name, shape, dt=FP32):
            return ctx.enter_context(nc.sbuf_tensor(name, shape, dt))

        def sem(name):
            return ctx.enter_context(nc.semaphore(name))

        SLOTS_P, SLOTS_PT = 4, 2 * BANKS
        PROBW = WIN + 2 * P
        q_stack = [sb(f"q_stack{i}", [PARTS, L], BF16) for i in range(2)]
        k_stack = [sb(f"k_stack{i}", [PARTS, 3, L], BF16) for i in range(2)]
        v_head = [sb(f"v_head{i}", [P, NB, 3, VC], BF16) for i in range(2)]
        v_rest = sb("v_rest", [P, NB, DK])
        rv_parts = sb("rv_parts", [P, RELW // P, 3, DK], BF16)
        rv_rest = sb("rv_rest", [P, RELW // P, DK])
        ident16 = sb("ident16", [P, P], FP16)
        rel = [sb(f"rel{i}", [P, RELW]) for i in range(2)]
        skewed = [sb(f"skewed{i}", [P, WIN]) for i in range(2)]
        scores = [sb(f"scores{i}", [P, L]) for i in range(SLOTS_P)]
        probs = [sb(f"probs{i}", [P, 2, L + 2 * P], FP16) for i in range(SLOTS_P)]
        unskewed = [sb(f"unskewed{i}", [P, 2, RELW], FP16) for i in range(2)]
        pt = [sb(f"pt{i}", [P, 2, CH], FP16) for i in range(SLOTS_PT)]
        no_values = sb("no_values", [P, 3 * VC], BF16)
        zeros = sb("zeros", [P, CH])
        part_max = sb("part_max", [P, 2, 8])
        neg_max = sb("neg_max", [P, 2])
        exp_bias = sb("exp_bias", [P, 2])
        row_sum = sb("row_sum", [P, 8])
        inv_sum = sb("inv_sum", [P, 2])
        o_sum = sb("o_sum", [P, 2, VC])
        o_lo = sb("o_lo", [P, 2, DK])
        o_hi = sb("o_hi", [P, 2, DK])
        psum = [ctx.enter_context(nc.psum_tensor(f"pb{i}", [P, CH], FP32)) for i in range(BANKS + 2)]
        score_ps, o_ps = psum[:BANKS], psum[BANKS:]
        t_ps = [ctx.enter_context(nc.psum_tensor(f"pt_ps{i}", [P, 2, CH], FP16)) for i in range(BANKS)]

        s_pad = sem("b_pads")
        s_stk = [sem(f"b_stacks{i}") for i in range(2)]
        s_vh = sem("b_v_head")
        s_g = sem("b_rel_product")
        s_ge = sem("b_rel_on_chip")
        s_gw = [sem(f"b_rel_stored{i}") for i in range(2)]
        s_gr = [sem(f"b_skewed{i}") for i in range(2)]
        s_s = sem("b_scores")
        s_add = sem("b_scores_added")
        s_nm = sem("b_neg_max")
        s_rm = sem("b_raw_max")
        s_exp = sem("b_exp")
        s_hi = sem("b_high")
        s_lo = sem("b_low")
        s_vp = sem("b_v_parts")
        s_rv = sem("b_rel_v_parts")
        s_pw = [sem(f"b_probs_stored{i}") for i in range(2)]
        s_pr = [sem(f"b_unskewed{i}") for i in range(2)]
        s_t = sem("b_transposed")
        s_ev = {"act": sem("b_t_evac_act"), "dve": sem("b_t_evac_dve")}
        s_pv = sem("b_pt_used")
        s_o1 = sem("b_out_scaled")
        s_o = sem("b_out_read")
        block = ctx.enter_context(nc.Block())
        pad_tensors = 2 * SLOTS_P + 2

        def skew_src(slot, width):
            return bass.AP(hbm["rel_scratch"].tensor, slot * P * RELW + P - 1, [[RELW - 1, P], [1, width]])

        def unskew_src(slot, width):
            return bass.AP(hbm["prob_scratch"].tensor, slot * P * 2 * PROBW + 1,
                           [[2 * PROBW + 1, P], [PROBW, 2], [1, width]])

        def pipeline(eng, step):
            for k in range(PEEL):
                step(0, k)
            with eng.Fori(0, UNITS // STEP - 1) as it:
                for k in range(PEEL, PEEL + STEP):
                    step(it, k)
            for k in range(PEEL, STEP + LAG_O):
                step(UNITS // STEP - 1, k)

        def exists(it, k):
            return not isinstance(it, int) or 0 <= STEP * it + k < UNITS

        def uses(it, k, slots, inc=1):
            return it * (STEP // slots * inc) + (k // slots + 1) * inc

        def bank_of(kind, k, n):
            return score_ps[ITEM_INDEX[(kind, k, n)] % BANKS]

        def wait_bank(it, kind, k, n):
            i = ITEM_INDEX[(kind, k, n)] - BANKS
            while i >= 0 and not exists(it, BANK_ITEMS[i][1]):
                i -= BANKS
            if i >= 0:
                last, u, m = BANK_ITEMS[i]
                if last == "scores":
                    nc.tensor.wait_ge(s_add, it * (4 * STEP) + 4 * u + m + 1)
                else:
                    nc.tensor.wait_ge(s_ge, rel_group_index(it, u) + m + 1)

        def load_stacks(sp, it, head):
            b = head % 2
            for s in range(6):
                rows = bass.ds((it + head // 2) * DK, DK)
                sp.dma_start(q_stack[b][DK * s:DK * (s + 1), :],
                             hbm["planes"][0, Q_PLANES[s], rows, b * L:(b + 1) * L]).then_inc(s_stk[b], 16)
                sp.dma_start(k_stack[b][DK * s:DK * (s + 1), :, :],
                             hbm["planes"][1:4, K_PLANES[s], rows, b * L:(b + 1) * L].rearrange(
                                 "v d n -> d v n")).then_inc(s_stk[b], 16)

        STK = 12 * 16

        @block.sync
        def _(sp):
            load_stacks(sp, 0, 0)

            def step(it, k):
                if k >= LAG_RSTORE and exists(it, k - LAG_RSTORE):
                    u = k - LAG_RSTORE
                    sp.wait_ge(s_ge, rel_group_index(it, u + 1))
                    sp.nop(nofuse=True)
                    if u >= 2:
                        sp.wait_ge(s_gr[u % 2], uses(it, u - 2, 2, 16))
                        sp.nop(nofuse=True)
                    w = (blocks(u % NB) + 1) * P
                    sp.dma_start(hbm["rel_scratch"][u % 2, :, 0:w], rel[u % 2][:, 0:w]).then_inc(s_gw[u % 2], 16)
                if k >= LAG_SKEW and exists(it, k - LAG_SKEW):
                    u = k - LAG_SKEW
                    sp.wait_ge(s_gw[u % 2], uses(it, u, 2, 16))
                    sp.nop(nofuse=True)
                    if u >= 2:
                        sp.wait_ge(s_add, it * (4 * STEP) + 4 * (u - 1))
                        sp.nop(nofuse=True)
                    w = blocks(u % NB) * P
                    sp.dma_start(skewed[u % 2][:, 0:w], skew_src(u % 2, w)).then_inc(s_gr[u % 2], 16)
                if k >= LAG_UNSKEW and exists(it, k - LAG_UNSKEW):
                    u = k - LAG_UNSKEW
                    sp.wait_ge(s_pw[u % 2], uses(it, u, 2, 16))
                    sp.nop(nofuse=True)
                    if u >= 2:
                        sp.wait_ge(s_t, t_group_index(it, u - 1))
                        sp.nop(nofuse=True)
                    w = (blocks(u % NB) + 1) * P
                    sp.dma_start(unskewed[u % 2][:, :, 0:w], unskew_src(u % 2, w)).then_inc(s_pr[u % 2], 16)
                if k >= LAG_PSTORE and exists(it, k - LAG_PSTORE):
                    u = k - LAG_PSTORE
                    c = u % NB
                    sp.wait_ge(s_lo, it * STEP + u + 1)
                    sp.nop(nofuse=True)
                    if u >= 2:
                        sp.wait_ge(s_pr[u % 2], uses(it, u - 2, 2, 16))
                        sp.nop(nofuse=True)
                    col, w = (c + window(c)[0]) * P, (blocks(c) + 2) * P
                    sp.dma_start(hbm["prob_scratch"][u % 2, :, :, 0:w],
                                 probs[u % SLOTS_P][:, :, col:col + w]).then_inc(s_pw[u % 2], 16)
                if k % NB == 6 and exists(it, k + NB):
                    head = k // NB + 1
                    if head >= 2:
                        sp.wait_ge(s_s, it * (4 * STEP) + 4 * NB * (head - 1))
                        sp.nop(nofuse=True)
                    load_stacks(sp, it, head)

            pipeline(sp, step)

        @block.gpsimd
        def _(pool):
            nc.gpsimd.memset(zeros[:, :], 0.0).then_inc(s_pad, 1)
            nc.gpsimd.memset(no_values[:, :], 0.0).then_inc(s_pad, 1)
            for i in range(SLOTS_P):
                nc.gpsimd.memset(probs[i][:, :, 0:P], 0.0).then_inc(s_pad, 1)
                nc.gpsimd.memset(probs[i][:, :, P + L:], 0.0).then_inc(s_pad, 1)
            nc.gpsimd.tensor_copy(ident16[:, :], keep["ident"][:, :]).then_inc(s_rv, 1)
            for i in range(2):
                for col in (0, VC - 1):
                    nc.gpsimd.memset(v_head[i][:, :, 0, col:col + 1], 1.0)
                    ins = nc.gpsimd.memset(v_head[i][:, :, 1:3, col:col + 1], 0.0)
            nc.gpsimd.tensor_copy(rv_parts[:, :, 0, :], keep["rv"][:, :, :]).then_inc(s_rv, 1)
            pool.wait_ge(s_rv, 2)
            nc.gpsimd.tensor_tensor(rv_rest[:, :, :], keep["rv"][:, :, :], rv_parts[:, :, 0, :],
                                    ALU.subtract).then_inc(s_rv, 1)
            pool.wait_ge(s_rv, 3)
            nc.gpsimd.tensor_copy(rv_parts[:, :, 1, :], rv_rest[:, :, :]).then_inc(s_rv, 1)
            pool.wait_ge(s_rv, 4)
            nc.gpsimd.tensor_tensor(rv_parts[:, :, 2, :], rv_rest[:, :, :], rv_parts[:, :, 1, :],
                                    ALU.subtract).then_inc(s_rv, 1)

            def v_parts(it, head):
                v = keep["v"][:, it + head // 2, (head % 2) * NB:(head % 2 + 1) * NB, :]
                parts = v_head[head % 2]
                n = it * 6 + head * 3
                if head >= 1:
                    pool.wait_ge(s_pv, t_group_index(it, (head - 1) * NB) + 1)
                    pool.nop(nofuse=True)
                nc.gpsimd.tensor_copy(parts[:, :, 0, 1:1 + DK], v).then_inc(s_vp, 1)
                pool.wait_ge(s_vp, n + 1)
                pool.nop(nofuse=True)
                nc.gpsimd.tensor_tensor(v_rest[:, :, :], v, parts[:, :, 0, 1:1 + DK], ALU.subtract).then_inc(s_vp, 1)
                pool.wait_ge(s_vp, n + 2)
                pool.nop(nofuse=True)
                nc.gpsimd.tensor_copy(parts[:, :, 1, 1:1 + DK], v_rest[:, :, :]).then_inc(s_vp, 1)
                pool.wait_ge(s_vp, n + 3)
                nc.gpsimd.tensor_tensor(parts[:, :, 2, 1:1 + DK], v_rest[:, :, :], parts[:, :, 1, 1:1 + DK],
                                        ALU.subtract).then_inc(s_vh, 1)

            def step(it, k):
                if k % NB == 0 and exists(it, k):
                    v_parts(it, k // NB)
                u = k - LAG_E
                if u >= 0 and exists(it, u):
                    pool.wait_ge(s_hi, it * STEP + u + 1)
                    nc.gpsimd.tensor_tensor(probs[u % SLOTS_P][:, 1, P:P + L], scores[u % SLOTS_P][:, :],
                                            probs[u % SLOTS_P][:, 0, P:P + L], ALU.subtract).then_inc(s_lo, 1)

            pipeline(pool, step)

        @block.tensor
        def _(pe):
            pe.sem_inc(s_pv, 1)
            pe.wait_ge(s_pad, pad_tensors)
            pe.wait_ge(s_rv, 5)

            def rel_group(it, k, n):
                c = k % NB
                if n == 0 and c == 0:
                    pe.wait_ge(s_stk[(k // NB) % 2], it * STK + (k // NB // 2 + 1) * STK)
                wait_bank(it, "rel", k, n)
                j0 = (window(c)[0] - M_LO) * P + n * CH
                w = min(CH, (blocks(c) + 1) * P - n * CH)
                nc.tensor.matmul(bank_of("rel", k, n)[:, 0:w], q_stack[(k // NB) % 2][:, c * P:(c + 1) * P],
                                 keep["rk_stack"][:, j0:j0 + w], start=True, stop=True).then_inc(s_g, 1)

            def score_bank(it, k, bank):
                c, head = k % NB, k // NB
                wait_bank(it, "scores", k, bank)
                ps = bank_of("scores", k, bank)
                for _, a, z, kind in [s for s in segments(c) if s[0] == bank]:
                    ins = nc.tensor.matmul(ps[:, a - bank * CH:z - bank * CH],
                                           q_stack[head % 2][:, c * P:(c + 1) * P],
                                           k_stack[head % 2][:, kind, a:z], start=True, stop=True)
                ins.then_inc(s_s, 1)

            def transposes(it, k, g):
                c = k % NB
                idx = t_group_static(k) + g
                if idx >= BANKS:
                    e, n = evac_of(it, k, g - BANKS)
                    pe.wait_ge(s_ev[e], n)
                if g == 0:
                    pe.wait_ge(s_lo, it * STEP + k + 1)
                if g == PGROUPS:
                    pe.wait_ge(s_pr[k % 2], uses(it, k, 2, 16))
                for part in range(2):
                    for i, blk in enumerate(group_blocks(c, g)):
                        src = probs[k % SLOTS_P][:, part, (1 + blk) * P:(2 + blk) * P] if g < PGROUPS else \
                            unskewed[k % 2][:, part, blk * P:(blk + 1) * P]
                        ins = nc.tensor.transpose(t_ps[idx % BANKS][:, part, i * P:(i + 1) * P], src, ident16[:, :])
                ins.then_inc(s_t, 1)

            def values(it, k, g):
                c, head = k % NB, k // NB
                lo, hi = window(c)
                idx = t_group_static(k) + g
                out = o_ps[k % 2][:, 0:3 * VC].rearrange("p (r n) -> p r n", r=3)
                src = pt[idx % SLOTS_PT]
                if g == 0:
                    if c == 0:
                        pe.wait_ge(s_vh, it * 2 + head + 1)
                    if k >= 2:
                        pe.wait_ge(s_o, it * STEP + k - 1)
                e, n = evac_of(it, k, g)
                pe.wait_ge(s_ev[e], n)
                if g == 0:
                    nc.tensor.matmul(o_ps[k % 2][:, 0:3 * VC], src[:, 0, 0:P], no_values[:, :], start=True, stop=False)
                last_group = g == PGROUPS + rel_groups(c) - 1
                blks = group_blocks(c, g)
                for i, blk in enumerate(blks):
                    if g < PGROUPS:
                        a, z = (0, DK + 1) if blk < c + lo else (1, DK + 2) if blk > c + hi else (1, DK + 1)
                        rhs = v_head[head % 2][:, blk, :, a:z]
                    else:
                        a, z = 1, DK + 1
                        rhs = rv_parts[:, blk + lo - M_LO, :, :]
                    for part in range(2):
                        ins = nc.tensor.matmul(out[:, :, a:z], src[:, part, i * P:(i + 1) * P], rhs, start=False,
                                               stop=last_group and i == len(blks) - 1 and part == 1)
                ins.then_inc(s_pv, 1)

            def step(it, k):
                work = []
                if k >= LAG_S and exists(it, k - LAG_S):
                    work += [(score_bank, k - LAG_S, bank) for bank in range(4)]
                if exists(it, k):
                    work += [(rel_group, k, n) for n in range(rel_groups(k % NB))]
                u = k - LAG_T
                groups = PGROUPS + rel_groups(u % NB) if u >= 0 and exists(it, u) else 0
                pending = []
                if u >= 1 and exists(it, u - 1):
                    last = PGROUPS + rel_groups((u - 1) % NB) - 1
                    pending = [(u - 1, last - 1), (u - 1, last)]
                for g in range(groups):
                    transposes(it, u, g)
                    if work:
                        f, a, n = work.pop(0)
                        f(it, a, n)
                    pending.append((u, g))
                    if len(pending) > 2:
                        values(it, *pending.pop(0))
                for f, a, n in work:
                    f(it, a, n)
                if not groups:
                    for unit, g in pending:
                        values(it, unit, g)

            pipeline(pe, step)

        def evacuate(eng_name, eng, it, k, g):
            c = k % NB
            lo, hi = window(c)
            idx = t_group_static(k) + g
            eng.wait_ge(s_t, t_group_index(it, k) + g + 1)
            if idx >= SLOTS_PT:
                eng.wait_ge(s_pv, t_group_index(it, k) + g + 2 - SLOTS_PT)
            blks = group_blocks(c, g)
            dst, src = pt[idx % SLOTS_PT], t_ps[idx % BANKS]
            a, z = 0, len(blks) * P
            if eng_name == "act":
                nc.scalar.copy(dst[:, :, a:z], src[:, :, a:z]).then_inc(s_ev["act"], 1)
                return
            if g == PGROUPS and lo == M_LO and c + lo > 0:
                ins = nc.vector.tensor_tensor(dst[:, :, 0:P], src[:, :, 0:P], keep["mask"][:, 0, :, :], ALU.mult)
                a = P
            if g == PGROUPS + rel_groups(c) - 1 and hi == M_HI and c + hi < NB - 1:
                z -= P
                ins = nc.vector.tensor_tensor(dst[:, :, z:z + P], src[:, :, z:z + P], keep["mask"][:, 1, :, :],
                                              ALU.mult)
            if a < z:
                ins = nc.vector.tensor_copy(dst[:, :, a:z], src[:, :, a:z])
            ins.then_inc(s_ev["dve"], 1)

        @block.scalar
        def _(act):
            act.wait_ge(s_pad, pad_tensors)

            def rel_evac(it, k, n):
                act.wait_ge(s_g, rel_group_index(it, k) + n + 1)
                if n == 0 and k >= 2:
                    act.wait_ge(s_gw[k % 2], uses(it, k - 2, 2, 16))
                w = min(CH, (blocks(k % NB) + 1) * P - n * CH)
                nc.scalar.copy(rel[k % 2][:, n * CH:n * CH + w], bank_of("rel", k, n)[:, 0:w]).then_inc(s_ge, 1)

            def exponentials(it, k):
                act.wait_ge(s_nm, it * STEP + k + 1)
                nc.scalar.activation(scores[k % SLOTS_P][:, :], scores[k % SLOTS_P][:, :], ACT.Exp,
                                     bias=exp_bias[:, k % 2:k % 2 + 1],
                                     accum_out=row_sum[:, k % 8:k % 8 + 1]).then_inc(s_exp, 1)

            def step(it, k):
                work = [None] * 4 if k >= LAG_S and exists(it, k - LAG_S) else []
                if exists(it, k):
                    work += list(range(rel_groups(k % NB)))
                u = k - LAG_T
                plan = evac_plan(u % NB) if u >= 0 and exists(it, u) else []
                for g, e in enumerate(plan):
                    if e == "act":
                        evacuate("act", act, it, u, g)
                    if work:
                        n = work.pop(0)
                        if n is not None:
                            rel_evac(it, k, n)
                    if g == 0 and exists(it, k - LAG_E):
                        exponentials(it, k - LAG_E)
                for n in work:
                    if n is not None:
                        rel_evac(it, k, n)
                if not plan and k >= LAG_E and exists(it, k - LAG_E):
                    exponentials(it, k - LAG_E)

            pipeline(act, step)

        @block.vector
        def _(dve):
            dve.wait_ge(s_pad, pad_tensors)

            def add_bank(it, k, bank):
                c = k % NB
                lo = window(c)[0]
                dve.wait_ge(s_s, it * (4 * STEP) + 4 * k + bank + 1)
                if bank == 0:
                    dve.wait_ge(s_gr[k % 2], uses(it, k, 2, 16))
                    if k >= SLOTS_P:
                        dve.wait_ge(s_lo, it * STEP + k - SLOTS_P + 1)
                    if k >= 2:
                        dve.wait_ge(s_exp, it * STEP + k - 1)
                dve.nop(nofuse=True)
                ps = bank_of("scores", k, bank)
                for n, (bk_, a, z, kind) in enumerate(segments(c)):
                    if bk_ != bank:
                        continue
                    col = a - (c + lo) * P
                    other = skewed[k % 2][:, col:col + z - a] if kind == 0 else zeros[:, 0:z - a]
                    ins = nc.vector.tensor_tensor_reduce(
                        out=scores[k % SLOTS_P][:, a:z], in0=ps[:, a - bank * CH:z - bank * CH],
                        in1=other, scale=1.0, scalar=-3.0e38, op0=ALU.add, op1=ALU.max,
                        accum_out=part_max[:, k % 2, n:n + 1])
                ins.then_inc(s_add, 1)

            def raw_maximum(it, k):
                dve.wait_ge(s_add, it * (4 * STEP) + 4 * k + 4)
                nc.vector.tensor_reduce(neg_max[:, k % 2:k % 2 + 1], part_max[:, k % 2, 0:len(segments(k % NB))],
                                        axis=AX.X, op=ALU.max, negate=True).then_inc(s_rm, 1)

            def maximum(it, k):
                dve.wait_ge(s_rm, it * STEP + k + 1)
                nc.vector.tensor_scalar(exp_bias[:, k % 2:k % 2 + 1], neg_max[:, k % 2:k % 2 + 1], PROB_SCALE_LN,
                                        None, ALU.add).then_inc(s_nm, 1)

            def high_part(it, k):
                dve.wait_ge(s_exp, it * STEP + k + 1)
                if k >= SLOTS_P:
                    dve.wait_ge(s_pw[k % 2], uses(it, k - SLOTS_P, 2, 16))
                    dve.wait_ge(s_t, t_group_index(it, k - SLOTS_P + 1))
                nc.vector.tensor_copy(probs[k % SLOTS_P][:, 0, P:P + L], scores[k % SLOTS_P][:, :]).then_inc(s_hi, 1)

            def output(it, k, link):
                c, head = k % NB, k // NB
                lo, hi = window(c)
                total = o_sum[:, k % 2, :]
                n = it * (4 * STEP) + 4 * k
                if link == 0:
                    dve.wait_ge(s_pv, t_group_index(it, k + 1) + 1)
                    nc.vector.reciprocal(inv_sum[:, k % 2:k % 2 + 1], row_sum[:, k % 8:k % 8 + 1]).then_inc(s_o1, 1)
                    o = o_ps[k % 2][:, 0:3 * VC].rearrange("p (r n) -> p n r", r=3)
                    nc.vector.tensor_reduce(total, o, axis=AX.X, op=ALU.add).then_inc(s_o1, 1)
                if link == 1:
                    dve.wait_ge(s_o1, n + 2)
                    if c + lo > 0:
                        nc.vector.scalar_tensor_tensor(out=o_lo[:, k % 2, :], in0=keep["rv_lo"][:, :],
                                                       scalar=total[:, 0:1], in1=total[:, 1:1 + DK], op0=ALU.mult,
                                                       op1=ALU.add).then_inc(s_o1, 1)
                    else:
                        nc.vector.tensor_copy(o_lo[:, k % 2, :], total[:, 1:1 + DK]).then_inc(s_o1, 1)
                if link == 2:
                    dve.wait_ge(s_o1, n + 3)
                    if c + hi < NB - 1:
                        nc.vector.scalar_tensor_tensor(out=o_hi[:, k % 2, :], in0=keep["rv_hi"][:, :],
                                                       scalar=total[:, 1 + DK:2 + DK], in1=o_lo[:, k % 2, :],
                                                       op0=ALU.mult, op1=ALU.add).then_inc(s_o1, 1)
                    else:
                        dve.sem_inc(s_o1, 1)
                if link == 3:
                    dve.wait_ge(s_o1, n + 4)
                    res = o_hi if c + hi < NB - 1 else o_lo
                    nc.vector.tensor_scalar(keep["v"][:, it + head // 2, (head % 2) * NB + c, :], res[:, k % 2, :],
                                            inv_sum[:, k % 2:k % 2 + 1], None, ALU.mult).then_inc(s_o, 1)

            def step(it, k):
                a, h, t, o = k - LAG_S, k - LAG_E, k - LAG_T, k - LAG_O
                adding = a >= 0 and exists(it, a)
                plan = evac_plan(t % NB) if t >= 0 and exists(it, t) else []
                ends = o >= 0
                for g in range(max(len(plan), 5)):
                    if g == 4 and adding:
                        raw_maximum(it, a)
                    if g < 4 and adding:
                        add_bank(it, a, g)
                    if g < len(plan) and plan[g] == "dve":
                        evacuate("dve", dve, it, t, g)
                    if 2 <= g <= 4 and ends:
                        output(it, o, g - 2)
                    if g == 3 and h >= 0 and exists(it, h):
                        high_part(it, h)
                if adding:
                    maximum(it, a)
                if ends:
                    output(it, o, 3)

            pipeline(dve, step)


def mix(nc, hbm, keep):
    with ExitStack() as ctx:
        def sb(name, shape, dt=FP32):
            return ctx.enter_context(nc.sbuf_tensor(name, shape, dt))

        def sem(name):
            return ctx.enter_context(nc.semaphore(name))

        NT = TOK // P
        logits = keep["logits"]
        wo = sb("wo", [P, KD, D])
        bias9 = sb("bias9", [NE + 1, D])
        x_res = sb("x_res", [P, 2, D])
        attn_tile = [sb(f"attn_tile{i}", [P, H, DK]) for i in range(2)]
        gates_tile = [sb(f"gates_tile{i}", [P, NE + 1]) for i in range(2)]
        attn_t = [sb(f"attn_t{i}", [P, KD, P]) for i in range(2)]
        gates_t = [sb(f"gates_t{i}", [NE + 1, P]) for i in range(2)]
        xT = sb("xT_sb", [P, KD, TOK])
        y = sb("y_sb", [P, NT, D])
        gw = [sb(f"gate_w{i}", [P, KD, F]) for i in range(2)]
        uw = [sb(f"up_w{i}", [P, KD, F]) for i in range(2)]
        dw = [sb(f"down_w{i}", [P, FT, D]) for i in range(2)]
        gb = [sb(f"gate_b{i}", [P, FT]) for i in range(2)]
        ub = [sb(f"up_b{i}", [P, FT]) for i in range(2)]
        ge = [sb(f"gates_e{i}", [P, NT]) for i in range(2)]
        act_g = [sb(f"silu{i}", [P, CH]) for i in range(2)]
        hid = [sb(f"hidden{i}", [P, FT, CH]) for i in range(2)]
        peak = sb("peak", [P, NT, 1])
        prob = sb("prob", [P, NT, NE])
        total = sb("total", [P, NT, 1])
        rest = sb("prob_rest", [P, NT, NE])
        same = sb("same", [P, NT, NE])
        index = sb("index", [P, NT, NE])
        index_i = sb("index_i", [P, NT, NE], mybir.dt.int32)
        pick = sb("pick", [P, NT, NE])
        first = sb("first", [P, NT, 1])
        chosen = sb("chosen", [P, 2, NT, NE])
        gates = sb("gates", [P, NT, NE + 1])
        psum = [ctx.enter_context(nc.psum_tensor(f"pc{i}", [P, CH], FP32)) for i in range(8)]

        s_w = sem("c_weights")
        s_x = [sem(f"c_x{i}") for i in range(2)]
        s_xt = sem("c_xT")
        s_ix = sem("c_index")
        s_r = sem("c_router")
        s_re = sem("c_router_exp")
        s_in = sem("c_tile_in")
        s_t = sem("c_tile_transposed")
        s_te = sem("c_tile_on_chip")
        s_p = sem("c_projected")
        s_y = sem("c_y_started")
        s_ew = [sem(f"c_expert{i}") for i in range(2)]
        s_ge = sem("c_gates_e")
        s_gu = sem("c_gate_up")
        s_si = sem("c_silu")
        s_h = sem("c_hidden")
        s_d = sem("c_down")
        s_ye = sem("c_y_added")
        s_out = sem("c_out")
        block = ctx.enter_context(nc.Block())

        def load_expert(sp, e, i):
            sp.dma_start(gw[i][:, :, :], hbm["gate_w"][e, :, :].rearrange("(k p) f -> p k f", p=P)).then_inc(s_ew[i], 16)
            sp.dma_start(uw[i][:, :, :], hbm["up_w"][e, :, :].rearrange("(k p) f -> p k f", p=P)).then_inc(s_ew[i], 16)
            sp.dma_start(dw[i][:, :, :], hbm["down_w"][e, :, :].rearrange("(k p) d -> p k d", p=P)).then_inc(s_ew[i], 16)
            sp.dma_start(gb[i][:, :], hbm["gate_b"][e, :, :]).then_inc(s_ew[i], 16)
            sp.dma_start(ub[i][:, :], hbm["up_b"][e, :, :]).then_inc(s_ew[i], 16)

        EW = 5 * 16

        @block.sync
        def _(sp):
            sp.dma_start(wo[:, :, :], hbm["woT"].rearrange("(k p) n -> p k n", p=P)).then_inc(s_w, 16)
            sp.dma_start(bias9[0:NE, :], hbm["down_b"]).then_inc(s_w, 16)
            sp.dma_start(bias9[NE:NE + 1, :], hbm["bo"]).then_inc(s_w, 16)
            sp.dma_start(xT[:, :, :], hbm["xT"]).then_inc(s_xt, 16)
            for i in range(2):
                load_expert(sp, i, i)
            with sp.Fori(0, NT // 2) as tt:
                for par in range(2):
                    sp.wait_ge(s_y, tt * 2 + par + 1)
                    sp.nop(nofuse=True)
                    sp.dma_start(x_res[:, par, :], hbm["x"][bass.ds(tt * (2 * P) + par * P, P), :]).then_inc(s_x[par], 16)
            with sp.Fori(0, NE // 2 - 1) as ee:
                for i in range(2):
                    sp.wait_ge(s_ye, ee * (2 * NT) + (i + 1) * NT + 1)
                    sp.nop(nofuse=True)
                    sp.wait_ge(s_h, ee * (2 * NCH * FT) + (i + 1) * NCH * FT)
                    sp.nop(nofuse=True)
                    load_expert(sp, ee * 2 + i + 2, i)
            for c in range(NCH):
                sp.wait_ge(s_ye, (NE - 1) * NT + (c + 1) * TPC + 1)
                sp.nop(nofuse=True)
                sp.dma_start(hbm["out"][c * CH:(c + 1) * CH, :].rearrange("(t p) d -> p t d", p=P),
                             y[:, c * TPC:(c + 1) * TPC, :]).then_inc(s_out, 16)
            sp.wait_ge(s_out, 16 * NCH)
            sp.nop(nofuse=True)

        @block.gpsimd
        def _(pool):
            nc.gpsimd.iota(index_i[:, :, :], pattern=[[0, NT], [1, NE]], base=-NE, channel_multiplier=0).then_inc(s_ix, 1)
            pool.wait_ge(s_ix, 1)
            nc.gpsimd.tensor_copy(index[:, :, :], index_i[:, :, :]).then_inc(s_ix, 1)

        @block.scalar
        def _(act):
            act.wait_ge(s_r, 2)
            nc.scalar.activation(prob[:, :, :], rest[:, :, :], ACT.Exp).then_inc(s_re, 1)
            act.wait_ge(s_r, ROUTER_LINKS)
            with act.Fori(0, B) as b:
                with act.Fori(0, NB // 2) as cc:
                    for par in range(2):
                        n = b * NB + cc * 2 + par
                        act.wait_ge(s_te, n + 1)
                        nc.scalar.copy(attn_tile[par][:, :, :], keep["v"][:, :, n, :])
                        nc.scalar.copy(gates_tile[par][:, :], gates[:, n, :]).then_inc(s_in, 1)
            with act.Fori(0, NE // 2) as ee:
                for i in range(2):
                    act.wait_ge(s_ew[i], ee * EW + EW)
                    act.wait_ge(s_ye, (ee * 2 + i) * NT + 1)
                    nc.scalar.copy(ge[i][:, :], gates[:, :, ee * 2 + i]).then_inc(s_ge, 1)
                    for c in range(NCH):
                        for f in range(FT):
                            n = ee * (2 * NCH * FT) + (i * NCH + c) * FT + f
                            act.wait_ge(s_gu, n * 2 + 1)
                            act.wait_ge(s_h, n + 1)
                            nc.scalar.activation(act_g[f % 2][:, :], psum[f % 2][:, :], ACT.Silu,
                                                 bias=gb[i][:, f:f + 1]).then_inc(s_si, 1)

        @block.vector
        def _(dve):
            dve.sem_inc(s_y, 2)
            dve.sem_inc(s_te, 2)
            dve.sem_inc(s_h, 2)
            dve.sem_inc(s_ye, 1)
            links = [0]

            def link(ins):
                links[0] += 1
                ins.then_inc(s_r, 1)
                dve.wait_ge(s_r, links[0])

            wide = [P, NT, NE]
            link(nc.vector.tensor_reduce(peak[:, :, :], logits[:, :, :], axis=AX.X, op=ALU.max))
            link(nc.vector.tensor_tensor(rest[:, :, :], logits[:, :, :], peak[:, :, :].to_broadcast(wide), ALU.subtract))
            dve.wait_ge(s_re, 1)
            link(nc.vector.tensor_reduce(total[:, :, :], prob[:, :, :], axis=AX.X, op=ALU.add))
            link(nc.vector.reciprocal(total[:, :, :], total[:, :, :]))
            link(nc.vector.tensor_tensor(prob[:, :, :], prob[:, :, :], total[:, :, :].to_broadcast(wide), ALU.mult))
            link(nc.vector.tensor_copy(rest[:, :, :], prob[:, :, :]))
            dve.wait_ge(s_ix, 2)
            for r in range(2):
                link(nc.vector.tensor_reduce(peak[:, :, :], rest[:, :, :], axis=AX.X, op=ALU.max))
                link(nc.vector.tensor_tensor(same[:, :, :], rest[:, :, :], peak[:, :, :].to_broadcast(wide), ALU.is_equal))
                link(nc.vector.tensor_tensor(pick[:, :, :], same[:, :, :], index[:, :, :], ALU.mult))
                link(nc.vector.tensor_reduce(first[:, :, :], pick[:, :, :], axis=AX.X, op=ALU.min))
                link(nc.vector.tensor_tensor(chosen[:, r, :, :], index[:, :, :], first[:, :, :].to_broadcast(wide),
                                             ALU.is_equal))
                if r == 0:
                    link(nc.vector.scalar_tensor_tensor(out=rest[:, :, :], in0=chosen[:, 0, :, :], scalar=-2.0,
                                                        in1=rest[:, :, :], op0=ALU.mult, op1=ALU.add))
            link(nc.vector.tensor_tensor(same[:, :, :], chosen[:, 0, :, :], chosen[:, 1, :, :], ALU.add))
            link(nc.vector.tensor_tensor(prob[:, :, :], prob[:, :, :], same[:, :, :], ALU.mult))
            link(nc.vector.tensor_reduce(total[:, :, :], prob[:, :, :], axis=AX.X, op=ALU.add))
            link(nc.vector.tensor_scalar(total[:, :, :], total[:, :, :], 1e-9, None, ALU.add))
            link(nc.vector.reciprocal(total[:, :, :], total[:, :, :]))
            link(nc.vector.tensor_tensor(gates[:, :, 0:NE], prob[:, :, :], total[:, :, :].to_broadcast(wide), ALU.mult))
            link(nc.vector.memset(gates[:, :, NE:NE + 1], 1.0))
            assert links[0] == ROUTER_LINKS, links
            with dve.Fori(0, NT // 2) as tt:
                for par in range(2):
                    n = tt * 2 + par
                    dve.wait_ge(s_t, n + 1)
                    nc.vector.tensor_copy(attn_t[par][:, :, :], psum[par][:, 0:KD * P].rearrange("p (k l) -> p k l", k=KD))
                    nc.vector.tensor_copy(gates_t[par][:, :], psum[par][0:NE + 1, KD * P:(KD + 1) * P]).then_inc(s_te, 1)
                    dve.wait_ge(s_p, n + 1)
                    dve.wait_ge(s_x[par], tt * 16 + 16)
                    nc.vector.tensor_tensor(y[:, n, :], psum[2 + par][:, 0:D], x_res[:, par, :], ALU.add).then_inc(s_y, 1)
            dve.wait_ge(s_y, NT + 2)
            with dve.Fori(0, NE // 2) as ee:
                for i in range(2):
                    dve.wait_ge(s_ew[i], ee * EW + EW)
                    dve.wait_ge(s_ge, ee * 2 + i + 1)
                    for c in range(NCH):
                        for f in range(FT):
                            n = ee * (2 * NCH * FT) + (i * NCH + c) * FT + f
                            dve.wait_ge(s_gu, n * 2 + 2)
                            dve.wait_ge(s_si, n + 1)
                            nc.vector.scalar_tensor_tensor(out=hid[c % 2][:, f, :], in0=psum[2 + f % 2][:, :],
                                                           scalar=ub[i][:, f:f + 1], in1=act_g[f % 2][:, :],
                                                           op0=ALU.add, op1=ALU.mult).then_inc(s_h, 1)
                        for t in range(TPC):
                            tile = c * TPC + t
                            m = ee * (2 * NT) + i * NT + tile
                            dve.wait_ge(s_d, m + 1)
                            nc.vector.scalar_tensor_tensor(out=y[:, tile, :], in0=psum[4 + t][:, 0:D],
                                                           scalar=ge[i][:, tile:tile + 1], in1=y[:, tile, :],
                                                           op0=ALU.mult, op1=ALU.add).then_inc(s_ye, 1)

        @block.tensor
        def _(pe):
            pe.wait_ge(s_w, 48)
            with pe.Fori(0, NT // 2) as tt:
                for par in range(2):
                    n = tt * 2 + par
                    pe.wait_ge(s_in, n + 1)
                    pe.wait_ge(s_te, n + 1)
                    flat = attn_tile[par][:, :, :].rearrange("p h d -> p (h d)")
                    for k in range(KD):
                        nc.tensor.transpose(psum[par][:, k * P:(k + 1) * P], flat[:, k * P:(k + 1) * P], keep["ident"][:, :])
                    nc.tensor.transpose(psum[par][0:NE + 1, KD * P:(KD + 1) * P], gates_tile[par][:, :],
                                        keep["ident"][:, :]).then_inc(s_t, 1)
                    pe.wait_ge(s_te, n + 3)
                    pe.wait_ge(s_y, n + 1)
                    for k in range(KD):
                        nc.tensor.matmul(psum[2 + par][:, 0:D], attn_t[par][:, k, :], wo[:, k, :], start=(k == 0), stop=False)
                    nc.tensor.matmul(psum[2 + par][:, 0:D], gates_t[par][:, :], bias9[:, :], start=False,
                                     stop=True).then_inc(s_p, 1)
            pe.wait_ge(s_xt, 16)
            pe.wait_ge(s_y, NT + 2)
            with pe.Fori(0, NE // 2) as ee:
                for i in range(2):
                    pe.wait_ge(s_ew[i], ee * EW + EW)
                    for c in range(NCH):
                        for f in range(FT):
                            n = ee * (2 * NCH * FT) + (i * NCH + c) * FT + f
                            pe.wait_ge(s_h, n + 1)
                            for w, bank in ((gw, f % 2), (uw, 2 + f % 2)):
                                for k in range(KD):
                                    ins = nc.tensor.matmul(psum[bank][:, :], w[i][:, k, f * P:(f + 1) * P],
                                                           xT[:, k, c * CH:(c + 1) * CH], start=(k == 0), stop=(k == KD - 1))
                                ins.then_inc(s_gu, 1)
                        for f in range(FT):
                            pe.wait_ge(s_h, ee * (2 * NCH * FT) + (i * NCH + c) * FT + f + 3)
                            for t in range(TPC):
                                if f == 0 and not (i == 0 and c == 0):
                                    pe.wait_ge(s_ye, ee * (2 * NT) + i * NT + (c - 1) * TPC + t + 2)
                                if f == 0 and i == 0 and c == 0 and t == 0:
                                    pe.wait_ge(s_ye, ee * (2 * NT) + 1)
                                ins = nc.tensor.matmul(psum[4 + t][:, 0:D], hid[c % 2][:, f, t * P:(t + 1) * P],
                                                       dw[i][:, f, :], start=(f == 0), stop=(f == FT - 1))
                                if f == FT - 1:
                                    ins.then_inc(s_d, 1)


ROUTER_LINKS = 2 + 4 + 11 + 7


def program(nc, hbm):
    with ExitStack() as ctx:
        def sb(name, shape, dt=FP32):
            return ctx.enter_context(nc.sbuf_tensor(name, shape, dt))

        keep = {
            "ident": sb("ident", [P, P]),
            "logits": sb("logits", [P, TOK // P, NE]),
            "v": sb("v_all", [P, H, B * NB, DK]),
        }
        hbm["xT"] = nc.dram_tensor("xT_scratch", (P, KD, TOK), FP32, kind="Internal").ap()
        hbm["planes"] = nc.dram_tensor("planes_scratch", (4, 3, D, TOK), BF16, kind="Internal").ap()
        hbm["rel_scratch"] = nc.dram_tensor("rel_scratch", (2, P, RELW), FP32, kind="Internal").ap()
        hbm["prob_scratch"] = nc.dram_tensor("prob_scratch", (2, P, 2, WIN + 2 * P), FP16, kind="Internal").ap()
        with ExitStack() as inner:
            def sbi(name, shape, dt=FP32):
                return inner.enter_context(nc.sbuf_tensor(name, shape, dt))

            keep["rk_stack"] = sbi("rk_stack", [PARTS, RELW], BF16)
            keep["rv"] = sbi("rv", [P, RELW // P, DK])
            keep["rv_lo"] = sbi("rv_lo", [P, DK])
            keep["rv_hi"] = sbi("rv_hi", [P, DK])
            keep["mask"] = sbi("mask", [P, 2, 2, P], FP16)
            project(nc, hbm, keep)
            attend(nc, hbm, keep)
        mix(nc, hbm, keep)


def kernel(**inputs):
    import numpy as np
    import concourse.bacc as bacc
    from concourse.bass_utils import run_bass_kernel_spmd

    def a(name):
        return np.asarray(inputs[name])

    row = np.arange(RELW) + REL0 + MAXLEN - 1
    row = np.clip(np.where(row < 0, row + 2 * MAXLEN - 1, row), 0, 2 * MAXLEN - 2)
    rel_k, rel_v = a("L0_attn_relative_k")[row], a("L0_attn_relative_v")[row]
    arrays = {
        "x": a("L0_attn_x").reshape(TOK, D),
        "wqT": a("L0_attn_Wq").T, "wkT": a("L0_attn_Wk").T, "wvT": a("L0_attn_Wv").T, "woT": a("L0_attn_Wo").T,
        "bq": a("L0_attn_bq").reshape(2, P).T, "bk": a("L0_attn_bk").reshape(2, P).T,
        "bv": a("L0_attn_bv").reshape(1, D), "bo": a("L0_attn_bo").reshape(1, D),
        "rel_kT": rel_k.T, "rel_k_ends": np.tile(rel_k[[0, -1]].T, (P // DK, 1)), "rel_v": rel_v,
        "router_wT": a("L0_ffn_router_w").T,
        "gate_w": a("L0_ffn_gate_w"), "up_w": a("L0_ffn_up_w"), "down_w": a("L0_ffn_down_w"),
        "gate_b": a("L0_ffn_gate_b").reshape(NE, FT, P).transpose(0, 2, 1),
        "up_b": a("L0_ffn_up_b").reshape(NE, FT, P).transpose(0, 2, 1),
        "down_b": a("L0_ffn_down_b"),
    }
    arrays = {n: np.ascontiguousarray(v) for n, v in arrays.items()}
    nc = bacc.Bacc("TRN2", target_bir_lowering=False, num_devices=1)
    hbm = {n: nc.dram_tensor(f"in_{n}", v.shape, mybir.dt.from_np(v.dtype), kind="ExternalInput").ap()
           for n, v in arrays.items()}
    hbm["out"] = nc.dram_tensor("out", (TOK, D), FP32, kind="ExternalOutput").ap()
    program(nc, hbm)
    r = run_bass_kernel_spmd(nc, [{f"in_{n}": v for n, v in arrays.items()}], core_ids=[0])
    return r.results[0]["out"].reshape(B, L, D)
```

```python
import math
from contextlib import ExitStack

import concourse.bass as bass
from concourse import mybir

FP32 = mybir.dt.float32
BF16 = mybir.dt.bfloat16
FP16 = mybir.dt.float16
ALU = mybir.AluOpType
ACT = mybir.ActivationFunctionType
AX = mybir.AxisListType

P = 128
B, L, D, H, DK = 2, 2048, 256, 16, 16
MAXLEN = 256
TOK = B * L
BH = B * H
NB = L // P
KD = D // P
CH = 512
NCH = TOK // CH
TPC = CH // P
NE, F = 8, 512
FT = F // P
EPS = 1e-5
PARTS = 6 * DK
Q_PLANES = (0, 0, 1, 1, 0, 2)
K_PLANES = (0, 1, 0, 1, 2, 0)

M_LO, M_HI = -6, 2
WIN = (M_HI - M_LO + 1) * P
RELW = WIN + P
REL0 = P * M_LO - (P - 1)


def window(c):
    return max(M_LO, -c), min(M_HI, NB - 1 - c)


def blocks(c):
    lo, hi = window(c)
    return hi - lo + 1


def rel_groups(c):
    return -(-(blocks(c) + 1) // 4)


GROUPS_BH = sum(rel_groups(c) for c in range(NB))
GROUPS_BEFORE = [sum(rel_groups(i) for i in range(c)) for c in range(NB)]
R_LO, R_HI = -6, 1
RVW = (R_HI - R_LO + 1) * P
PGROUPS = NB // 4
TGROUPS = PGROUPS + 2


def rel_blocks(c):
    return max(R_LO, -(c + 1)), min(R_HI, NB - 1 - c)


def left_end(c):
    return c + R_LO >= 0


def right_end(c):
    return c + R_HI + 1 < NB


def groups_of(c):
    lo, hi = rel_blocks(c)
    return PGROUPS + -(-(hi - lo + 1) // 4)


STEP = 2 * NB
UNITS = BH * NB
LAG_RSTORE, LAG_SKEW, LAG_S, LAG_E, LAG_PSTORE, LAG_UNSKEW, LAG_T, LAG_O = 1, 2, 3, 4, 5, 6, 7, 8
VC = DK + 2
PROB_SCALE_LN = 12 * math.log(2.0)
PEEL = 10


def rel_group_index(it, k):
    return it * (2 * GROUPS_BH) + (k // NB) * GROUPS_BH + GROUPS_BEFORE[k % NB]


def t_group_index(it, k):
    return it * (STEP * TGROUPS) + k * TGROUPS


def t_count(c, g):
    return TGROUPS - g if g == groups_of(c) - 1 else 1


def evac_plan(c):
    return ["act", "dve", "act", "dve", "act", "dve"][:groups_of(c)]


EV = {e: [sum(evac_plan(i).count(e) for i in range(c)) for c in range(NB)] for e in ("act", "dve")}
EV_BH = {e: sum(evac_plan(c).count(e) for c in range(NB)) for e in ("act", "dve")}


def evac_count(e, it, k, g):
    c = k % NB
    return it * (2 * EV_BH[e]) + (k // NB) * EV_BH[e] + EV[e][c] + evac_plan(c)[: g + 1].count(e)


def evac_of(it, k, g):
    if g < 0:
        k, g = k - 1, g + TGROUPS
    g = min(g, groups_of(k % NB) - 1)
    e = evac_plan(k % NB)[g]
    return e, evac_count(e, it, k, g)


def bank_items(k):
    scores = [("scores", k - LAG_S, bank) for bank in range(L // CH)] if k >= LAG_S else []
    return scores + [("rel", k, n) for n in range(rel_groups(k % NB))]


BANKS = 3
BANK_ITEMS = [item for k in range(PEEL + STEP + LAG_O) for item in bank_items(k)]
ITEM_INDEX = {item: i for i, item in enumerate(BANK_ITEMS)}
assert (STEP * TGROUPS) % (2 * BANKS) == 0
assert (ITEM_INDEX[("rel", PEEL + STEP, 0)] - ITEM_INDEX[("rel", PEEL, 0)]) % BANKS == 0


def group_blocks(c, g):
    if g < PGROUPS:
        return range(4 * g, 4 * g + 4)
    lo, hi = rel_blocks(c)
    n = 4 * (g - PGROUPS)
    return range(n, min(n + 4, hi - lo + 1))


def segments(c):
    lo, hi = window(c)
    edges = [(0, (c + lo) * P, -1), ((c + lo) * P, (c + hi + 1) * P, 0), ((c + hi + 1) * P, L, 1)]
    out = []
    for bank in range(L // CH):
        for a, z, kind in edges:
            a, z = max(a, bank * CH), min(z, (bank + 1) * CH)
            if a < z:
                out.append((bank, a, z, kind))
    return out


def project(nc, hbm, keep):
    with ExitStack() as ctx:
        def sb(name, shape, dt=FP32):
            return ctx.enter_context(nc.sbuf_tensor(name, shape, dt))

        def sem(name):
            return ctx.enter_context(nc.semaphore(name))

        FULL = ((0, 0), (0, 1), (1, 0), (1, 1))
        NFULL = len(FULL)
        wq = sb("wq", [P, KD, D])
        wk = sb("wk", [P, KD, D])
        wv = sb("wv", [P, KD, D])
        wr = sb("wr", [P, KD, NE])
        bq = sb("bq", [P, 2])
        bk = sb("bk", [P, 2])
        kbias = sb("kbias", [P, 2])
        bv = sb("bv", [P, D])
        rk = sb("rk", [DK, RELW])
        rk_rest = sb("rk_rest", [DK, RELW])
        rk_parts = sb("rk_parts", [DK, 3, RELW], BF16)
        xin = sb("xin", [P, 2, TPC, D])
        stats = sb("stats", [P, TPC, 6])
        moments = sb("moments", [P, 2, TPC, 2])
        eps = sb("eps", [P, 1])
        std = sb("std", [P, 2, TPC])
        rstd = sb("rstd", [P, 2, TPC])
        xn = sb("xn", [P, 2, TPC, D])
        xc = [sb(f"xc{i}", [P, KD, CH]) for i in range(2)]
        full = sb("full", [P, NFULL, CH])
        rest = sb("rest", [P, NFULL, CH])
        planes = sb("planes", [P, NFULL, 3, CH], BF16)
        psum = [ctx.enter_context(nc.psum_tensor(f"pa{i}", [P, CH], FP32)) for i in range(8)]
        xt_ps, qk_ps, v_ps, r_ps = psum[0:2], psum[2:4], psum[6:8], psum[4]

        s_x = [sem(f"a_x{i}") for i in range(2)]
        s_w = sem("a_weights")
        s_rk = sem("a_rel_k")
        s_rkp = sem("a_rel_k_parts")
        s_rkd = sem("a_rel_k_stacked")
        s_kb = sem("a_k_bias")
        s_st = sem("a_stats")
        s_mo = sem("a_moments")
        s_std = sem("a_std")
        s_rstd = sem("a_rstd")
        s_xn = sem("a_xn")
        s_xt = sem("a_xt")
        s_xc = sem("a_xc")
        s_xcw = [sem(f"a_xc_stored{i}") for i in range(2)]
        s_qk = sem("a_qk")
        s_f = sem("a_full")
        s_hi = sem("a_high")
        s_fr = sem("a_rest")
        s_mid = sem("a_middle")
        s_pl = sem("a_planes")
        s_plw = [sem(f"a_planes_stored{v}") for v in range(NFULL)]
        s_v = sem("a_v_router")
        s_ve = sem("a_v_router_read")
        s_id = sem("a_constants")
        s_pre = sem("a_memset")
        block = ctx.enter_context(nc.Block())
        weights = 10

        def chunks(eng, step):
            for par in range(2):
                step(0, par, True, False)
            with eng.Fori(1, NCH // 2 - 1) as gg:
                for par in range(2):
                    step(gg, par, False, False)
            for par in range(2):
                step(NCH // 2 - 1, par, False, True)

        @block.sync
        def _(sp):
            def load_x(gg, par):
                g = gg * 2 + par
                sp.dma_start(xin[:, par, :, :], hbm["x"][bass.ds(g * CH, CH), :].rearrange(
                    "(t p) d -> p t d", p=P)).then_inc(s_x[par], 16)

            load_x(0, 0)
            load_x(0, 1)
            for t, src in ((wq, hbm["wqT"]), (wk, hbm["wkT"]), (wv, hbm["wvT"]), (wr, hbm["router_wT"])):
                sp.dma_start(t[:, :, :], src.rearrange("(k p) n -> p k n", p=P)).then_inc(s_w, 16)
            for t, src in ((bq, hbm["bq"]), (bk, hbm["bk"])):
                sp.dma_start(t[:, :], src).then_inc(s_w, 16)
            sp.dma_start(bv[:, :], hbm["bv"].to_broadcast([P, D])).then_inc(s_w, 16)
            sp.dma_start(keep["rv"][:, :, :], hbm["rel_v"].rearrange("(n p) d -> p n d", p=P)).then_inc(s_w, 16)
            for i, end in enumerate(("rv_lo", "rv_hi")):
                sp.dma_start(keep[end][:, :], hbm["rel_v_ends"][i:i + 1, :].to_broadcast([P, DK])).then_inc(s_w, 16)
            sp.dma_start(rk[:, :], hbm["rel_kT"]).then_inc(s_rk, 16)

            def step(gg, par, first, last):
                g = gg * 2 + par
                if not last:
                    sp.wait_ge(s_xn, g + 1)
                    sp.nop(nofuse=True)
                    load_x(gg + 1, par)
                sp.wait_ge(s_xc, g + 1)
                sp.nop(nofuse=True)
                sp.dma_start(hbm["xT"][:, :, bass.ds(g * CH, CH)], xc[par][:, :, :]).then_inc(s_xcw[par], 16)
                for v, (kind, half) in enumerate(FULL):
                    sp.wait_ge(s_pl, g * NFULL + v + 1)
                    sp.nop(nofuse=True)
                    rows = hbm["planes"][kind, :, half * P:(half + 1) * P, bass.ds(g * CH, CH)]
                    sp.dma_start(rows.rearrange("r p n -> p r n"), planes[:, v, :, :]).then_inc(s_plw[v], 16)

            chunks(sp, step)
            sp.wait_ge(s_rkp, 4)
            sp.nop(nofuse=True)
            for s, plane in enumerate(K_PLANES):
                sp.dma_start(keep["rk_stack"][DK * s:DK * (s + 1), :], rk_parts[:, plane, :]).then_inc(s_rkd, 16)
            sp.wait_ge(s_rkd, 16 * len(K_PLANES))
            sp.nop(nofuse=True)
            for i in range(2):
                sp.wait_ge(s_xcw[i], 16 * NCH // 2)
                sp.nop(nofuse=True)
            for v in range(NFULL):
                sp.wait_ge(s_plw[v], 16 * NCH)
                sp.nop(nofuse=True)

        @block.gpsimd
        def _(pool):
            ident, upper = keep["ident"], keep["upper"]
            nc.gpsimd.memset(ident[:, :], 0.0).then_inc(s_pre, 1)
            nc.gpsimd.memset(upper[:, :], 1.0).then_inc(s_pre, 1)
            pool.wait_ge(s_pre, 2)
            nc.gpsimd.affine_select(out=ident[:, :], in_=ident[:, :], compare_op=ALU.not_equal,
                                    fill=1.0, base=0, pattern=[[-1, P]], channel_multiplier=1).then_inc(s_id, 1)
            nc.gpsimd.affine_select(out=upper[:, :], in_=upper[:, :], compare_op=ALU.is_ge,
                                    fill=0.0, base=0, pattern=[[1, P]], channel_multiplier=-1).then_inc(s_id, 1)
            with pool.Fori(0, NCH) as g:
                for v in range(NFULL):
                    pool.wait_ge(s_mid, g * NFULL + v + 1)
                    pool.nop(nofuse=True)
                    nc.gpsimd.tensor_tensor(planes[:, v, 2, :], rest[:, v, :], planes[:, v, 1, :],
                                            ALU.subtract).then_inc(s_pl, 1)

        @block.scalar
        def _(act):
            def deviations(gg, par):
                act.wait_ge(s_mo, (gg * 2 + par) * TPC + TPC)
                nc.scalar.activation(std[:, par, :], moments[:, par, :, 1], ACT.Sqrt,
                                     bias=eps[:, 0:1]).then_inc(s_std, 1)

            act.wait_ge(s_kb, 1)
            deviations(0, 0)
            act.wait_ge(s_kb, 2)

            def step(gg, par, first, last):
                g = gg * 2 + par
                if not (last and par):
                    deviations(*((gg, 1) if par == 0 else (gg + 1, 0)))

                def middle(v):
                    act.wait_ge(s_fr, g * NFULL + v + 1)
                    nc.scalar.copy(planes[:, v, 1, :], rest[:, v, :]).then_inc(s_mid, 1)

                for v, (kind, half) in enumerate(FULL):
                    act.wait_ge(s_qk, g * NFULL + v + 1)
                    if not (first and par == 0):
                        act.wait_ge(s_fr, (g - 1) * NFULL + v + 1)
                    bias, scale = (bq, 1.0) if kind == 0 else (kbias, DK ** -0.5)
                    nc.scalar.activation(full[:, v, :], qk_ps[half][:, :], ACT.Identity,
                                         bias=bias[:, half:half + 1], scale=scale).then_inc(s_f, 1)
                    if v >= 1:
                        middle(v - 1)
                middle(NFULL - 1)

            chunks(act, step)

        @block.vector
        def _(dve):
            nc.vector.memset(eps[:, :], EPS).then_inc(s_kb, 1)

            def normalise(gg, par):
                g = gg * 2 + par
                dve.wait_ge(s_x[par], gg * 16 + 16)
                for t in range(TPC):
                    nc.vector.bn_stats(stats[:, t, :], xin[:, par, t, :]).then_inc(s_st, 1)
                dve.wait_ge(s_st, g * TPC + TPC)
                dve.nop(nofuse=True)
                for t in range(TPC):
                    nc.vector.bn_aggr(moments[:, par, t, :], stats[:, t, :]).then_inc(s_mo, 1)
                dve.wait_ge(s_std, g + 1)
                nc.vector.reciprocal(rstd[:, par, :], std[:, par, :]).then_inc(s_rstd, 1)
                dve.wait_ge(s_rstd, g + 1)
                for t in range(TPC):
                    ins = nc.vector.tensor_scalar(xn[:, par, t, :], xin[:, par, t, :], moments[:, par, t, 0:1],
                                                  rstd[:, par, t:t + 1], ALU.subtract, ALU.mult)
                ins.then_inc(s_xn, 1)

            normalise(0, 0)
            dve.wait_ge(s_w, 16 * weights)
            nc.vector.tensor_scalar(kbias[:, :], bk[:, :], DK ** -0.5, None, ALU.mult).then_inc(s_kb, 1)

            def step(gg, par, first, last):
                g = gg * 2 + par
                if not first:
                    dve.wait_ge(s_xcw[par], gg * 16)
                dve.wait_ge(s_xt, g + 1)
                for k in range(KD):
                    ins = nc.vector.tensor_copy(xc[par][:, k, :], xt_ps[k][:, :])
                ins.then_inc(s_xc, 1)
                if not (last and par):
                    normalise(*((gg, 1) if par == 0 else (gg + 1, 0)))
                for v in range(NFULL):
                    i = g * NFULL + v
                    dve.wait_ge(s_f, i + 1)
                    if not (first and par == 0):
                        dve.wait_ge(s_plw[v], g * 16)
                    nc.vector.tensor_copy(planes[:, v, 0, :], full[:, v, :]).then_inc(s_hi, 1)
                    dve.wait_ge(s_hi, i + 1)
                    nc.vector.tensor_tensor(rest[:, v, :], full[:, v, :], planes[:, v, 0, :],
                                            ALU.subtract).then_inc(s_fr, 1)
                for t in range(TPC):
                    if t % 2 == 0:
                        dve.wait_ge(s_v, g * 3 + t // 2 + 1)
                    ins = nc.vector.tensor_tensor(
                        keep["v"][:, :, g * TPC + t, :],
                        v_ps[t // 2][:, (t % 2) * D:(t % 2 + 1) * D].rearrange("p (h d) -> p h d", h=H),
                        bv[:, :].rearrange("p (h d) -> p h d", h=H), ALU.add)
                    if t % 2:
                        ins.then_inc(s_ve, 1)
                dve.wait_ge(s_v, g * 3 + 3)
                nc.vector.tensor_copy(keep["logits"][:, bass.ds(g * TPC, TPC), :],
                                      r_ps[:, 0:TPC * NE].rearrange("p (t e) -> p t e", t=TPC)).then_inc(s_ve, 1)

            chunks(dve, step)
            dve.wait_ge(s_rk, 16)
            nc.vector.tensor_copy(rk_parts[:, 0, :], rk[:, :]).then_inc(s_rkp, 1)
            dve.wait_ge(s_rkp, 1)
            nc.vector.tensor_tensor(rk_rest[:, :], rk[:, :], rk_parts[:, 0, :], ALU.subtract).then_inc(s_rkp, 1)
            dve.wait_ge(s_rkp, 2)
            nc.vector.tensor_copy(rk_parts[:, 1, :], rk_rest[:, :]).then_inc(s_rkp, 1)
            dve.wait_ge(s_rkp, 3)
            nc.vector.tensor_tensor(rk_parts[:, 2, :], rk_rest[:, :], rk_parts[:, 1, :],
                                    ALU.subtract).then_inc(s_rkp, 1)

        @block.tensor
        def _(pe):
            pe.wait_ge(s_id, 2)
            pe.wait_ge(s_w, 16 * weights)

            def step(gg, par, first, last):
                g = gg * 2 + par
                start = first and par == 0
                pe.wait_ge(s_xn, g + 1)
                if not start:
                    pe.wait_ge(s_xc, g)
                for k in range(KD):
                    for t in range(TPC):
                        ins = nc.tensor.transpose(xt_ps[k][:, t * P:(t + 1) * P],
                                                  xn[:, par, t, k * P:(k + 1) * P], keep["ident"][:, :])
                ins.then_inc(s_xt, 1)
                pe.wait_ge(s_xc, g + 1)
                for v, (kind, half) in enumerate(FULL):
                    if not (start and v < 2):
                        pe.wait_ge(s_f, g * NFULL + v - 1)
                    for k in range(KD):
                        ins = nc.tensor.matmul(qk_ps[half][:, :], (wq, wk)[kind][:, k, half * P:(half + 1) * P],
                                               xc[par][:, k, :], start=(k == 0), stop=(k == KD - 1))
                    ins.then_inc(s_qk, 1)
                for t in range(TPC):
                    if t % 2 == 0 and not start:
                        pe.wait_ge(s_ve, (g - 1) * 3 + t // 2 + 1)
                    for k in range(KD):
                        ins = nc.tensor.matmul(v_ps[t // 2][:, (t % 2) * D:(t % 2 + 1) * D],
                                               xc[par][:, k, t * P:(t + 1) * P], wv[:, k, :],
                                               start=(k == 0), stop=(k == KD - 1))
                    if t % 2:
                        ins.then_inc(s_v, 1)
                if not start:
                    pe.wait_ge(s_ve, g * 3)
                for t in range(TPC):
                    for k in range(KD):
                        ins = nc.tensor.matmul(r_ps[:, t * NE:(t + 1) * NE], xc[par][:, k, t * P:(t + 1) * P],
                                               wr[:, k, :], start=(k == 0), stop=(k == KD - 1))
                ins.then_inc(s_v, 1)

            chunks(pe, step)


def attend(nc, hbm, keep):
    with ExitStack() as ctx:
        def sb(name, shape, dt=FP32):
            return ctx.enter_context(nc.sbuf_tensor(name, shape, dt))

        def sem(name):
            return ctx.enter_context(nc.semaphore(name))

        SLOTS_P, SLOTS_PT = 4, 2 * BANKS
        PROBW = RVW + P
        q_stack = [sb(f"q_stack{i}", [PARTS, L], BF16) for i in range(2)]
        k_stack = [sb(f"k_stack{i}", [PARTS, L], BF16) for i in range(2)]
        v_head = [sb(f"v_head{i}", [P, NB, 3, VC], BF16) for i in range(2)]
        v_rest = sb("v_rest", [P, NB, DK])
        rv_parts = sb("rv_parts", [P, RVW // P, 3, DK + 1], BF16)
        rv_rest = sb("rv_rest", [P, RVW // P, DK])
        rv_step = sb("rv_step", [P, DK])
        ident16 = sb("ident16", [P, P], FP16)
        rel = [sb(f"rel{i}", [P, RELW]) for i in range(2)]
        skewed = [sb(f"skewed{i}", [P, WIN]) for i in range(2)]
        scores = [sb(f"scores{i}", [P, L]) for i in range(SLOTS_P)]
        probs = [sb(f"probs{i}", [P, 2, L + 2 * P], FP16) for i in range(SLOTS_P)]
        unskewed = [sb(f"unskewed{i}", [P, 2, RVW], FP16) for i in range(2)]
        pt = [sb(f"pt{i}", [P, 2, CH], FP16) for i in range(SLOTS_PT)]
        no_values = sb("no_values", [P, 3 * VC], BF16)
        end_part = sb("end_part", [P, P])
        end_sum = sb("end_sum", [P, 8])
        left_sum = sb("left_sum", [P, 2])
        right_sum = sb("right_sum", [P, 2])
        part_max = sb("part_max", [P, 2, 8])
        neg_max = sb("neg_max", [P, 2])
        exp_bias = sb("exp_bias", [P, 2])
        row_sum = sb("row_sum", [P, 8])
        inv_sum = sb("inv_sum", [P, 2])
        o_sum = sb("o_sum", [P, 2, VC])
        o_lo = sb("o_lo", [P, 2, DK])
        o_hi = sb("o_hi", [P, 2, DK])
        psum = [ctx.enter_context(nc.psum_tensor(f"pb{i}", [P, CH], FP32)) for i in range(BANKS + 2)]
        score_ps, o_ps = psum[:BANKS], psum[BANKS:]
        t_ps = [ctx.enter_context(nc.psum_tensor(f"pt_ps{i}", [P, 2, CH], FP16)) for i in range(BANKS)]

        s_pad = sem("b_pads")
        s_stk = [sem(f"b_stacks{i}") for i in range(2)]
        s_vh = sem("b_v_head")
        s_g = sem("b_rel_product")
        s_ge = sem("b_rel_on_chip")
        s_gw = [sem(f"b_rel_stored{i}") for i in range(2)]
        s_gr = [sem(f"b_skewed{i}") for i in range(2)]
        s_s = sem("b_scores")
        s_add = sem("b_scores_added")
        s_nm = sem("b_neg_max")
        s_rm = sem("b_raw_max")
        s_exp = sem("b_exp")
        s_hi = sem("b_high")
        s_lo = sem("b_low")
        s_vp = sem("b_v_parts")
        s_rv = sem("b_rel_v_parts")
        s_pw = [sem(f"b_probs_stored{i}") for i in range(2)]
        s_pr = [sem(f"b_unskewed{i}") for i in range(2)]
        s_t = sem("b_transposed")
        s_ev = {"act": sem("b_t_evac_act"), "dve": sem("b_t_evac_dve")}
        s_pv = sem("b_pt_used")
        s_o1 = sem("b_out_scaled")
        s_o = sem("b_out_read")
        block = ctx.enter_context(nc.Block())
        pad_tensors = 2 * SLOTS_P + 1

        def skew_src(slot, width):
            return bass.AP(hbm["rel_scratch"].tensor, slot * P * RELW + P - 1, [[RELW - 1, P], [1, width]])

        def unskew_src(slot, width):
            return bass.AP(hbm["prob_scratch"].tensor, slot * P * 2 * PROBW,
                           [[2 * PROBW + 1, P], [PROBW, 2], [1, width]])

        def pipeline(eng, step):
            for k in range(PEEL):
                step(0, k)
            with eng.Fori(0, UNITS // STEP - 1) as it:
                for k in range(PEEL, PEEL + STEP):
                    step(it, k)
            for k in range(PEEL, STEP + LAG_O):
                step(UNITS // STEP - 1, k)

        def exists(it, k):
            return not isinstance(it, int) or 0 <= STEP * it + k < UNITS

        def uses(it, k, slots, inc=1):
            return it * (STEP // slots * inc) + (k // slots + 1) * inc

        def bank_of(kind, k, n):
            return score_ps[ITEM_INDEX[(kind, k, n)] % BANKS]

        def wait_bank(it, kind, k, n):
            i = ITEM_INDEX[(kind, k, n)] - BANKS
            while i >= 0 and not exists(it, BANK_ITEMS[i][1]):
                i -= BANKS
            if i >= 0:
                last, u, m = BANK_ITEMS[i]
                if last == "scores":
                    nc.tensor.wait_ge(s_add, it * (4 * STEP) + 4 * u + m + 1)
                else:
                    nc.tensor.wait_ge(s_ge, rel_group_index(it, u) + m + 1)

        def load_stacks(sp, it, head):
            b = head % 2
            for s in range(6):
                rows = bass.ds((it + head // 2) * DK, DK)
                sp.dma_start(q_stack[b][DK * s:DK * (s + 1), :],
                             hbm["planes"][0, Q_PLANES[s], rows, b * L:(b + 1) * L]).then_inc(s_stk[b], 16)
                sp.dma_start(k_stack[b][DK * s:DK * (s + 1), :],
                             hbm["planes"][1, K_PLANES[s], rows, b * L:(b + 1) * L]).then_inc(s_stk[b], 16)

        STK = 12 * 16

        @block.sync
        def _(sp):
            load_stacks(sp, 0, 0)

            def step(it, k):
                if k >= LAG_RSTORE and exists(it, k - LAG_RSTORE):
                    u = k - LAG_RSTORE
                    sp.wait_ge(s_ge, rel_group_index(it, u + 1))
                    sp.nop(nofuse=True)
                    if u >= 2:
                        sp.wait_ge(s_gr[u % 2], uses(it, u - 2, 2, 16))
                        sp.nop(nofuse=True)
                    w = (blocks(u % NB) + 1) * P
                    sp.dma_start(hbm["rel_scratch"][u % 2, :, 0:w], rel[u % 2][:, 0:w]).then_inc(s_gw[u % 2], 16)
                if k >= LAG_SKEW and exists(it, k - LAG_SKEW):
                    u = k - LAG_SKEW
                    sp.wait_ge(s_gw[u % 2], uses(it, u, 2, 16))
                    sp.nop(nofuse=True)
                    if u >= 2:
                        sp.wait_ge(s_add, it * (4 * STEP) + 4 * (u - 1))
                        sp.nop(nofuse=True)
                    w = blocks(u % NB) * P
                    sp.dma_start(skewed[u % 2][:, 0:w], skew_src(u % 2, w)).then_inc(s_gr[u % 2], 16)
                if k >= LAG_UNSKEW and exists(it, k - LAG_UNSKEW):
                    u = k - LAG_UNSKEW
                    sp.wait_ge(s_pw[u % 2], uses(it, u, 2, 16))
                    sp.nop(nofuse=True)
                    if u >= 2:
                        sp.wait_ge(s_t, t_group_index(it, u - 1))
                        sp.nop(nofuse=True)
                    lo, hi = rel_blocks(u % NB)
                    w = (hi - lo + 1) * P
                    sp.dma_start(unskewed[u % 2][:, :, 0:w], unskew_src(u % 2, w)).then_inc(s_pr[u % 2], 16)
                if k >= LAG_PSTORE and exists(it, k - LAG_PSTORE):
                    u = k - LAG_PSTORE
                    c = u % NB
                    sp.wait_ge(s_lo, it * STEP + u + 1)
                    sp.nop(nofuse=True)
                    if u >= 2:
                        sp.wait_ge(s_pr[u % 2], uses(it, u - 2, 2, 16))
                        sp.nop(nofuse=True)
                    lo, hi = rel_blocks(c)
                    col, w = (1 + c + lo) * P, (hi - lo + 2) * P
                    sp.dma_start(hbm["prob_scratch"][u % 2, :, :, 0:w],
                                 probs[u % SLOTS_P][:, :, col:col + w]).then_inc(s_pw[u % 2], 16)
                if k % NB == 6 and exists(it, k + NB):
                    head = k // NB + 1
                    if head >= 2:
                        sp.wait_ge(s_s, it * (4 * STEP) + 4 * NB * (head - 1))
                        sp.nop(nofuse=True)
                    load_stacks(sp, it, head)

            pipeline(sp, step)

        @block.gpsimd
        def _(pool):
            nc.gpsimd.memset(no_values[:, :], 0.0).then_inc(s_pad, 1)
            for i in range(SLOTS_P):
                nc.gpsimd.memset(probs[i][:, :, 0:P], 0.0).then_inc(s_pad, 1)
                nc.gpsimd.memset(probs[i][:, :, P + L:], 0.0).then_inc(s_pad, 1)
            nc.gpsimd.tensor_copy(ident16[:, :], keep["ident"][:, :]).then_inc(s_rv, 1)
            for i in range(2):
                nc.gpsimd.memset(v_head[i][:, :, 0, VC - 1:VC], 1.0)
                nc.gpsimd.memset(v_head[i][:, :, 1:3, VC - 1:VC], 0.0)
            nc.gpsimd.memset(rv_parts[:, :, 0, 0:1], 1.0)
            nc.gpsimd.memset(rv_parts[:, :, 1:3, 0:1], 0.0)
            nc.gpsimd.tensor_copy(rv_parts[:, :, 0, 1:], keep["rv"][:, :, :]).then_inc(s_rv, 1)
            pool.wait_ge(s_rv, 2)
            nc.gpsimd.tensor_tensor(rv_rest[:, :, :], keep["rv"][:, :, :], rv_parts[:, :, 0, 1:],
                                    ALU.subtract).then_inc(s_rv, 1)
            pool.wait_ge(s_rv, 3)
            nc.gpsimd.tensor_copy(rv_parts[:, :, 1, 1:], rv_rest[:, :, :]).then_inc(s_rv, 1)
            pool.wait_ge(s_rv, 4)
            nc.gpsimd.tensor_tensor(rv_parts[:, :, 2, 1:], rv_rest[:, :, :], rv_parts[:, :, 1, 1:],
                                    ALU.subtract).then_inc(s_rv, 1)

            def v_parts(it, head):
                v = keep["v"][:, it + head // 2, (head % 2) * NB:(head % 2 + 1) * NB, :]
                parts = v_head[head % 2]
                n = it * 6 + head * 3
                if head >= 1:
                    pool.wait_ge(s_pv, t_group_index(it, (head - 1) * NB) + 1)
                    pool.nop(nofuse=True)
                nc.gpsimd.tensor_copy(parts[:, :, 0, 1:1 + DK], v).then_inc(s_vp, 1)
                pool.wait_ge(s_vp, n + 1)
                pool.nop(nofuse=True)
                nc.gpsimd.tensor_tensor(v_rest[:, :, :], v, parts[:, :, 0, 1:1 + DK], ALU.subtract).then_inc(s_vp, 1)
                pool.wait_ge(s_vp, n + 2)
                pool.nop(nofuse=True)
                nc.gpsimd.tensor_copy(parts[:, :, 1, 1:1 + DK], v_rest[:, :, :]).then_inc(s_vp, 1)
                pool.wait_ge(s_vp, n + 3)
                nc.gpsimd.tensor_tensor(parts[:, :, 2, 1:1 + DK], v_rest[:, :, :], parts[:, :, 1, 1:1 + DK],
                                        ALU.subtract).then_inc(s_vh, 1)

            def step(it, k):
                if k % NB == 0 and exists(it, k):
                    v_parts(it, k // NB)
                u = k - LAG_E
                if u >= 0 and exists(it, u):
                    pool.wait_ge(s_hi, it * STEP + u + 1)
                    nc.gpsimd.tensor_tensor(probs[u % SLOTS_P][:, 1, P:P + L], scores[u % SLOTS_P][:, :],
                                            probs[u % SLOTS_P][:, 0, P:P + L], ALU.subtract).then_inc(s_lo, 1)

            pipeline(pool, step)

        @block.tensor
        def _(pe):
            pe.sem_inc(s_pv, 1)
            pe.wait_ge(s_pad, pad_tensors)
            pe.wait_ge(s_rv, 5)

            def rel_group(it, k, n):
                c = k % NB
                if n == 0 and c == 0:
                    pe.wait_ge(s_stk[(k // NB) % 2], it * STK + (k // NB // 2 + 1) * STK)
                wait_bank(it, "rel", k, n)
                j0 = (window(c)[0] - M_LO) * P + n * CH
                w = min(CH, (blocks(c) + 1) * P - n * CH)
                nc.tensor.matmul(bank_of("rel", k, n)[:, 0:w], q_stack[(k // NB) % 2][:, c * P:(c + 1) * P],
                                 keep["rk_stack"][:, j0:j0 + w], start=True, stop=True).then_inc(s_g, 1)

            def score_bank(it, k, bank):
                c, head = k % NB, k // NB
                wait_bank(it, "scores", k, bank)
                ps = bank_of("scores", k, bank)
                nc.tensor.matmul(ps[:, :], q_stack[head % 2][:, c * P:(c + 1) * P],
                                 k_stack[head % 2][:, bank * CH:(bank + 1) * CH], start=True, stop=True).then_inc(s_s, 1)

            def transposes(it, k, g):
                c = k % NB
                idx = k * TGROUPS + g
                if idx >= BANKS:
                    e, n = evac_of(it, k, g - BANKS)
                    pe.wait_ge(s_ev[e], n)
                if g == 0:
                    pe.wait_ge(s_lo, it * STEP + k + 1)
                if g == PGROUPS:
                    pe.wait_ge(s_pr[k % 2], uses(it, k, 2, 16))
                for part in range(2):
                    for i, blk in enumerate(group_blocks(c, g)):
                        src = probs[k % SLOTS_P][:, part, (1 + blk) * P:(2 + blk) * P] if g < PGROUPS else \
                            unskewed[k % 2][:, part, blk * P:(blk + 1) * P]
                        ins = nc.tensor.transpose(t_ps[idx % BANKS][:, part, i * P:(i + 1) * P], src, ident16[:, :])
                ins.then_inc(s_t, t_count(c, g))

            def values(it, k, g):
                c, head = k % NB, k // NB
                idx = k * TGROUPS + g
                out = o_ps[k % 2][:, 0:3 * VC].rearrange("p (r n) -> p r n", r=3)
                src = pt[idx % SLOTS_PT]
                if g == 0:
                    if c == 0:
                        pe.wait_ge(s_vh, it * 2 + head + 1)
                    if k >= 2:
                        pe.wait_ge(s_o, it * STEP + k - 1)
                e, n = evac_of(it, k, g)
                pe.wait_ge(s_ev[e], n)
                if g == 0:
                    nc.tensor.matmul(o_ps[k % 2][:, 0:3 * VC], src[:, 0, 0:P], no_values[:, :], start=True, stop=False)
                last_group = g == groups_of(c) - 1
                blks = group_blocks(c, g)
                for i, blk in enumerate(blks):
                    if g < PGROUPS:
                        a, z = 1, DK + 1 + (blk > c + R_HI + 1)
                        rhs = v_head[head % 2][:, blk, :, a:z]
                    else:
                        a, z = 0, DK + 1
                        rhs = rv_parts[:, blk + rel_blocks(c)[0] - R_LO, :, :]
                    for part in range(2):
                        ins = nc.tensor.matmul(out[:, :, a:z], src[:, part, i * P:(i + 1) * P], rhs, start=False,
                                               stop=last_group and i == len(blks) - 1 and part == 1)
                ins.then_inc(s_pv, t_count(c, g))

            def step(it, k):
                work = []
                if k >= LAG_S and exists(it, k - LAG_S):
                    work += [(score_bank, k - LAG_S, bank) for bank in range(4)]
                if exists(it, k):
                    work += [(rel_group, k, n) for n in range(rel_groups(k % NB))]
                u = k - LAG_T
                groups = groups_of(u % NB) if u >= 0 and exists(it, u) else 0
                pending = []
                if u >= 1 and exists(it, u - 1):
                    last = groups_of((u - 1) % NB) - 1
                    pending = [(u - 1, last - 1), (u - 1, last)]
                for g in range(groups):
                    transposes(it, u, g)
                    if work:
                        f, a, n = work.pop(0)
                        f(it, a, n)
                    pending.append((u, g))
                    if len(pending) > 2:
                        values(it, *pending.pop(0))
                for f, a, n in work:
                    f(it, a, n)
                if not groups:
                    for unit, g in pending:
                        values(it, unit, g)

            pipeline(pe, step)

        def evacuate(eng_name, eng, it, k, g):
            c = k % NB
            idx = k * TGROUPS + g
            eng.wait_ge(s_t, t_group_index(it, k) + g + 1)
            if idx >= SLOTS_PT:
                eng.wait_ge(s_pv, t_group_index(it, k) + g + 2 - SLOTS_PT)
            blks = group_blocks(c, g)
            dst, src = pt[idx % SLOTS_PT], t_ps[idx % BANKS]
            z = len(blks) * P
            copy = nc.scalar.copy if eng_name == "act" else nc.vector.tensor_copy
            copy(dst[:, :, 0:z], src[:, :, 0:z]).then_inc(s_ev[eng_name], 1)

        @block.scalar
        def _(act):
            act.wait_ge(s_pad, pad_tensors)

            def rel_evac(it, k, n):
                act.wait_ge(s_g, rel_group_index(it, k) + n + 1)
                if n == 0 and k >= 2:
                    act.wait_ge(s_gw[k % 2], uses(it, k - 2, 2, 16))
                w = min(CH, (blocks(k % NB) + 1) * P - n * CH)
                nc.scalar.copy(rel[k % 2][:, n * CH:n * CH + w], bank_of("rel", k, n)[:, 0:w]).then_inc(s_ge, 1)

            def exponentials(it, k):
                act.wait_ge(s_nm, it * STEP + k + 1)
                nc.scalar.activation(scores[k % SLOTS_P][:, :], scores[k % SLOTS_P][:, :], ACT.Exp,
                                     bias=exp_bias[:, k % 2:k % 2 + 1],
                                     accum_out=row_sum[:, k % 8:k % 8 + 1]).then_inc(s_exp, 1)

            def step(it, k):
                work = [None] * 4 if k >= LAG_S and exists(it, k - LAG_S) else []
                if exists(it, k):
                    work += list(range(rel_groups(k % NB)))
                u = k - LAG_T
                plan = evac_plan(u % NB) if u >= 0 and exists(it, u) else []
                for g, e in enumerate(plan):
                    if e == "act":
                        evacuate("act", act, it, u, g)
                    if work:
                        n = work.pop(0)
                        if n is not None:
                            rel_evac(it, k, n)
                    if g == 0 and exists(it, k - LAG_E):
                        exponentials(it, k - LAG_E)
                for n in work:
                    if n is not None:
                        rel_evac(it, k, n)
                if not plan and k >= LAG_E and exists(it, k - LAG_E):
                    exponentials(it, k - LAG_E)

            pipeline(act, step)

        @block.vector
        def _(dve):
            dve.wait_ge(s_pad, pad_tensors)
            nc.vector.tensor_tensor(rv_step[:, :], keep["rv_hi"][:, :], keep["rv_lo"][:, :], ALU.subtract)

            def add_bank(it, k, bank):
                c = k % NB
                lo = window(c)[0]
                dve.wait_ge(s_s, it * (4 * STEP) + 4 * k + bank + 1)
                if bank == 0:
                    dve.wait_ge(s_gr[k % 2], uses(it, k, 2, 16))
                    if k >= SLOTS_P:
                        dve.wait_ge(s_lo, it * STEP + k - SLOTS_P + 1)
                    if k >= 2:
                        dve.wait_ge(s_exp, it * STEP + k - 1)
                dve.nop(nofuse=True)
                ps = bank_of("scores", k, bank)
                for n, (bk_, a, z, kind) in enumerate(segments(c)):
                    if bk_ != bank:
                        continue
                    col = {-1: 0, 0: a - (c + lo) * P, 1: blocks(c) * P - 1}[kind]
                    other = skewed[k % 2][:, col:col + (z - a if kind == 0 else 1)]
                    if kind:
                        other = other.to_broadcast([P, z - a])
                    ins = nc.vector.tensor_tensor_reduce(
                        out=scores[k % SLOTS_P][:, a:z], in0=ps[:, a - bank * CH:z - bank * CH],
                        in1=other, scale=1.0, scalar=-3.0e38, op0=ALU.add, op1=ALU.max,
                        accum_out=part_max[:, k % 2, n:n + 1])
                ins.then_inc(s_add, 1)

            def raw_maximum(it, k):
                dve.wait_ge(s_add, it * (4 * STEP) + 4 * k + 4)
                nc.vector.tensor_reduce(neg_max[:, k % 2:k % 2 + 1], part_max[:, k % 2, 0:len(segments(k % NB))],
                                        axis=AX.X, op=ALU.max, negate=True).then_inc(s_rm, 1)

            def maximum(it, k):
                dve.wait_ge(s_rm, it * STEP + k + 1)
                nc.vector.tensor_scalar(exp_bias[:, k % 2:k % 2 + 1], neg_max[:, k % 2:k % 2 + 1], PROB_SCALE_LN,
                                        None, ALU.add).then_inc(s_nm, 1)

            def high_part(it, k):
                c = k % NB
                dve.wait_ge(s_exp, it * STEP + k + 1)
                if right_end(c):
                    a = (c + R_HI + 1) * P
                    nc.vector.tensor_tensor_reduce(
                        out=end_part[:, :], in0=scores[k % SLOTS_P][:, a:a + P], in1=keep["upper"][:, :], scale=1.0,
                        scalar=0.0, op0=ALU.mult, op1=ALU.add, accum_out=end_sum[:, k % 8:k % 8 + 1])
                if k >= SLOTS_P:
                    dve.wait_ge(s_pw[k % 2], uses(it, k - SLOTS_P, 2, 16))
                    dve.wait_ge(s_t, t_group_index(it, k - SLOTS_P + 1))
                nc.vector.tensor_copy(probs[k % SLOTS_P][:, 0, P:P + L], scores[k % SLOTS_P][:, :]).then_inc(s_hi, 1)

            def output(it, k, link):
                c, head = k % NB, k // NB
                slot = k % 2
                total = o_sum[:, slot, :]
                n = it * (6 * STEP) + 6 * k
                left, right = left_end(c), right_end(c)
                if link == 0:
                    dve.wait_ge(s_pv, t_group_index(it, k + 1) + 1)
                    nc.vector.reciprocal(inv_sum[:, slot:slot + 1], row_sum[:, k % 8:k % 8 + 1]).then_inc(s_o1, 1)
                    o = o_ps[slot][:, 0:3 * VC].rearrange("p (r n) -> p n r", r=3)
                    nc.vector.tensor_reduce(total, o, axis=AX.X, op=ALU.add).then_inc(s_o1, 1)
                if link == 1:
                    dve.wait_ge(s_o1, n + 2)
                    if left:
                        nc.vector.tensor_tensor(left_sum[:, slot:slot + 1], row_sum[:, k % 8:k % 8 + 1], total[:, 0:1],
                                                ALU.subtract).then_inc(s_o1, 1 if right else 2)
                    if right:
                        nc.vector.tensor_tensor(right_sum[:, slot:slot + 1], end_sum[:, k % 8:k % 8 + 1],
                                                total[:, 1 + DK:2 + DK], ALU.add).then_inc(s_o1, 1 if left else 2)
                if link == 2:
                    dve.wait_ge(s_o1, n + 4)
                    if left:
                        nc.vector.scalar_tensor_tensor(out=o_lo[:, slot, :], in0=keep["rv_lo"][:, :],
                                                       scalar=left_sum[:, slot:slot + 1], in1=total[:, 1:1 + DK],
                                                       op0=ALU.mult, op1=ALU.add).then_inc(s_o1, 1 if right else 2)
                    else:
                        nc.vector.tensor_copy(o_lo[:, slot, :], total[:, 1:1 + DK]).then_inc(s_o1, 1)
                if link == 3 and right:
                    dve.wait_ge(s_o1, n + 5)
                    values = rv_step if left else keep["rv_hi"]
                    nc.vector.scalar_tensor_tensor(out=o_hi[:, slot, :], in0=values[:, :],
                                                   scalar=right_sum[:, slot:slot + 1], in1=o_lo[:, slot, :],
                                                   op0=ALU.mult, op1=ALU.add).then_inc(s_o1, 1)
                if link == 4:
                    dve.wait_ge(s_o1, n + 6)
                    res = o_hi if right else o_lo
                    nc.vector.tensor_scalar(keep["v"][:, it + head // 2, (head % 2) * NB + c, :], res[:, slot, :],
                                            inv_sum[:, slot:slot + 1], None, ALU.mult).then_inc(s_o, 1)

            def step(it, k):
                a, h, t, o = k - LAG_S, k - LAG_E, k - LAG_T, k - LAG_O
                adding = a >= 0 and exists(it, a)
                plan = evac_plan(t % NB) if t >= 0 and exists(it, t) else []
                ends = o >= 0
                for g in range(max(len(plan), 5)):
                    if g == 4 and adding:
                        raw_maximum(it, a)
                    if g < 4 and adding:
                        add_bank(it, a, g)
                    if g < len(plan) and plan[g] == "dve":
                        evacuate("dve", dve, it, t, g)
                    if 2 <= g <= 4 and ends:
                        output(it, o, g - 2)
                    if g == 3 and h >= 0 and exists(it, h):
                        high_part(it, h)
                if ends:
                    output(it, o, 3)
                if adding:
                    maximum(it, a)
                if ends:
                    output(it, o, 4)

            pipeline(dve, step)


def mix(nc, hbm, keep):
    with ExitStack() as ctx:
        def sb(name, shape, dt=FP32):
            return ctx.enter_context(nc.sbuf_tensor(name, shape, dt))

        def sem(name):
            return ctx.enter_context(nc.semaphore(name))

        NT = TOK // P
        logits = keep["logits"]
        wo = sb("wo", [P, KD, D])
        bias9 = sb("bias9", [NE + 1, D])
        x_res = sb("x_res", [P, 2, D])
        attn_tile = [sb(f"attn_tile{i}", [P, H, DK]) for i in range(2)]
        gates_tile = [sb(f"gates_tile{i}", [P, NE + 1]) for i in range(2)]
        attn_t = [sb(f"attn_t{i}", [P, KD, P]) for i in range(2)]
        gates_t = [sb(f"gates_t{i}", [NE + 1, P]) for i in range(2)]
        xT = sb("xT_sb", [P, KD, TOK])
        y = sb("y_sb", [P, NT, D])
        gw = [sb(f"gate_w{i}", [P, KD, F]) for i in range(2)]
        uw = [sb(f"up_w{i}", [P, KD, F]) for i in range(2)]
        dw = [sb(f"down_w{i}", [P, FT, D]) for i in range(2)]
        gb = [sb(f"gate_b{i}", [P, FT]) for i in range(2)]
        ub = [sb(f"up_b{i}", [P, FT]) for i in range(2)]
        ge = [sb(f"gates_e{i}", [P, NT]) for i in range(2)]
        act_g = [sb(f"silu{i}", [P, CH]) for i in range(2)]
        hid = [sb(f"hidden{i}", [P, FT, CH]) for i in range(2)]
        peak = sb("peak", [P, NT, 1])
        prob = sb("prob", [P, NT, NE])
        total = sb("total", [P, NT, 1])
        rest = sb("prob_rest", [P, NT, NE])
        same = sb("same", [P, NT, NE])
        index = sb("index", [P, NT, NE])
        index_i = sb("index_i", [P, NT, NE], mybir.dt.int32)
        pick = sb("pick", [P, NT, NE])
        first = sb("first", [P, NT, 1])
        chosen = sb("chosen", [P, 2, NT, NE])
        gates = sb("gates", [P, NT, NE + 1])
        psum = [ctx.enter_context(nc.psum_tensor(f"pc{i}", [P, CH], FP32)) for i in range(8)]

        s_w = sem("c_weights")
        s_x = [sem(f"c_x{i}") for i in range(2)]
        s_xt = sem("c_xT")
        s_ix = sem("c_index")
        s_r = sem("c_router")
        s_re = sem("c_router_exp")
        s_in = sem("c_tile_in")
        s_t = sem("c_tile_transposed")
        s_te = sem("c_tile_on_chip")
        s_p = sem("c_projected")
        s_y = sem("c_y_started")
        s_ew = [sem(f"c_expert{i}") for i in range(2)]
        s_ge = sem("c_gates_e")
        s_gu = sem("c_gate_up")
        s_si = sem("c_silu")
        s_h = sem("c_hidden")
        s_d = sem("c_down")
        s_ye = sem("c_y_added")
        s_out = sem("c_out")
        block = ctx.enter_context(nc.Block())

        def load_expert(sp, e, i):
            sp.dma_start(gw[i][:, :, :], hbm["gate_w"][e, :, :].rearrange("(k p) f -> p k f", p=P)).then_inc(s_ew[i], 16)
            sp.dma_start(uw[i][:, :, :], hbm["up_w"][e, :, :].rearrange("(k p) f -> p k f", p=P)).then_inc(s_ew[i], 16)
            sp.dma_start(dw[i][:, :, :], hbm["down_w"][e, :, :].rearrange("(k p) d -> p k d", p=P)).then_inc(s_ew[i], 16)
            sp.dma_start(gb[i][:, :], hbm["gate_b"][e, :, :]).then_inc(s_ew[i], 16)
            sp.dma_start(ub[i][:, :], hbm["up_b"][e, :, :]).then_inc(s_ew[i], 16)

        EW = 5 * 16

        @block.sync
        def _(sp):
            sp.dma_start(wo[:, :, :], hbm["woT"].rearrange("(k p) n -> p k n", p=P)).then_inc(s_w, 16)
            sp.dma_start(bias9[0:NE, :], hbm["down_b"]).then_inc(s_w, 16)
            sp.dma_start(bias9[NE:NE + 1, :], hbm["bo"]).then_inc(s_w, 16)
            sp.dma_start(xT[:, :, :], hbm["xT"]).then_inc(s_xt, 16)
            for i in range(2):
                load_expert(sp, i, i)
            with sp.Fori(0, NT // 2) as tt:
                for par in range(2):
                    sp.wait_ge(s_y, tt * 2 + par + 1)
                    sp.nop(nofuse=True)
                    sp.dma_start(x_res[:, par, :], hbm["x"][bass.ds(tt * (2 * P) + par * P, P), :]).then_inc(s_x[par], 16)
            with sp.Fori(0, NE // 2 - 1) as ee:
                for i in range(2):
                    sp.wait_ge(s_ye, ee * (2 * NT) + (i + 1) * NT + 1)
                    sp.nop(nofuse=True)
                    sp.wait_ge(s_h, ee * (2 * NCH * FT) + (i + 1) * NCH * FT)
                    sp.nop(nofuse=True)
                    load_expert(sp, ee * 2 + i + 2, i)
            for c in range(NCH):
                sp.wait_ge(s_ye, (NE - 1) * NT + (c + 1) * TPC + 1)
                sp.nop(nofuse=True)
                sp.dma_start(hbm["out"][c * CH:(c + 1) * CH, :].rearrange("(t p) d -> p t d", p=P),
                             y[:, c * TPC:(c + 1) * TPC, :]).then_inc(s_out, 16)
            sp.wait_ge(s_out, 16 * NCH)
            sp.nop(nofuse=True)

        @block.gpsimd
        def _(pool):
            nc.gpsimd.iota(index_i[:, :, :], pattern=[[0, NT], [1, NE]], base=-NE, channel_multiplier=0).then_inc(s_ix, 1)
            pool.wait_ge(s_ix, 1)
            nc.gpsimd.tensor_copy(index[:, :, :], index_i[:, :, :]).then_inc(s_ix, 1)

        @block.scalar
        def _(act):
            act.wait_ge(s_r, 2)
            nc.scalar.activation(prob[:, :, :], rest[:, :, :], ACT.Exp).then_inc(s_re, 1)
            act.wait_ge(s_r, ROUTER_LINKS)
            with act.Fori(0, B) as b:
                with act.Fori(0, NB // 2) as cc:
                    for par in range(2):
                        n = b * NB + cc * 2 + par
                        act.wait_ge(s_te, n + 1)
                        nc.scalar.copy(attn_tile[par][:, :, :], keep["v"][:, :, n, :])
                        nc.scalar.copy(gates_tile[par][:, :], gates[:, n, :]).then_inc(s_in, 1)
            with act.Fori(0, NE // 2) as ee:
                for i in range(2):
                    act.wait_ge(s_ew[i], ee * EW + EW)
                    act.wait_ge(s_ye, (ee * 2 + i) * NT + 1)
                    nc.scalar.copy(ge[i][:, :], gates[:, :, ee * 2 + i]).then_inc(s_ge, 1)
                    for c in range(NCH):
                        for f in range(FT):
                            n = ee * (2 * NCH * FT) + (i * NCH + c) * FT + f
                            act.wait_ge(s_gu, n * 2 + 1)
                            act.wait_ge(s_h, n + 1)
                            nc.scalar.activation(act_g[f % 2][:, :], psum[f % 2][:, :], ACT.Silu,
                                                 bias=gb[i][:, f:f + 1]).then_inc(s_si, 1)

        @block.vector
        def _(dve):
            dve.sem_inc(s_y, 2)
            dve.sem_inc(s_te, 2)
            dve.sem_inc(s_h, 2)
            dve.sem_inc(s_ye, 1)
            links = [0]

            def link(ins):
                links[0] += 1
                ins.then_inc(s_r, 1)
                dve.wait_ge(s_r, links[0])

            wide = [P, NT, NE]
            link(nc.vector.tensor_reduce(peak[:, :, :], logits[:, :, :], axis=AX.X, op=ALU.max))
            link(nc.vector.tensor_tensor(rest[:, :, :], logits[:, :, :], peak[:, :, :].to_broadcast(wide), ALU.subtract))
            dve.wait_ge(s_re, 1)
            link(nc.vector.tensor_reduce(total[:, :, :], prob[:, :, :], axis=AX.X, op=ALU.add))
            link(nc.vector.reciprocal(total[:, :, :], total[:, :, :]))
            link(nc.vector.tensor_tensor(prob[:, :, :], prob[:, :, :], total[:, :, :].to_broadcast(wide), ALU.mult))
            link(nc.vector.tensor_copy(rest[:, :, :], prob[:, :, :]))
            dve.wait_ge(s_ix, 2)
            for r in range(2):
                link(nc.vector.tensor_reduce(peak[:, :, :], rest[:, :, :], axis=AX.X, op=ALU.max))
                link(nc.vector.tensor_tensor(same[:, :, :], rest[:, :, :], peak[:, :, :].to_broadcast(wide), ALU.is_equal))
                link(nc.vector.tensor_tensor(pick[:, :, :], same[:, :, :], index[:, :, :], ALU.mult))
                link(nc.vector.tensor_reduce(first[:, :, :], pick[:, :, :], axis=AX.X, op=ALU.min))
                link(nc.vector.tensor_tensor(chosen[:, r, :, :], index[:, :, :], first[:, :, :].to_broadcast(wide),
                                             ALU.is_equal))
                if r == 0:
                    link(nc.vector.scalar_tensor_tensor(out=rest[:, :, :], in0=chosen[:, 0, :, :], scalar=-2.0,
                                                        in1=rest[:, :, :], op0=ALU.mult, op1=ALU.add))
            link(nc.vector.tensor_tensor(same[:, :, :], chosen[:, 0, :, :], chosen[:, 1, :, :], ALU.add))
            link(nc.vector.tensor_tensor(prob[:, :, :], prob[:, :, :], same[:, :, :], ALU.mult))
            link(nc.vector.tensor_reduce(total[:, :, :], prob[:, :, :], axis=AX.X, op=ALU.add))
            link(nc.vector.tensor_scalar(total[:, :, :], total[:, :, :], 1e-9, None, ALU.add))
            link(nc.vector.reciprocal(total[:, :, :], total[:, :, :]))
            link(nc.vector.tensor_tensor(gates[:, :, 0:NE], prob[:, :, :], total[:, :, :].to_broadcast(wide), ALU.mult))
            link(nc.vector.memset(gates[:, :, NE:NE + 1], 1.0))
            assert links[0] == ROUTER_LINKS, links
            with dve.Fori(0, NT // 2) as tt:
                for par in range(2):
                    n = tt * 2 + par
                    dve.wait_ge(s_t, n + 1)
                    nc.vector.tensor_copy(attn_t[par][:, :, :], psum[par][:, 0:KD * P].rearrange("p (k l) -> p k l", k=KD))
                    nc.vector.tensor_copy(gates_t[par][:, :], psum[par][0:NE + 1, KD * P:(KD + 1) * P]).then_inc(s_te, 1)
                    dve.wait_ge(s_p, n + 1)
                    dve.wait_ge(s_x[par], tt * 16 + 16)
                    nc.vector.tensor_tensor(y[:, n, :], psum[2 + par][:, 0:D], x_res[:, par, :], ALU.add).then_inc(s_y, 1)
            dve.wait_ge(s_y, NT + 2)
            with dve.Fori(0, NE // 2) as ee:
                for i in range(2):
                    dve.wait_ge(s_ew[i], ee * EW + EW)
                    dve.wait_ge(s_ge, ee * 2 + i + 1)
                    for c in range(NCH):
                        for f in range(FT):
                            n = ee * (2 * NCH * FT) + (i * NCH + c) * FT + f
                            dve.wait_ge(s_gu, n * 2 + 2)
                            dve.wait_ge(s_si, n + 1)
                            nc.vector.scalar_tensor_tensor(out=hid[c % 2][:, f, :], in0=psum[2 + f % 2][:, :],
                                                           scalar=ub[i][:, f:f + 1], in1=act_g[f % 2][:, :],
                                                           op0=ALU.add, op1=ALU.mult).then_inc(s_h, 1)
                        for t in range(TPC):
                            tile = c * TPC + t
                            m = ee * (2 * NT) + i * NT + tile
                            dve.wait_ge(s_d, m + 1)
                            nc.vector.scalar_tensor_tensor(out=y[:, tile, :], in0=psum[4 + t][:, 0:D],
                                                           scalar=ge[i][:, tile:tile + 1], in1=y[:, tile, :],
                                                           op0=ALU.mult, op1=ALU.add).then_inc(s_ye, 1)

        @block.tensor
        def _(pe):
            pe.wait_ge(s_w, 48)
            with pe.Fori(0, NT // 2) as tt:
                for par in range(2):
                    n = tt * 2 + par
                    pe.wait_ge(s_in, n + 1)
                    pe.wait_ge(s_te, n + 1)
                    flat = attn_tile[par][:, :, :].rearrange("p h d -> p (h d)")
                    for k in range(KD):
                        nc.tensor.transpose(psum[par][:, k * P:(k + 1) * P], flat[:, k * P:(k + 1) * P], keep["ident"][:, :])
                    nc.tensor.transpose(psum[par][0:NE + 1, KD * P:(KD + 1) * P], gates_tile[par][:, :],
                                        keep["ident"][:, :]).then_inc(s_t, 1)
                    pe.wait_ge(s_te, n + 3)
                    pe.wait_ge(s_y, n + 1)
                    for k in range(KD):
                        nc.tensor.matmul(psum[2 + par][:, 0:D], attn_t[par][:, k, :], wo[:, k, :], start=(k == 0), stop=False)
                    nc.tensor.matmul(psum[2 + par][:, 0:D], gates_t[par][:, :], bias9[:, :], start=False,
                                     stop=True).then_inc(s_p, 1)
            pe.wait_ge(s_xt, 16)
            pe.wait_ge(s_y, NT + 2)
            with pe.Fori(0, NE // 2) as ee:
                for i in range(2):
                    pe.wait_ge(s_ew[i], ee * EW + EW)
                    for c in range(NCH):
                        for f in range(FT):
                            n = ee * (2 * NCH * FT) + (i * NCH + c) * FT + f
                            pe.wait_ge(s_h, n + 1)
                            for w, bank in ((gw, f % 2), (uw, 2 + f % 2)):
                                for k in range(KD):
                                    ins = nc.tensor.matmul(psum[bank][:, :], w[i][:, k, f * P:(f + 1) * P],
                                                           xT[:, k, c * CH:(c + 1) * CH], start=(k == 0), stop=(k == KD - 1))
                                ins.then_inc(s_gu, 1)
                        for f in range(FT):
                            pe.wait_ge(s_h, ee * (2 * NCH * FT) + (i * NCH + c) * FT + f + 3)
                            for t in range(TPC):
                                if f == 0 and not (i == 0 and c == 0):
                                    pe.wait_ge(s_ye, ee * (2 * NT) + i * NT + (c - 1) * TPC + t + 2)
                                if f == 0 and i == 0 and c == 0 and t == 0:
                                    pe.wait_ge(s_ye, ee * (2 * NT) + 1)
                                ins = nc.tensor.matmul(psum[4 + t][:, 0:D], hid[c % 2][:, f, t * P:(t + 1) * P],
                                                       dw[i][:, f, :], start=(f == 0), stop=(f == FT - 1))
                                if f == FT - 1:
                                    ins.then_inc(s_d, 1)


ROUTER_LINKS = 2 + 4 + 11 + 7


def program(nc, hbm):
    with ExitStack() as ctx:
        def sb(name, shape, dt=FP32):
            return ctx.enter_context(nc.sbuf_tensor(name, shape, dt))

        keep = {
            "ident": sb("ident", [P, P]),
            "logits": sb("logits", [P, TOK // P, NE]),
            "v": sb("v_all", [P, H, B * NB, DK]),
        }
        hbm["xT"] = nc.dram_tensor("xT_scratch", (P, KD, TOK), FP32, kind="Internal").ap()
        hbm["planes"] = nc.dram_tensor("planes_scratch", (2, 3, D, TOK), BF16, kind="Internal").ap()
        hbm["rel_scratch"] = nc.dram_tensor("rel_scratch", (2, P, RELW), FP32, kind="Internal").ap()
        hbm["prob_scratch"] = nc.dram_tensor("prob_scratch", (2, P, 2, RVW + P), FP16, kind="Internal").ap()
        with ExitStack() as inner:
            def sbi(name, shape, dt=FP32):
                return inner.enter_context(nc.sbuf_tensor(name, shape, dt))

            keep["rk_stack"] = sbi("rk_stack", [PARTS, RELW], BF16)
            keep["rv"] = sbi("rv", [P, RVW // P, DK])
            keep["rv_lo"] = sbi("rv_lo", [P, DK])
            keep["rv_hi"] = sbi("rv_hi", [P, DK])
            keep["upper"] = sbi("upper", [P, P])
            project(nc, hbm, keep)
            attend(nc, hbm, keep)
        mix(nc, hbm, keep)


def kernel(**inputs):
    import numpy as np
    import concourse.bacc as bacc
    from concourse.bass_utils import run_bass_kernel_spmd

    def a(name):
        return np.asarray(inputs[name])

    def rows(first, count):
        row = np.arange(count) + first + MAXLEN - 1
        return np.clip(np.where(row < 0, row + 2 * MAXLEN - 1, row), 0, 2 * MAXLEN - 2)

    rel_k, rel_v = a("L0_attn_relative_k")[rows(REL0, RELW)], a("L0_attn_relative_v")
    arrays = {
        "x": a("L0_attn_x").reshape(TOK, D),
        "wqT": a("L0_attn_Wq").T, "wkT": a("L0_attn_Wk").T, "wvT": a("L0_attn_Wv").T, "woT": a("L0_attn_Wo").T,
        "bq": a("L0_attn_bq").reshape(2, P).T, "bk": a("L0_attn_bk").reshape(2, P).T,
        "bv": a("L0_attn_bv").reshape(1, D), "bo": a("L0_attn_bo").reshape(1, D),
        "rel_kT": rel_k.T, "rel_v": rel_v[rows(R_LO * P, RVW)],
        "rel_v_ends": rel_v[[rows(R_LO * P - 1, 1)[0], rows((R_HI + 1) * P, 1)[0]]],
        "router_wT": a("L0_ffn_router_w").T,
        "gate_w": a("L0_ffn_gate_w"), "up_w": a("L0_ffn_up_w"), "down_w": a("L0_ffn_down_w"),
        "gate_b": a("L0_ffn_gate_b").reshape(NE, FT, P).transpose(0, 2, 1),
        "up_b": a("L0_ffn_up_b").reshape(NE, FT, P).transpose(0, 2, 1),
        "down_b": a("L0_ffn_down_b"),
    }
    arrays = {n: np.ascontiguousarray(v) for n, v in arrays.items()}
    nc = bacc.Bacc("TRN2", target_bir_lowering=False, num_devices=1)
    hbm = {n: nc.dram_tensor(f"in_{n}", v.shape, mybir.dt.from_np(v.dtype), kind="ExternalInput").ap()
           for n, v in arrays.items()}
    hbm["out"] = nc.dram_tensor("out", (TOK, D), FP32, kind="ExternalOutput").ap()
    program(nc, hbm)
    r = run_bass_kernel_spmd(nc, [{f"in_{n}": v for n, v in arrays.items()}], core_ids=[0])
    return r.results[0]["out"].reshape(B, L, D)
```

```python
import math
from contextlib import ExitStack

import concourse.bass as bass
from concourse import mybir

FP32 = mybir.dt.float32
BF16 = mybir.dt.bfloat16
FP16 = mybir.dt.float16
ALU = mybir.AluOpType
ACT = mybir.ActivationFunctionType
AX = mybir.AxisListType

P = 128
B, L, D, H, DK = 2, 2048, 256, 16, 16
MAXLEN = 256
TOK = B * L
BH = B * H
NB = L // P
KD = D // P
CH = 512
NCH = TOK // CH
TPC = CH // P
NE, F = 8, 512
FT = F // P
EPS = 1e-5
PARTS = 6 * DK
Q_PLANES = (0, 0, 1, 1, 0, 2)
K_PLANES = (0, 1, 0, 1, 2, 0)

M_LO, M_HI = -6, 2
WIN = (M_HI - M_LO + 1) * P
RELW = WIN + P
REL0 = P * M_LO - (P - 1)


def window(c):
    return max(M_LO, -c), min(M_HI, NB - 1 - c)


def blocks(c):
    lo, hi = window(c)
    return hi - lo + 1


def rel_groups(c):
    return -(-(blocks(c) + 1) // 4)


GROUPS_BH = sum(rel_groups(c) for c in range(NB))
GROUPS_BEFORE = [sum(rel_groups(i) for i in range(c)) for c in range(NB)]
R_LO, R_HI = -6, 1
RVW = (R_HI - R_LO + 1) * P
PGROUPS = NB // 4
TGROUPS = PGROUPS + 2


def rel_blocks(c):
    return max(R_LO, -(c + 1)), min(R_HI, NB - 1 - c)


def left_end(c):
    return c + R_LO >= 0


def right_end(c):
    return c + R_HI + 1 < NB


def groups_of(c):
    lo, hi = rel_blocks(c)
    return PGROUPS + -(-(hi - lo + 1) // 4)


V_STEP = 10
STEP = 2 * NB
UNITS = BH * NB
LAG_RSTORE, LAG_SKEW, LAG_S, LAG_E, LAG_PSTORE, LAG_UNSKEW, LAG_T, LAG_O = 1, 2, 3, 4, 5, 6, 7, 8
VC = DK + 2
PROB_SCALE_LN = 12 * math.log(2.0)
WEIGHTS = ("gate_w", "up_w", "down_w")
W_SCALE = 16.0
PEEL = 10


def rel_group_index(it, k):
    return it * (2 * GROUPS_BH) + (k // NB) * GROUPS_BH + GROUPS_BEFORE[k % NB]


def t_group_index(it, k):
    return it * (STEP * TGROUPS) + k * TGROUPS


def t_count(c, g):
    return TGROUPS - g if g == groups_of(c) - 1 else 1


def evac_plan(c):
    return ["act", "dve", "act", "dve", "act", "dve"][:groups_of(c)]


EV = {e: [sum(evac_plan(i).count(e) for i in range(c)) for c in range(NB)] for e in ("act", "dve")}
EV_BH = {e: sum(evac_plan(c).count(e) for c in range(NB)) for e in ("act", "dve")}


def evac_count(e, it, k, g):
    c = k % NB
    return it * (2 * EV_BH[e]) + (k // NB) * EV_BH[e] + EV[e][c] + evac_plan(c)[: g + 1].count(e)


def evac_of(it, k, g):
    if g < 0:
        k, g = k - 1, g + TGROUPS
    g = min(g, groups_of(k % NB) - 1)
    e = evac_plan(k % NB)[g]
    return e, evac_count(e, it, k, g)


def bank_items(k):
    scores = [("scores", k - LAG_S, bank) for bank in range(L // CH)] if k >= LAG_S else []
    return scores + [("rel", k, n) for n in range(rel_groups(k % NB))]


BANKS = 3
BANK_ITEMS = [item for k in range(PEEL + STEP + LAG_O) for item in bank_items(k)]
ITEM_INDEX = {item: i for i, item in enumerate(BANK_ITEMS)}
assert (STEP * TGROUPS) % (2 * BANKS) == 0
assert (ITEM_INDEX[("rel", PEEL + STEP, 0)] - ITEM_INDEX[("rel", PEEL, 0)]) % BANKS == 0


def group_blocks(c, g):
    if g < PGROUPS:
        return range(4 * g, 4 * g + 4)
    lo, hi = rel_blocks(c)
    n = 4 * (g - PGROUPS)
    return range(n, min(n + 4, hi - lo + 1))


def segments(c):
    lo, hi = window(c)
    edges = [(0, (c + lo) * P, -1), ((c + lo) * P, (c + hi + 1) * P, 0), ((c + hi + 1) * P, L, 1)]
    out = []
    for bank in range(L // CH):
        for a, z, kind in edges:
            a, z = max(a, bank * CH), min(z, (bank + 1) * CH)
            if a < z:
                out.append((bank, a, z, kind))
    return out


def project(nc, hbm, keep):
    with ExitStack() as ctx:
        def sb(name, shape, dt=FP32):
            return ctx.enter_context(nc.sbuf_tensor(name, shape, dt))

        def sem(name):
            return ctx.enter_context(nc.semaphore(name))

        FULL = ((0, 0), (0, 1), (1, 0), (1, 1))
        NFULL = len(FULL)
        wq = sb("wq", [P, KD, D])
        wk = sb("wk", [P, KD, D])
        wv = sb("wv", [P, KD, D])
        wr = sb("wr", [P, KD, NE])
        bq = sb("bq", [P, 2])
        bk = sb("bk", [P, 2])
        kbias = sb("kbias", [P, 2])
        bv = sb("bv", [P, D])
        rk = sb("rk", [DK, RELW])
        rk_rest = sb("rk_rest", [DK, RELW])
        rk_parts = sb("rk_parts", [DK, 3, RELW], BF16)
        xin = sb("xin", [P, 2, TPC, D])
        stats = sb("stats", [P, TPC, 6])
        moments = sb("moments", [P, 2, TPC, 2])
        eps = sb("eps", [P, 1])
        std = sb("std", [P, 2, TPC])
        rstd = sb("rstd", [P, 2, TPC])
        xn = sb("xn", [P, 2, TPC, D])
        xc = [sb(f"xc{i}", [P, KD, CH]) for i in range(2)]
        xh = [sb(f"xh{i}", [P, KD, CH], FP16) for i in range(2)]
        xl = [sb(f"xl{i}", [P, KD, CH], FP16) for i in range(2)]
        full = sb("full", [P, NFULL, CH])
        rest = sb("rest", [P, NFULL, CH])
        planes = sb("planes", [P, NFULL, 3, CH], BF16)
        psum = [ctx.enter_context(nc.psum_tensor(f"pa{i}", [P, CH], FP32)) for i in range(8)]
        xt_ps, qk_ps, v_ps, r_ps = psum[0:2], psum[2:4], psum[6:8], psum[4]

        s_x = [sem(f"a_x{i}") for i in range(2)]
        s_w = sem("a_weights")
        s_rk = sem("a_rel_k")
        s_rkp = sem("a_rel_k_parts")
        s_rkd = sem("a_rel_k_stacked")
        s_kb = sem("a_k_bias")
        s_st = sem("a_stats")
        s_mo = sem("a_moments")
        s_std = sem("a_std")
        s_rstd = sem("a_rstd")
        s_xn = sem("a_xn")
        s_xt = sem("a_xt")
        s_xc = sem("a_xc")
        s_xh = sem("a_x_high")
        s_xl = sem("a_x_low")
        s_xw = [sem(f"a_x_stored{i}") for i in range(2)]
        s_qk = sem("a_qk")
        s_f = sem("a_full")
        s_hi = sem("a_high")
        s_fr = sem("a_rest")
        s_mid = sem("a_middle")
        s_pl = sem("a_planes")
        s_plw = [sem(f"a_planes_stored{v}") for v in range(NFULL)]
        s_v = sem("a_v_router")
        s_ve = sem("a_v_router_read")
        s_id = sem("a_constants")
        s_pre = sem("a_memset")
        block = ctx.enter_context(nc.Block())
        weights = 10

        def chunks(eng, step):
            for par in range(2):
                step(0, par, True, False)
            with eng.Fori(1, NCH // 2 - 1) as gg:
                for par in range(2):
                    step(gg, par, False, False)
            for par in range(2):
                step(NCH // 2 - 1, par, False, True)

        @block.sync
        def _(sp):
            def load_x(gg, par):
                g = gg * 2 + par
                sp.dma_start(xin[:, par, :, :], hbm["x"][bass.ds(g * CH, CH), :].rearrange(
                    "(t p) d -> p t d", p=P)).then_inc(s_x[par], 16)

            load_x(0, 0)
            load_x(0, 1)
            for t, src in ((wq, hbm["wqT"]), (wk, hbm["wkT"]), (wv, hbm["wvT"]), (wr, hbm["router_wT"])):
                sp.dma_start(t[:, :, :], src.rearrange("(k p) n -> p k n", p=P)).then_inc(s_w, 16)
            for t, src in ((bq, hbm["bq"]), (bk, hbm["bk"])):
                sp.dma_start(t[:, :], src).then_inc(s_w, 16)
            sp.dma_start(bv[:, :], hbm["bv"].to_broadcast([P, D])).then_inc(s_w, 16)
            sp.dma_start(keep["rv"][:, :, :], hbm["rel_v"].rearrange("(n p) d -> p n d", p=P)).then_inc(s_w, 16)
            for i, end in enumerate(("rv_lo", "rv_hi")):
                sp.dma_start(keep[end][:, :], hbm["rel_v_ends"][i:i + 1, :].to_broadcast([P, DK])).then_inc(s_w, 16)
            sp.dma_start(rk[:, :], hbm["rel_kT"]).then_inc(s_rk, 16)

            def step(gg, par, first, last):
                g = gg * 2 + par
                if not last:
                    sp.wait_ge(s_xn, g + 1)
                    sp.nop(nofuse=True)
                    load_x(gg + 1, par)
                sp.wait_ge(s_xl, g + 1)
                sp.nop(nofuse=True)
                for part, src in enumerate((xh, xl)):
                    sp.dma_start(hbm["x_parts"][part, :, :, bass.ds(g * CH, CH)],
                                 src[par][:, :, :]).then_inc(s_xw[par], 16)
                for v, (kind, half) in enumerate(FULL):
                    sp.wait_ge(s_pl, g * NFULL + v + 1)
                    sp.nop(nofuse=True)
                    rows = hbm["planes"][kind, :, half * P:(half + 1) * P, bass.ds(g * CH, CH)]
                    sp.dma_start(rows.rearrange("r p n -> p r n"), planes[:, v, :, :]).then_inc(s_plw[v], 16)

                if last and par == 0:
                    sp.wait_ge(s_rkp, 4)
                    sp.nop(nofuse=True)
                    for s, plane in enumerate(K_PLANES):
                        sp.dma_start(keep["rk_stack"][DK * s:DK * (s + 1), :],
                                     rk_parts[:, plane, :]).then_inc(s_rkd, 16)

            chunks(sp, step)
            sp.wait_ge(s_rkd, 16 * len(K_PLANES))
            sp.nop(nofuse=True)
            for i in range(2):
                sp.wait_ge(s_xw[i], 2 * 16 * NCH // 2)
                sp.nop(nofuse=True)
            for v in range(NFULL):
                sp.wait_ge(s_plw[v], 16 * NCH)
                sp.nop(nofuse=True)

        @block.gpsimd
        def _(pool):
            ident, upper = keep["ident"], keep["upper"]
            nc.gpsimd.memset(ident[:, :], 0.0).then_inc(s_pre, 1)
            nc.gpsimd.memset(upper[:, :], 1.0).then_inc(s_pre, 1)
            pool.wait_ge(s_pre, 2)
            nc.gpsimd.affine_select(out=ident[:, :], in_=ident[:, :], compare_op=ALU.not_equal,
                                    fill=1.0, base=0, pattern=[[-1, P]], channel_multiplier=1).then_inc(s_id, 1)
            nc.gpsimd.affine_select(out=upper[:, :], in_=upper[:, :], compare_op=ALU.is_ge,
                                    fill=0.0, base=0, pattern=[[1, P]], channel_multiplier=-1).then_inc(s_id, 1)

            def step(gg, par, first, last):
                g = gg * 2 + par
                pool.wait_ge(s_xh, g + 1)
                pool.nop(nofuse=True)
                nc.gpsimd.tensor_tensor(xl[par][:, :, :], xc[par][:, :, :], xh[par][:, :, :],
                                        ALU.subtract).then_inc(s_xl, 1)
                for v in range(NFULL):
                    pool.wait_ge(s_mid, g * NFULL + v + 1)
                    pool.nop(nofuse=True)
                    nc.gpsimd.tensor_tensor(planes[:, v, 2, :], rest[:, v, :], planes[:, v, 1, :],
                                            ALU.subtract).then_inc(s_pl, 1)

            chunks(pool, step)

        @block.scalar
        def _(act):
            def deviations(gg, par):
                act.wait_ge(s_mo, (gg * 2 + par) * TPC + TPC)
                nc.scalar.activation(std[:, par, :], moments[:, par, :, 1], ACT.Sqrt,
                                     bias=eps[:, 0:1]).then_inc(s_std, 1)

            act.wait_ge(s_kb, 1)
            deviations(0, 0)
            act.wait_ge(s_kb, 2)

            def step(gg, par, first, last):
                g = gg * 2 + par
                if not (last and par):
                    deviations(*((gg, 1) if par == 0 else (gg + 1, 0)))

                act.wait_ge(s_xc, g + 1)
                if not first:
                    act.wait_ge(s_xw[par], gg * 32)
                nc.scalar.copy(xh[par][:, :, :], xc[par][:, :, :]).then_inc(s_xh, 1)

                def middle(v):
                    act.wait_ge(s_fr, g * NFULL + v + 1)
                    nc.scalar.copy(planes[:, v, 1, :], rest[:, v, :]).then_inc(s_mid, 1)

                for v, (kind, half) in enumerate(FULL):
                    act.wait_ge(s_qk, g * NFULL + v + 1)
                    if not (first and par == 0):
                        act.wait_ge(s_fr, (g - 1) * NFULL + v + 1)
                    bias, scale = (bq, 1.0) if kind == 0 else (kbias, DK ** -0.5)
                    nc.scalar.activation(full[:, v, :], qk_ps[half][:, :], ACT.Identity,
                                         bias=bias[:, half:half + 1], scale=scale).then_inc(s_f, 1)
                    if v >= 1:
                        middle(v - 1)
                middle(NFULL - 1)

            chunks(act, step)

        @block.vector
        def _(dve):
            nc.vector.memset(eps[:, :], EPS).then_inc(s_kb, 1)

            def normalise(gg, par):
                g = gg * 2 + par
                dve.wait_ge(s_x[par], gg * 16 + 16)
                for t in range(TPC):
                    nc.vector.bn_stats(stats[:, t, :], xin[:, par, t, :]).then_inc(s_st, 1)
                dve.wait_ge(s_st, g * TPC + TPC)
                dve.nop(nofuse=True)
                for t in range(TPC):
                    nc.vector.bn_aggr(moments[:, par, t, :], stats[:, t, :]).then_inc(s_mo, 1)
                dve.wait_ge(s_std, g + 1)
                nc.vector.reciprocal(rstd[:, par, :], std[:, par, :]).then_inc(s_rstd, 1)
                dve.wait_ge(s_rstd, g + 1)
                for t in range(TPC):
                    ins = nc.vector.tensor_scalar(xn[:, par, t, :], xin[:, par, t, :], moments[:, par, t, 0:1],
                                                  rstd[:, par, t:t + 1], ALU.subtract, ALU.mult)
                ins.then_inc(s_xn, 1)

            normalise(0, 0)
            dve.wait_ge(s_w, 16 * weights)
            nc.vector.tensor_scalar(kbias[:, :], bk[:, :], DK ** -0.5, None, ALU.mult).then_inc(s_kb, 1)

            def relative_keys():
                dve.wait_ge(s_rk, 16)
                nc.vector.tensor_copy(rk_parts[:, 0, :], rk[:, :]).then_inc(s_rkp, 1)
                dve.wait_ge(s_rkp, 1)
                nc.vector.tensor_tensor(rk_rest[:, :], rk[:, :], rk_parts[:, 0, :], ALU.subtract).then_inc(s_rkp, 1)
                dve.wait_ge(s_rkp, 2)
                nc.vector.tensor_copy(rk_parts[:, 1, :], rk_rest[:, :]).then_inc(s_rkp, 1)
                dve.wait_ge(s_rkp, 3)
                nc.vector.tensor_tensor(rk_parts[:, 2, :], rk_rest[:, :], rk_parts[:, 1, :],
                                        ALU.subtract).then_inc(s_rkp, 1)

            def step(gg, par, first, last):
                g = gg * 2 + par
                if not first:
                    dve.wait_ge(s_xl, g - 1)
                dve.wait_ge(s_xt, g + 1)
                for k in range(KD):
                    ins = nc.vector.tensor_copy(xc[par][:, k, :], xt_ps[k][:, :])
                ins.then_inc(s_xc, 1)
                if not (last and par):
                    normalise(*((gg, 1) if par == 0 else (gg + 1, 0)))
                for v in range(NFULL):
                    i = g * NFULL + v
                    dve.wait_ge(s_f, i + 1)
                    if not (first and par == 0):
                        dve.wait_ge(s_plw[v], g * 16)
                    nc.vector.tensor_copy(planes[:, v, 0, :], full[:, v, :]).then_inc(s_hi, 1)
                    dve.wait_ge(s_hi, i + 1)
                    nc.vector.tensor_tensor(rest[:, v, :], full[:, v, :], planes[:, v, 0, :],
                                            ALU.subtract).then_inc(s_fr, 1)
                for t in range(TPC):
                    if t % 2 == 0:
                        dve.wait_ge(s_v, g * 3 + t // 2 + 1)
                    ins = nc.vector.tensor_tensor(
                        keep["v"][:, :, g * TPC + t, :],
                        v_ps[t // 2][:, (t % 2) * D:(t % 2 + 1) * D].rearrange("p (h d) -> p h d", h=H),
                        bv[:, :].rearrange("p (h d) -> p h d", h=H), ALU.add)
                    if t % 2:
                        ins.then_inc(s_ve, 1)
                dve.wait_ge(s_v, g * 3 + 3)
                nc.vector.tensor_copy(keep["logits"][:, bass.ds(g * TPC, TPC), :],
                                      r_ps[:, 0:TPC * NE].rearrange("p (t e) -> p t e", t=TPC)).then_inc(s_ve, 1)

                if first and par:
                    relative_keys()

            chunks(dve, step)

        @block.tensor
        def _(pe):
            pe.wait_ge(s_id, 2)
            pe.wait_ge(s_w, 16 * weights)

            def step(gg, par, first, last):
                g = gg * 2 + par
                start = first and par == 0
                pe.wait_ge(s_xn, g + 1)
                if not start:
                    pe.wait_ge(s_xc, g)
                for k in range(KD):
                    for t in range(TPC):
                        ins = nc.tensor.transpose(xt_ps[k][:, t * P:(t + 1) * P],
                                                  xn[:, par, t, k * P:(k + 1) * P], keep["ident"][:, :])
                ins.then_inc(s_xt, 1)
                pe.wait_ge(s_xc, g + 1)
                for v, (kind, half) in enumerate(FULL):
                    if not (start and v < 2):
                        pe.wait_ge(s_f, g * NFULL + v - 1)
                    for k in range(KD):
                        ins = nc.tensor.matmul(qk_ps[half][:, :], (wq, wk)[kind][:, k, half * P:(half + 1) * P],
                                               xc[par][:, k, :], start=(k == 0), stop=(k == KD - 1))
                    ins.then_inc(s_qk, 1)
                for t in range(TPC):
                    if t % 2 == 0 and not start:
                        pe.wait_ge(s_ve, (g - 1) * 3 + t // 2 + 1)
                    for k in range(KD):
                        ins = nc.tensor.matmul(v_ps[t // 2][:, (t % 2) * D:(t % 2 + 1) * D],
                                               xc[par][:, k, t * P:(t + 1) * P], wv[:, k, :],
                                               start=(k == 0), stop=(k == KD - 1))
                    if t % 2:
                        ins.then_inc(s_v, 1)
                if not start:
                    pe.wait_ge(s_ve, g * 3)
                for t in range(TPC):
                    for k in range(KD):
                        ins = nc.tensor.matmul(r_ps[:, t * NE:(t + 1) * NE], xc[par][:, k, t * P:(t + 1) * P],
                                               wr[:, k, :], start=(k == 0), stop=(k == KD - 1))
                ins.then_inc(s_v, 1)

            chunks(pe, step)


def attend(nc, hbm, keep):
    with ExitStack() as ctx:
        def sb(name, shape, dt=FP32):
            return ctx.enter_context(nc.sbuf_tensor(name, shape, dt))

        def sem(name):
            return ctx.enter_context(nc.semaphore(name))

        SLOTS_P, SLOTS_PT = 4, 2 * BANKS
        PROBW = RVW + P
        HALF = P // 2
        q_stack = [sb(f"q_stack{i}", [PARTS, L], BF16) for i in range(2)]
        k_stack = [sb(f"k_stack{i}", [PARTS, L], BF16) for i in range(2)]
        v_head = [sb(f"v_head{i}", [P, NB, 3, VC], BF16) for i in range(2)]
        v_rest = sb("v_rest", [P, NB, DK])
        rv_parts = sb("rv_parts", [P, RVW // P, 3, DK + 1], BF16)
        rv_rest = sb("rv_rest", [P, RVW // P, DK])
        rv_ends = sb("rv_ends", [P, 2, DK])
        ident16 = sb("ident16", [P, P], FP16)
        rel = [sb(f"rel{i}", [P, RELW]) for i in range(2)]
        skewed = [sb(f"skewed{i}", [P, WIN]) for i in range(2)]
        scores = [sb(f"scores{i}", [P, L]) for i in range(SLOTS_P)]
        probs = [sb(f"probs{i}", [P, 2, L + 2 * P], FP16) for i in range(SLOTS_P)]
        unskewed = [sb(f"unskewed{i}", [P, 2, RVW], FP16) for i in range(2)]
        pt = [sb(f"pt{i}", [P, 2, CH], FP16) for i in range(SLOTS_PT)]
        no_values = sb("no_values", [P, 3 * VC], BF16)
        end_part = sb("end_part", [P, P])
        end_sums = sb("end_sums", [P, 2, 2])
        end_values = sb("end_values", [P, 2, 2, DK])
        part_max = sb("part_max", [P, 2, 8])
        neg_max = sb("neg_max", [P, 2])
        exp_bias = sb("exp_bias", [P, 2])
        sums = sb("sums", [P, 8, 2])
        inv_sum = sb("inv_sum", [P, 2])
        o_sum = sb("o_sum", [P, 2, VC])
        o_lo = sb("o_lo", [P, 2, DK])
        o_hi = sb("o_hi", [P, 2, DK])
        psum = [ctx.enter_context(nc.psum_tensor(f"pb{i}", [P, CH], FP32)) for i in range(BANKS + 2)]
        score_ps, o_ps = psum[:BANKS], psum[BANKS:]
        t_ps = [ctx.enter_context(nc.psum_tensor(f"pt_ps{i}", [P, 2, CH], FP16)) for i in range(BANKS)]

        s_pad = sem("b_pads")
        s_stk = [sem(f"b_stacks{i}") for i in range(2)]
        s_vh = sem("b_v_head")
        s_g = sem("b_rel_product")
        s_ge = sem("b_rel_on_chip")
        s_gw = [sem(f"b_rel_stored{i}") for i in range(2)]
        s_gr = [sem(f"b_skewed{i}") for i in range(2)]
        s_s = sem("b_scores")
        s_add = sem("b_scores_added")
        s_nm = sem("b_neg_max")
        s_rm = sem("b_raw_max")
        s_exp = sem("b_exp")
        s_hi = sem("b_high")
        s_lo = sem("b_low")
        s_vp = sem("b_v_parts")
        s_rv = sem("b_rel_v_parts")
        s_pw = [sem(f"b_probs_stored{i}") for i in range(2)]
        s_pr = [sem(f"b_unskewed{i}") for i in range(2)]
        s_t = sem("b_transposed")
        s_ev = {"act": sem("b_t_evac_act"), "dve": sem("b_t_evac_dve")}
        s_pv = sem("b_pt_used")
        s_o1 = sem("b_out_scaled")
        s_os = sem("b_out_summed")
        s_o = sem("b_out")
        block = ctx.enter_context(nc.Block())
        pad_tensors = 2 * SLOTS_P + 1

        def skew_src(slot, width):
            return bass.AP(hbm["rel_scratch"].tensor, slot * P * RELW + P - 1, [[RELW - 1, P], [1, width]])

        def unskew_src(slot, width):
            return bass.AP(hbm["prob_scratch"].tensor, slot * P * 2 * PROBW,
                           [[2 * PROBW + 1, P], [PROBW, 2], [1, width]])

        def pipeline(eng, step):
            for k in range(PEEL):
                step(0, k)
            with eng.Fori(0, UNITS // STEP - 1) as it:
                for k in range(PEEL, PEEL + STEP):
                    step(it, k)
            for k in range(PEEL, STEP + LAG_O):
                step(UNITS // STEP - 1, k)

        def exists(it, k):
            return not isinstance(it, int) or 0 <= STEP * it + k < UNITS

        def uses(it, k, slots, inc=1):
            return it * (STEP // slots * inc) + (k // slots + 1) * inc

        def bank_of(kind, k, n):
            return score_ps[ITEM_INDEX[(kind, k, n)] % BANKS]

        def wait_bank(it, kind, k, n):
            i = ITEM_INDEX[(kind, k, n)] - BANKS
            while i >= 0 and not exists(it, BANK_ITEMS[i][1]):
                i -= BANKS
            if i >= 0:
                last, u, m = BANK_ITEMS[i]
                if last == "scores":
                    nc.tensor.wait_ge(s_add, it * (4 * STEP) + 4 * u + m + 1)
                else:
                    nc.tensor.wait_ge(s_ge, rel_group_index(it, u) + m + 1)

        def load_stacks(sp, it, head, planes=range(6)):
            b = head % 2
            for s in planes:
                rows = bass.ds((it + head // 2) * DK, DK)
                sp.dma_start(q_stack[b][DK * s:DK * (s + 1), :],
                             hbm["planes"][0, Q_PLANES[s], rows, b * L:(b + 1) * L]).then_inc(s_stk[b], 16)
                sp.dma_start(k_stack[b][DK * s:DK * (s + 1), :],
                             hbm["planes"][1, K_PLANES[s], rows, b * L:(b + 1) * L]).then_inc(s_stk[b], 16)

        STK = 12 * 16

        @block.sync
        def _(sp):
            load_stacks(sp, 0, 0)

            def step(it, k):
                if k >= LAG_RSTORE and exists(it, k - LAG_RSTORE):
                    u = k - LAG_RSTORE
                    sp.wait_ge(s_ge, rel_group_index(it, u + 1))
                    sp.nop(nofuse=True)
                    if u >= 2:
                        sp.wait_ge(s_gr[u % 2], uses(it, u - 2, 2, 16))
                        sp.nop(nofuse=True)
                    w = (blocks(u % NB) + 1) * P
                    for rows, cols in ((slice(0, HALF), slice(HALF, w)), (slice(HALF, P), slice(0, w - HALF))):
                        sp.dma_start(hbm["rel_scratch"][u % 2, rows, cols],
                                     rel[u % 2][rows, cols]).then_inc(s_gw[u % 2], 16)
                if k >= LAG_SKEW and exists(it, k - LAG_SKEW):
                    u = k - LAG_SKEW
                    sp.wait_ge(s_gw[u % 2], uses(it, u, 2, 32))
                    sp.nop(nofuse=True)
                    if u >= 2:
                        sp.wait_ge(s_add, it * (4 * STEP) + 4 * (u - 1))
                        sp.nop(nofuse=True)
                    w = blocks(u % NB) * P
                    sp.dma_start(skewed[u % 2][:, 0:w], skew_src(u % 2, w)).then_inc(s_gr[u % 2], 16)
                if k >= LAG_UNSKEW and exists(it, k - LAG_UNSKEW):
                    u = k - LAG_UNSKEW
                    sp.wait_ge(s_pw[u % 2], uses(it, u, 2, 32))
                    sp.nop(nofuse=True)
                    if u >= 2:
                        sp.wait_ge(s_t, t_group_index(it, u - 1))
                        sp.nop(nofuse=True)
                    lo, hi = rel_blocks(u % NB)
                    w = (hi - lo + 1) * P
                    sp.dma_start(unskewed[u % 2][:, :, 0:w], unskew_src(u % 2, w)).then_inc(s_pr[u % 2], 16)
                if k >= LAG_PSTORE and exists(it, k - LAG_PSTORE):
                    u = k - LAG_PSTORE
                    c = u % NB
                    sp.wait_ge(s_lo, it * STEP + u + 1)
                    sp.nop(nofuse=True)
                    if u >= 2:
                        sp.wait_ge(s_pr[u % 2], uses(it, u - 2, 2, 16))
                        sp.nop(nofuse=True)
                    lo, hi = rel_blocks(c)
                    col, w = (1 + c + lo) * P, (hi - lo + 2) * P
                    for rows, a, z in ((slice(0, HALF), 0, w - HALF), (slice(HALF, P), HALF, w)):
                        sp.dma_start(hbm["prob_scratch"][u % 2, rows, :, a:z],
                                     probs[u % SLOTS_P][rows, :, col + a:col + z]).then_inc(s_pw[u % 2], 16)
                if 4 <= k % NB < 10 and exists(it, (k // NB + 1) * NB):
                    head = k // NB + 1
                    if head >= 2 and k % NB == 4:
                        sp.wait_ge(s_s, it * (4 * STEP) + 4 * NB * (head - 1))
                        sp.nop(nofuse=True)
                    load_stacks(sp, it, head, [k % NB - 4])

            pipeline(sp, step)

        @block.gpsimd
        def _(pool):
            nc.gpsimd.memset(no_values[:, :], 0.0).then_inc(s_pad, 1)
            for i in range(SLOTS_P):
                nc.gpsimd.memset(probs[i][:, :, 0:P], 0.0).then_inc(s_pad, 1)
                nc.gpsimd.memset(probs[i][:, :, P + L:], 0.0).then_inc(s_pad, 1)
            nc.gpsimd.tensor_copy(ident16[:, :], keep["ident"][:, :]).then_inc(s_rv, 1)
            for i in range(2):
                nc.gpsimd.memset(v_head[i][:, :, 0, VC - 1:VC], 1.0)
                nc.gpsimd.memset(v_head[i][:, :, 1:3, VC - 1:VC], 0.0)
            nc.gpsimd.memset(rv_parts[:, :, 0, 0:1], -1.0)
            nc.gpsimd.memset(rv_parts[:, :, 1:3, 0:1], 0.0)
            nc.gpsimd.tensor_copy(rv_parts[:, :, 0, 1:], keep["rv"][:, :, :]).then_inc(s_rv, 1)
            pool.wait_ge(s_rv, 2)
            nc.gpsimd.tensor_tensor(rv_rest[:, :, :], keep["rv"][:, :, :], rv_parts[:, :, 0, 1:],
                                    ALU.subtract).then_inc(s_rv, 1)
            pool.wait_ge(s_rv, 3)
            nc.gpsimd.tensor_copy(rv_parts[:, :, 1, 1:], rv_rest[:, :, :]).then_inc(s_rv, 1)
            pool.wait_ge(s_rv, 4)
            nc.gpsimd.tensor_tensor(rv_parts[:, :, 2, 1:], rv_rest[:, :, :], rv_parts[:, :, 1, 1:],
                                    ALU.subtract).then_inc(s_rv, 1)

            def v_part(it, head, stage):
                v = keep["v"][:, it + head // 2, (head % 2) * NB:(head % 2 + 1) * NB, :]
                parts = v_head[head % 2]
                n = it * 6 + head * 3
                if stage == 0 and head >= 1:
                    pool.wait_ge(s_pv, t_group_index(it, (head - 1) * NB) + 1)
                    pool.nop(nofuse=True)
                if stage > 0:
                    pool.wait_ge(s_vp, n + stage)
                    pool.nop(nofuse=True)
                if stage == 0:
                    nc.gpsimd.tensor_copy(parts[:, :, 0, 1:1 + DK], v).then_inc(s_vp, 1)
                if stage == 1:
                    nc.gpsimd.tensor_tensor(v_rest[:, :, :], v, parts[:, :, 0, 1:1 + DK], ALU.subtract).then_inc(s_vp, 1)
                if stage == 2:
                    nc.gpsimd.tensor_copy(parts[:, :, 1, 1:1 + DK], v_rest[:, :, :]).then_inc(s_vp, 1)
                if stage == 3:
                    nc.gpsimd.tensor_tensor(parts[:, :, 2, 1:1 + DK], v_rest[:, :, :], parts[:, :, 1, 1:1 + DK],
                                            ALU.subtract).then_inc(s_vh, 1)

            def output(it, k):
                c, head = k % NB, k // NB
                slot = k % 2
                total = o_sum[:, slot, :]
                left, right = left_end(c), right_end(c)
                links = [it * (4 * STEP) + 4 * k]

                def link(ins, n=1):
                    links[0] += n
                    ins.then_inc(s_o1, n)
                    pool.wait_ge(s_o1, links[0])
                    pool.nop(nofuse=True)

                pool.wait_ge(s_os, it * STEP + k + 1)
                pool.nop(nofuse=True)
                e = slice(0 if left else 1, 2 if right else 1)
                count = 2 if left and right else 1
                cols = total[:, 0:2 + DK:1 + DK] if count == 2 else total[:, (1 + DK) * e.start:(1 + DK) * e.start + 1]
                link(nc.gpsimd.tensor_tensor(end_sums[:, slot, e], sums[:, k % 8, e], cols, ALU.add))
                values = rv_ends[:, e, :] if left else keep["rv_hi"][:, :].rearrange("p (e d) -> p e d", e=1)
                link(nc.gpsimd.tensor_tensor(
                    end_values[:, slot, e, :], values,
                    end_sums[:, slot, e].rearrange("p (e d) -> p e d", d=1).to_broadcast([P, count, DK]), ALU.mult))
                res = total[:, 1:1 + DK]
                if left:
                    link(nc.gpsimd.tensor_tensor(o_lo[:, slot, :], end_values[:, slot, 0, :], res, ALU.add),
                         1 if right else 2)
                    res = o_lo[:, slot, :]
                if right:
                    link(nc.gpsimd.tensor_tensor(o_hi[:, slot, :], end_values[:, slot, 1, :], res, ALU.add),
                         1 if left else 2)
                    res = o_hi[:, slot, :]
                nc.gpsimd.tensor_tensor(keep["v"][:, it + head // 2, (head % 2) * NB + c, :], res,
                                        inv_sum[:, slot:slot + 1].to_broadcast([P, DK]), ALU.mult).then_inc(s_o, 1)

            def step(it, k):
                if k >= LAG_O:
                    output(it, k - LAG_O)
                u = k - LAG_E
                if u >= 0 and exists(it, u):
                    pool.wait_ge(s_hi, it * STEP + u + 1)
                    nc.gpsimd.tensor_tensor(probs[u % SLOTS_P][:, 1, P:P + L], scores[u % SLOTS_P][:, :],
                                            probs[u % SLOTS_P][:, 0, P:P + L], ALU.subtract).then_inc(s_lo, 1)
                if V_STEP <= k % NB < V_STEP + 4 and exists(it, (k // NB + 1) * NB):
                    v_part(it, k // NB + 1, k % NB - V_STEP)

            for stage in range(4):
                v_part(0, 0, stage)
            pipeline(pool, step)

        @block.tensor
        def _(pe):
            pe.sem_inc(s_pv, 1)
            pe.wait_ge(s_pad, pad_tensors)
            pe.wait_ge(s_rv, 5)

            def rel_group(it, k, n):
                c = k % NB
                if n == 0 and c == 0:
                    pe.wait_ge(s_stk[(k // NB) % 2], it * STK + (k // NB // 2 + 1) * STK)
                wait_bank(it, "rel", k, n)
                j0 = (window(c)[0] - M_LO) * P + n * CH
                w = min(CH, (blocks(c) + 1) * P - n * CH)
                nc.tensor.matmul(bank_of("rel", k, n)[:, 0:w], q_stack[(k // NB) % 2][:, c * P:(c + 1) * P],
                                 keep["rk_stack"][:, j0:j0 + w], start=True, stop=True).then_inc(s_g, 1)

            def score_bank(it, k, bank):
                c, head = k % NB, k // NB
                wait_bank(it, "scores", k, bank)
                ps = bank_of("scores", k, bank)
                nc.tensor.matmul(ps[:, :], q_stack[head % 2][:, c * P:(c + 1) * P],
                                 k_stack[head % 2][:, bank * CH:(bank + 1) * CH], start=True, stop=True).then_inc(s_s, 1)

            def transposes(it, k, g):
                c = k % NB
                idx = k * TGROUPS + g
                if idx >= BANKS:
                    e, n = evac_of(it, k, g - BANKS)
                    pe.wait_ge(s_ev[e], n)
                if g == 0:
                    pe.wait_ge(s_lo, it * STEP + k + 1)
                if g == PGROUPS:
                    pe.wait_ge(s_pr[k % 2], uses(it, k, 2, 16))
                for part in range(2):
                    for i, blk in enumerate(group_blocks(c, g)):
                        src = probs[k % SLOTS_P][:, part, (1 + blk) * P:(2 + blk) * P] if g < PGROUPS else \
                            unskewed[k % 2][:, part, blk * P:(blk + 1) * P]
                        ins = nc.tensor.transpose(t_ps[idx % BANKS][:, part, i * P:(i + 1) * P], src, ident16[:, :])
                ins.then_inc(s_t, t_count(c, g))

            def values(it, k, g):
                c, head = k % NB, k // NB
                idx = k * TGROUPS + g
                out = o_ps[k % 2][:, 0:3 * VC].rearrange("p (r n) -> p r n", r=3)
                src = pt[idx % SLOTS_PT]
                if g == 0:
                    if c == 0:
                        pe.wait_ge(s_vh, it * 2 + head + 1)
                    if k >= 2:
                        pe.wait_ge(s_os, it * STEP + k - 1)
                e, n = evac_of(it, k, g)
                pe.wait_ge(s_ev[e], n)
                if g == 0:
                    nc.tensor.matmul(o_ps[k % 2][:, 0:3 * VC], src[:, 0, 0:P], no_values[:, :], start=True, stop=False)
                last_group = g == groups_of(c) - 1
                blks = group_blocks(c, g)
                for i, blk in enumerate(blks):
                    if g < PGROUPS:
                        a, z = 1, DK + 1 + (blk > c + R_HI + 1)
                        rhs = v_head[head % 2][:, blk, :, a:z]
                    else:
                        a, z = 0, DK + 1
                        rhs = rv_parts[:, blk + rel_blocks(c)[0] - R_LO, :, :]
                    for part in range(2):
                        ins = nc.tensor.matmul(out[:, :, a:z], src[:, part, i * P:(i + 1) * P], rhs, start=False,
                                               stop=last_group and i == len(blks) - 1 and part == 1)
                ins.then_inc(s_pv, t_count(c, g))

            def step(it, k):
                work = []
                if k >= LAG_S and exists(it, k - LAG_S):
                    work += [(score_bank, k - LAG_S, bank) for bank in range(4)]
                if exists(it, k):
                    work += [(rel_group, k, n) for n in range(rel_groups(k % NB))]
                u = k - LAG_T
                groups = groups_of(u % NB) if u >= 0 and exists(it, u) else 0
                pending = []
                if u >= 1 and exists(it, u - 1):
                    last = groups_of((u - 1) % NB) - 1
                    pending = [(u - 1, last - 1), (u - 1, last)]
                for g in range(groups):
                    transposes(it, u, g)
                    if work:
                        f, a, n = work.pop(0)
                        f(it, a, n)
                    pending.append((u, g))
                    if len(pending) > 2:
                        values(it, *pending.pop(0))
                for f, a, n in work:
                    f(it, a, n)
                if not groups:
                    for unit, g in pending:
                        values(it, unit, g)

            pipeline(pe, step)

        def evacuate(eng_name, eng, it, k, g):
            c = k % NB
            idx = k * TGROUPS + g
            eng.wait_ge(s_t, t_group_index(it, k) + g + 1)
            if idx >= SLOTS_PT:
                eng.wait_ge(s_pv, t_group_index(it, k) + g + 2 - SLOTS_PT)
            blks = group_blocks(c, g)
            dst, src = pt[idx % SLOTS_PT], t_ps[idx % BANKS]
            z = len(blks) * P
            copy = nc.scalar.copy if eng_name == "act" else nc.vector.tensor_copy
            copy(dst[:, :, 0:z], src[:, :, 0:z]).then_inc(s_ev[eng_name], 1)

        @block.scalar
        def _(act):
            act.wait_ge(s_pad, pad_tensors)

            def rel_evac(it, k, n):
                act.wait_ge(s_g, rel_group_index(it, k) + n + 1)
                if n == 0 and k >= 2:
                    act.wait_ge(s_gw[k % 2], uses(it, k - 2, 2, 32))
                w = min(CH, (blocks(k % NB) + 1) * P - n * CH)
                nc.scalar.copy(rel[k % 2][:, n * CH:n * CH + w], bank_of("rel", k, n)[:, 0:w]).then_inc(s_ge, 1)

            def exponentials(it, k):
                act.wait_ge(s_nm, it * STEP + k + 1)
                nc.scalar.activation(scores[k % SLOTS_P][:, :], scores[k % SLOTS_P][:, :], ACT.Exp,
                                     bias=exp_bias[:, k % 2:k % 2 + 1],
                                     accum_out=sums[:, k % 8, 0:1]).then_inc(s_exp, 1)

            def step(it, k):
                work = [None] * 4 if k >= LAG_S and exists(it, k - LAG_S) else []
                if exists(it, k):
                    work += list(range(rel_groups(k % NB)))
                u = k - LAG_T
                plan = evac_plan(u % NB) if u >= 0 and exists(it, u) else []
                for g, e in enumerate(plan):
                    if e == "act":
                        evacuate("act", act, it, u, g)
                    if work:
                        n = work.pop(0)
                        if n is not None:
                            rel_evac(it, k, n)
                    if g == 0 and exists(it, k - LAG_E):
                        exponentials(it, k - LAG_E)
                for n in work:
                    if n is not None:
                        rel_evac(it, k, n)
                if not plan and k >= LAG_E and exists(it, k - LAG_E):
                    exponentials(it, k - LAG_E)

            pipeline(act, step)

        @block.vector
        def _(dve):
            dve.wait_ge(s_pad, pad_tensors)
            nc.vector.tensor_copy(rv_ends[:, 0, :], keep["rv_lo"][:, :])
            nc.vector.tensor_tensor(rv_ends[:, 1, :], keep["rv_hi"][:, :], keep["rv_lo"][:, :], ALU.subtract)

            def add_bank(it, k, bank):
                c = k % NB
                lo = window(c)[0]
                dve.wait_ge(s_s, it * (4 * STEP) + 4 * k + bank + 1)
                if bank == 0:
                    dve.wait_ge(s_gr[k % 2], uses(it, k, 2, 16))
                    if k >= SLOTS_P:
                        dve.wait_ge(s_lo, it * STEP + k - SLOTS_P + 1)
                    if k >= 2:
                        dve.wait_ge(s_exp, it * STEP + k - 1)
                dve.nop(nofuse=True)
                ps = bank_of("scores", k, bank)
                for n, (bk_, a, z, kind) in enumerate(segments(c)):
                    if bk_ != bank:
                        continue
                    col = {-1: 0, 0: a - (c + lo) * P, 1: blocks(c) * P - 1}[kind]
                    other = skewed[k % 2][:, col:col + (z - a if kind == 0 else 1)]
                    if kind:
                        other = other.to_broadcast([P, z - a])
                    ins = nc.vector.tensor_tensor_reduce(
                        out=scores[k % SLOTS_P][:, a:z], in0=ps[:, a - bank * CH:z - bank * CH],
                        in1=other, scale=1.0, scalar=-3.0e38, op0=ALU.add, op1=ALU.max,
                        accum_out=part_max[:, k % 2, n:n + 1])
                ins.then_inc(s_add, 1)

            def raw_maximum(it, k):
                dve.wait_ge(s_add, it * (4 * STEP) + 4 * k + 4)
                nc.vector.tensor_reduce(neg_max[:, k % 2:k % 2 + 1], part_max[:, k % 2, 0:len(segments(k % NB))],
                                        axis=AX.X, op=ALU.max, negate=True).then_inc(s_rm, 1)

            def maximum(it, k):
                dve.wait_ge(s_rm, it * STEP + k + 1)
                nc.vector.tensor_scalar(exp_bias[:, k % 2:k % 2 + 1], neg_max[:, k % 2:k % 2 + 1], PROB_SCALE_LN,
                                        None, ALU.add).then_inc(s_nm, 1)

            def high_part(it, k):
                c = k % NB
                dve.wait_ge(s_exp, it * STEP + k + 1)
                if right_end(c):
                    a = (c + R_HI + 1) * P
                    nc.vector.tensor_tensor_reduce(
                        out=end_part[:, :], in0=scores[k % SLOTS_P][:, a:a + P], in1=keep["upper"][:, :], scale=1.0,
                        scalar=0.0, op0=ALU.mult, op1=ALU.add, accum_out=sums[:, k % 8, 1:2])
                if k >= SLOTS_P:
                    dve.wait_ge(s_pw[k % 2], uses(it, k - SLOTS_P, 2, 32))
                    dve.wait_ge(s_t, t_group_index(it, k - SLOTS_P + 1))
                nc.vector.tensor_copy(probs[k % SLOTS_P][:, 0, P:P + L], scores[k % SLOTS_P][:, :]).then_inc(s_hi, 1)

            def output_sum(it, k):
                dve.wait_ge(s_pv, t_group_index(it, k + 1) + 1)
                if k >= 2:
                    dve.wait_ge(s_o, it * STEP + k - 1)
                nc.vector.reciprocal(inv_sum[:, k % 2:k % 2 + 1], sums[:, k % 8, 0:1])
                o = o_ps[k % 2][:, 0:3 * VC].rearrange("p (r n) -> p n r", r=3)
                nc.vector.tensor_reduce(o_sum[:, k % 2, :], o, axis=AX.X, op=ALU.add).then_inc(s_os, 1)

            def step(it, k):
                a, h, t, o = k - LAG_S, k - LAG_E, k - LAG_T, k - LAG_O
                adding = a >= 0 and exists(it, a)
                plan = evac_plan(t % NB) if t >= 0 and exists(it, t) else []
                for g in range(max(len(plan), 5)):
                    if g == 4 and adding:
                        raw_maximum(it, a)
                    if g < 4 and adding:
                        add_bank(it, a, g)
                    if g < len(plan) and plan[g] == "dve":
                        evacuate("dve", dve, it, t, g)
                    if g == 2 and o >= 0:
                        output_sum(it, o)
                    if g == 3 and h >= 0 and exists(it, h):
                        high_part(it, h)
                if adding:
                    maximum(it, a)

            pipeline(dve, step)


def mix(nc, hbm, keep):
    with ExitStack() as ctx:
        def sb(name, shape, dt=FP32):
            return ctx.enter_context(nc.sbuf_tensor(name, shape, dt))

        def sem(name):
            return ctx.enter_context(nc.semaphore(name))

        NT = TOK // P
        logits = keep["logits"]
        wo = sb("wo", [P, KD, D])
        bias9 = sb("bias9", [NE + 1, D])
        x_res = sb("x_res", [P, 2, D])
        attn_tile = [sb(f"attn_tile{i}", [P, H, DK]) for i in range(2)]
        gates_tile = [sb(f"gates_tile{i}", [P, NE + 1]) for i in range(2)]
        attn_t = [sb(f"attn_t{i}", [P, KD, P]) for i in range(2)]
        gates_t = [sb(f"gates_t{i}", [NE + 1, P]) for i in range(2)]
        xh = sb("x_high", [P, KD, TOK], FP16)
        xl = sb("x_low", [P, KD, TOK], FP16)
        y = sb("y_sb", [P, NT, D])
        stage = {"gate_w": sb("gate_w", [P, KD, F]), "up_w": sb("up_w", [P, KD, F]),
                 "down_w": sb("down_w", [P, FT, D]), "gate_b": sb("gate_b", [P, FT]), "up_b": sb("up_b", [P, FT])}
        parts = [{w: [sb(f"{w}_{part}{i}", stage[w].shape, FP16) for part in ("high", "low")]
                  for w in WEIGHTS} for i in range(2)]
        gb = [sb(f"gate_bias{i}", [P, FT]) for i in range(2)]
        ub = [sb(f"up_bias{i}", [P, FT]) for i in range(2)]
        ge = [sb(f"gates_e{i}", [P, NT]) for i in range(2)]
        act_g = [sb(f"silu{i}", [P, CH]) for i in range(2)]
        hid = [sb(f"hidden{f}", [P, CH]) for f in range(FT)]
        hid_high = [sb(f"hidden_high{i}", [P, FT, CH], FP16) for i in range(2)]
        hid_low = [sb(f"hidden_low{i}", [P, FT, CH], FP16) for i in range(2)]
        peak = sb("peak", [P, NT, 1])
        prob = sb("prob", [P, NT, NE])
        total = sb("total", [P, NT, 1])
        rest = sb("prob_rest", [P, NT, NE])
        same = sb("same", [P, NT, NE])
        index = sb("index", [P, NT, NE])
        index_i = sb("index_i", [P, NT, NE], mybir.dt.int32)
        pick = sb("pick", [P, NT, NE])
        first = sb("first", [P, NT, 1])
        chosen = sb("chosen", [P, 2, NT, NE])
        gates = sb("gates", [P, NT, NE + 1])
        psum = [ctx.enter_context(nc.psum_tensor(f"pc{i}", [P, CH], FP32)) for i in range(8)]

        s_w = sem("c_weights")
        s_x = [sem(f"c_x{i}") for i in range(2)]
        s_xp = sem("c_x_parts")
        s_ix = sem("c_index")
        s_r = sem("c_router")
        s_re = sem("c_router_exp")
        s_in = sem("c_tile_in")
        s_t = sem("c_tile_transposed")
        s_te = sem("c_tile_on_chip")
        s_p = sem("c_projected")
        s_y = sem("c_y_started")
        s_ew = sem("c_expert_landed")
        s_wh = sem("c_weights_high")
        s_wl = sem("c_weights_low")
        s_gu = sem("c_gate_up")
        s_si = sem("c_silu")
        s_h = sem("c_hidden")
        s_hh = sem("c_hidden_high")
        s_hl = sem("c_hidden_low")
        s_d = sem("c_down")
        s_ye = sem("c_y_added")
        s_out = sem("c_out")
        block = ctx.enter_context(nc.Block())

        EW = 5 * 16
        NC = 2 * NCH

        def load_expert(sp, e):
            for w in WEIGHTS:
                sp.dma_start(stage[w][:, :, :], hbm[w][e, :, :].rearrange("(k p) n -> p k n", p=P)).then_inc(s_ew, 16)
            for b in ("gate_b", "up_b"):
                sp.dma_start(stage[b][:, :], hbm[b][e, :, :]).then_inc(s_ew, 16)

        def tiles(eng, step):
            for par in range(2):
                step(0, par, True)
            with eng.Fori(1, NT // 2) as tt:
                for par in range(2):
                    step(tt, par, False)

        def experts(eng, pair):
            with eng.Fori(0, NE // 2 - 1) as ee:
                pair(ee, False)
            pair(NE // 2 - 1, True)

        @block.sync
        def _(sp):
            sp.dma_start(wo[:, :, :], hbm["woT"].rearrange("(k p) n -> p k n", p=P)).then_inc(s_w, 16)
            sp.dma_start(bias9[0:NE, :], hbm["down_b"]).then_inc(s_w, 16)
            sp.dma_start(bias9[NE:NE + 1, :], hbm["bo"]).then_inc(s_w, 16)
            load_expert(sp, 0)
            for part, dst in enumerate((xh, xl)):
                sp.dma_start(dst[:, :, :], hbm["x_parts"][part, :, :, :]).then_inc(s_xp, 16)

            def step(tt, par, first):
                if not first:
                    sp.wait_ge(s_y, tt * 2 + par)
                    sp.nop(nofuse=True)
                sp.dma_start(x_res[:, par, :], hbm["x"][bass.ds(tt * (2 * P) + par * P, P), :]).then_inc(s_x[par], 16)

            tiles(sp, step)

            def pair(ee, last):
                for i in range(2):
                    if not (last and i):
                        sp.wait_ge(s_wl, (ee * 2 + i) * 4 + 4)
                        sp.nop(nofuse=True)
                        load_expert(sp, ee * 2 + i + 1)

            experts(sp, pair)
            for c in range(NCH):
                sp.wait_ge(s_ye, (NE - 1) * NT + (c + 1) * TPC + 1)
                sp.nop(nofuse=True)
                sp.dma_start(hbm["out"][c * CH:(c + 1) * CH, :].rearrange("(t p) d -> p t d", p=P),
                             y[:, c * TPC:(c + 1) * TPC, :]).then_inc(s_out, 16)
            sp.wait_ge(s_out, 16 * NCH)
            sp.nop(nofuse=True)

        @block.gpsimd
        def _(pool):
            nc.gpsimd.iota(index_i[:, :, :], pattern=[[0, NT], [1, NE]], base=-NE, channel_multiplier=0).then_inc(s_ix, 1)
            pool.wait_ge(s_ix, 1)
            nc.gpsimd.tensor_copy(index[:, :, :], index_i[:, :, :]).then_inc(s_ix, 1)

        @block.scalar
        def _(act):
            act.wait_ge(s_r, 2)
            nc.scalar.activation(prob[:, :, :], rest[:, :, :], ACT.Exp).then_inc(s_re, 1)

            def high_weights(e, i):
                act.wait_ge(s_ew, e * EW + EW)
                if not (isinstance(e, int) and e < 2):
                    act.wait_ge(s_d, (e - 1) * NT + 2 * TPC)
                    act.wait_ge(s_ye, (e - 1) * NT + 1)
                for w in WEIGHTS:
                    nc.scalar.activation(parts[i][w][0][:, :, :], stage[w][:, :, :], ACT.Copy,
                                         scale=W_SCALE).then_inc(s_wh, 1)
                nc.scalar.copy(gb[i][:, :], stage["gate_b"][:, :]).then_inc(s_wh, 1)
                if isinstance(e, int) and e == 0:
                    act.wait_ge(s_r, ROUTER_LINKS)
                nc.scalar.activation(ge[i][:, :], gates[:, :, e], ACT.Copy, scale=1.0 / W_SCALE).then_inc(s_wh, 1)

            high_weights(0, 0)

            with act.Fori(0, B) as b:
                with act.Fori(0, NB // 2) as cc:
                    for par in range(2):
                        n = b * NB + cc * 2 + par
                        act.wait_ge(s_te, n + 1)
                        nc.scalar.copy(attn_tile[par][:, :, :], keep["v"][:, :, n, :])
                        nc.scalar.copy(gates_tile[par][:, :], gates[:, n, :]).then_inc(s_in, 1)

            def pair(ee, last):
                def high(m):
                    j, f = m // FT, m % FT
                    act.wait_ge(s_h, ee * (NC * FT) + m + 3)
                    if f == 0:
                        act.wait_ge(s_d, ee * (NC * TPC) + j * TPC + TPC)
                    nc.scalar.activation(hid_high[j % 2][:, f, :], hid[f][:, :], ACT.Copy,
                                         scale=1.0 / W_SCALE).then_inc(s_hh, 1)

                for j in range(NC):
                    i = j // NCH
                    if j % NCH == NCH // 2 and not (last and i):
                        high_weights(ee * 2 + i + 1, 1 - i)
                    for f in range(FT):
                        m = j * FT + f
                        act.wait_ge(s_gu, (ee * (NC * FT) + m) * 2 + 1)
                        act.wait_ge(s_h, ee * (NC * FT) + m + 1)
                        nc.scalar.activation(act_g[f % 2][:, :], psum[f % 2][:, :], ACT.Silu,
                                             bias=gb[i][:, f:f + 1], scale=1.0 / W_SCALE).then_inc(s_si, 1)
                        if m:
                            high(m - 1)
                high(NC * FT - 1)

            experts(act, pair)

        @block.vector
        def _(dve):
            dve.sem_inc(s_te, 2)
            dve.sem_inc(s_y, 1)
            dve.sem_inc(s_h, 2)
            dve.sem_inc(s_hl, FT)
            dve.sem_inc(s_ye, 1)
            links = [0]

            def link(ins):
                links[0] += 1
                ins.then_inc(s_r, 1)
                dve.wait_ge(s_r, links[0])

            wide = [P, NT, NE]
            link(nc.vector.tensor_reduce(peak[:, :, :], logits[:, :, :], axis=AX.X, op=ALU.max))
            link(nc.vector.tensor_tensor(rest[:, :, :], logits[:, :, :], peak[:, :, :].to_broadcast(wide), ALU.subtract))
            dve.wait_ge(s_re, 1)
            link(nc.vector.tensor_reduce(total[:, :, :], prob[:, :, :], axis=AX.X, op=ALU.add))
            link(nc.vector.reciprocal(total[:, :, :], total[:, :, :]))
            link(nc.vector.tensor_tensor(prob[:, :, :], prob[:, :, :], total[:, :, :].to_broadcast(wide), ALU.mult))
            link(nc.vector.tensor_copy(rest[:, :, :], prob[:, :, :]))
            dve.wait_ge(s_ix, 2)
            for r in range(2):
                link(nc.vector.tensor_reduce(peak[:, :, :], rest[:, :, :], axis=AX.X, op=ALU.max))
                link(nc.vector.tensor_tensor(same[:, :, :], rest[:, :, :], peak[:, :, :].to_broadcast(wide), ALU.is_equal))
                link(nc.vector.tensor_tensor(pick[:, :, :], same[:, :, :], index[:, :, :], ALU.mult))
                link(nc.vector.tensor_reduce(first[:, :, :], pick[:, :, :], axis=AX.X, op=ALU.min))
                link(nc.vector.tensor_tensor(chosen[:, r, :, :], index[:, :, :], first[:, :, :].to_broadcast(wide),
                                             ALU.is_equal))
                if r == 0:
                    link(nc.vector.scalar_tensor_tensor(out=rest[:, :, :], in0=chosen[:, 0, :, :], scalar=-2.0,
                                                        in1=rest[:, :, :], op0=ALU.mult, op1=ALU.add))
            link(nc.vector.tensor_tensor(same[:, :, :], chosen[:, 0, :, :], chosen[:, 1, :, :], ALU.add))
            link(nc.vector.tensor_tensor(prob[:, :, :], prob[:, :, :], same[:, :, :], ALU.mult))
            link(nc.vector.tensor_reduce(total[:, :, :], prob[:, :, :], axis=AX.X, op=ALU.add))
            link(nc.vector.tensor_scalar(total[:, :, :], total[:, :, :], 1e-9, None, ALU.add))
            link(nc.vector.reciprocal(total[:, :, :], total[:, :, :]))
            link(nc.vector.tensor_tensor(gates[:, :, 0:NE], prob[:, :, :], total[:, :, :].to_broadcast(wide), ALU.mult))
            link(nc.vector.memset(gates[:, :, NE:NE + 1], 1.0))
            assert links[0] == ROUTER_LINKS, links
            def low_weights(e, i):
                dve.wait_ge(s_wh, e * 5 + 5)
                for w in WEIGHTS:
                    high, low = parts[i][w]
                    nc.vector.scalar_tensor_tensor(out=low[:, :, :], in0=stage[w][:, :, :], scalar=W_SCALE,
                                                   in1=high[:, :, :], op0=ALU.mult, op1=ALU.subtract).then_inc(s_wl, 1)
                nc.vector.tensor_scalar(ub[i][:, :], stage["up_b"][:, :], W_SCALE, None, ALU.mult).then_inc(s_wl, 1)

            low_weights(0, 0)

            def add_tile(tt, par):
                n = tt * 2 + par
                dve.wait_ge(s_p, n + 1)
                dve.wait_ge(s_x[par], tt * 16 + 16)
                nc.vector.tensor_tensor(y[:, n, :], psum[2 + par][:, 0:D], x_res[:, par, :], ALU.add).then_inc(s_y, 1)

            def tile(tt, par, first):
                n = tt * 2 + par
                dve.wait_ge(s_t, n + 1)
                if not first:
                    dve.wait_ge(s_p, n - 1)
                nc.vector.tensor_copy(attn_t[par][:, :, :], psum[par][:, 0:KD * P].rearrange("p (k l) -> p k l", k=KD))
                nc.vector.tensor_copy(gates_t[par][:, :], psum[par][0:NE + 1, KD * P:(KD + 1) * P]).then_inc(s_te, 1)
                if not (first and par == 0):
                    add_tile(*((tt, 0) if par else (tt - 1, 1)))

            tiles(dve, tile)
            add_tile(NT // 2 - 1, 1)
            dve.wait_ge(s_y, NT + 1)

            def pair(ee, last):
                def low(m):
                    j, f = m // FT, m % FT
                    dve.wait_ge(s_hh, ee * (NC * FT) + m + 1)
                    nc.vector.scalar_tensor_tensor(out=hid_low[j % 2][:, f, :], in0=hid[f][:, :], scalar=1.0 / W_SCALE,
                                                   in1=hid_high[j % 2][:, f, :], op0=ALU.mult,
                                                   op1=ALU.subtract).then_inc(s_hl, 1)

                def add_down(j):
                    for t in range(TPC):
                        tile_ = (j % NCH) * TPC + t
                        m = ee * (NC * TPC) + j * TPC + t
                        dve.wait_ge(s_d, m + 1 + 2 * TPC)
                        nc.vector.scalar_tensor_tensor(out=y[:, tile_, :], in0=psum[4 + t][:, 0:D],
                                                       scalar=ge[j // NCH][:, tile_:tile_ + 1], in1=y[:, tile_, :],
                                                       op0=ALU.mult, op1=ALU.add).then_inc(s_ye, 1)

                for j in range(NC):
                    i = j // NCH
                    if j % NCH == NCH // 2 and not (last and i):
                        low_weights(ee * 2 + i + 1, 1 - i)
                    for f in range(FT):
                        m = j * FT + f
                        dve.wait_ge(s_gu, (ee * (NC * FT) + m) * 2 + 2)
                        dve.wait_ge(s_si, ee * (NC * FT) + m + 1)
                        dve.wait_ge(s_hl, ee * (NC * FT) + m + 1)
                        nc.vector.scalar_tensor_tensor(out=hid[f][:, :], in0=psum[2 + f % 2][:, :],
                                                       scalar=ub[i][:, f:f + 1], in1=act_g[f % 2][:, :],
                                                       op0=ALU.add, op1=ALU.mult).then_inc(s_h, 1)
                        if m:
                            low(m - 1)
                    if j:
                        add_down(j - 1)
                low(NC * FT - 1)
                add_down(NC - 1)

            experts(dve, pair)

        @block.tensor
        def _(pe):
            pe.sem_inc(s_d, 2 * TPC)
            pe.wait_ge(s_w, 48)

            def project_tile(tt, par, first):
                n = tt * 2 + par
                pe.wait_ge(s_te, n + 3)
                if not first:
                    pe.wait_ge(s_y, n)
                for k in range(KD):
                    nc.tensor.matmul(psum[2 + par][:, 0:D], attn_t[par][:, k, :], wo[:, k, :], start=(k == 0), stop=False)
                nc.tensor.matmul(psum[2 + par][:, 0:D], gates_t[par][:, :], bias9[:, :], start=False,
                                 stop=True).then_inc(s_p, 1)

            def tile(tt, par, first):
                n = tt * 2 + par
                pe.wait_ge(s_in, n + 1)
                pe.wait_ge(s_te, n + 1)
                flat = attn_tile[par][:, :, :].rearrange("p h d -> p (h d)")
                for k in range(KD):
                    nc.tensor.transpose(psum[par][:, k * P:(k + 1) * P], flat[:, k * P:(k + 1) * P], keep["ident"][:, :])
                nc.tensor.transpose(psum[par][0:NE + 1, KD * P:(KD + 1) * P], gates_tile[par][:, :],
                                    keep["ident"][:, :]).then_inc(s_t, 1)
                if first and par == 0:
                    return
                if par:
                    project_tile(tt, 0, first)
                else:
                    project_tile(tt - 1, 1, False)

            tiles(pe, tile)
            project_tile(NT // 2 - 1, 1, False)
            pe.wait_ge(s_xp, 32)
            pe.wait_ge(s_y, NT + 1)

            def pair(ee, last):
                def down(j):
                    dw = parts[j // NCH]["down_w"]
                    for f in range(FT):
                        pe.wait_ge(s_hl, ee * (NC * FT) + j * FT + f + 1 + FT)
                        for t in range(TPC):
                            if f == 0:
                                pe.wait_ge(s_ye, ee * (NC * TPC) + max(j - 1, 0) * TPC + (t + 1 if j else 0) + 1)
                            cols = slice(t * P, (t + 1) * P)
                            for n, (a, z) in enumerate(((hid_high, 0), (hid_high, 1), (hid_low, 0))):
                                ins = nc.tensor.matmul(psum[4 + t][:, 0:D], a[j % 2][:, f, cols], dw[z][:, f, :],
                                                       start=(f == 0 and n == 0), stop=(f == FT - 1 and n == 2))
                            if f == FT - 1:
                                ins.then_inc(s_d, 1)

                for j in range(NC):
                    i, c = j // NCH, j % NCH
                    if c == 0:
                        pe.wait_ge(s_wl, (ee * 2 + i) * 4 + 4)
                    for f in range(FT):
                        pe.wait_ge(s_h, ee * (NC * FT) + j * FT + f + 1)
                        for w, bank in (("gate_w", f % 2), ("up_w", 2 + f % 2)):
                            high, low = parts[i][w]
                            for n, (a, z) in enumerate(((high, xh), (high, xl), (low, xh))):
                                for k in range(KD):
                                    ins = nc.tensor.matmul(psum[bank][:, :], a[:, k, f * P:(f + 1) * P],
                                                           z[:, k, c * CH:(c + 1) * CH],
                                                           start=(n == 0 and k == 0), stop=(n == 2 and k == KD - 1))
                            ins.then_inc(s_gu, 1)
                    if j:
                        down(j - 1)
                down(NC - 1)

            experts(pe, pair)


ROUTER_LINKS = 2 + 4 + 11 + 7


def program(nc, hbm):
    with ExitStack() as ctx:
        def sb(name, shape, dt=FP32):
            return ctx.enter_context(nc.sbuf_tensor(name, shape, dt))

        keep = {
            "ident": sb("ident", [P, P]),
            "logits": sb("logits", [P, TOK // P, NE]),
            "v": sb("v_all", [P, H, B * NB, DK]),
        }
        hbm["x_parts"] = nc.dram_tensor("x_parts_scratch", (2, P, KD, TOK), FP16, kind="Internal").ap()
        hbm["planes"] = nc.dram_tensor("planes_scratch", (2, 3, D, TOK), BF16, kind="Internal").ap()
        hbm["rel_scratch"] = nc.dram_tensor("rel_scratch", (2, P, RELW), FP32, kind="Internal").ap()
        hbm["prob_scratch"] = nc.dram_tensor("prob_scratch", (2, P, 2, RVW + P), FP16, kind="Internal").ap()
        with ExitStack() as inner:
            def sbi(name, shape, dt=FP32):
                return inner.enter_context(nc.sbuf_tensor(name, shape, dt))

            keep["rk_stack"] = sbi("rk_stack", [PARTS, RELW], BF16)
            keep["rv"] = sbi("rv", [P, RVW // P, DK])
            keep["rv_lo"] = sbi("rv_lo", [P, DK])
            keep["rv_hi"] = sbi("rv_hi", [P, DK])
            keep["upper"] = sbi("upper", [P, P])
            project(nc, hbm, keep)
            attend(nc, hbm, keep)
        mix(nc, hbm, keep)


def kernel(**inputs):
    import numpy as np
    import concourse.bacc as bacc
    from concourse.bass_utils import run_bass_kernel_spmd

    def a(name):
        return np.asarray(inputs[name])

    def rows(first, count):
        row = np.arange(count) + first + MAXLEN - 1
        return np.clip(np.where(row < 0, row + 2 * MAXLEN - 1, row), 0, 2 * MAXLEN - 2)

    rel_k, rel_v = a("L0_attn_relative_k")[rows(REL0, RELW)], a("L0_attn_relative_v")
    arrays = {
        "x": a("L0_attn_x").reshape(TOK, D),
        "wqT": a("L0_attn_Wq").T, "wkT": a("L0_attn_Wk").T, "wvT": a("L0_attn_Wv").T, "woT": a("L0_attn_Wo").T,
        "bq": a("L0_attn_bq").reshape(2, P).T, "bk": a("L0_attn_bk").reshape(2, P).T,
        "bv": a("L0_attn_bv").reshape(1, D), "bo": a("L0_attn_bo").reshape(1, D),
        "rel_kT": rel_k.T, "rel_v": rel_v[rows(R_LO * P, RVW)],
        "rel_v_ends": rel_v[[rows(R_LO * P - 1, 1)[0], rows((R_HI + 1) * P, 1)[0]]],
        "router_wT": a("L0_ffn_router_w").T,
        "gate_w": a("L0_ffn_gate_w"), "up_w": a("L0_ffn_up_w"), "down_w": a("L0_ffn_down_w"),
        "gate_b": a("L0_ffn_gate_b").reshape(NE, FT, P).transpose(0, 2, 1),
        "up_b": a("L0_ffn_up_b").reshape(NE, FT, P).transpose(0, 2, 1),
        "down_b": a("L0_ffn_down_b"),
    }
    arrays = {n: np.ascontiguousarray(v) for n, v in arrays.items()}
    nc = bacc.Bacc("TRN2", target_bir_lowering=False, num_devices=1)
    hbm = {n: nc.dram_tensor(f"in_{n}", v.shape, mybir.dt.from_np(v.dtype), kind="ExternalInput").ap()
           for n, v in arrays.items()}
    hbm["out"] = nc.dram_tensor("out", (TOK, D), FP32, kind="ExternalOutput").ap()
    program(nc, hbm)
    r = run_bass_kernel_spmd(nc, [{f"in_{n}": v for n, v in arrays.items()}], core_ids=[0])
    return r.results[0]["out"].reshape(B, L, D)
```
